# Optimizing a Trainium2 kernel written in Bass

```python
import numpy as np
import jax
import jax.numpy as jnp

def _softmax(x, axis=-1):
    return jax.nn.softmax(x, axis=axis)

def _gelu(x):
    return jax.nn.gelu(x, approximate=True)

def _silu(x):
    return jax.nn.silu(x)

def _sigmoid(x):
    return jax.nn.sigmoid(x)

def _layernorm(x, axis=-1, eps=1e-05):
    m = jnp.mean(x, axis=axis, keepdims=True)
    v = jnp.var(x, axis=axis, keepdims=True)
    return (x - m) / jnp.sqrt(v + eps)

def _scatter_add(tgt, idx, src, axis=0):
    return tgt.at[idx].add(src)

def _segment_sum(src, seg, n):
    return jax.ops.segment_sum(src, seg, n)
kernel_name = 'mk_adj_resnorm_d4_adj_r2_ae16e1'

def setup_inputs(seed: int=0):
    np.random.seed(seed)
    _w = jnp.asarray

    def _rec_inputs():
        import jax
        import jax.numpy as jnp
        _gk = jax.random.key(seed)
        x = 7.22e-05 + 1 * jax.random.normal(jax.random.fold_in(_gk, 1), (16, 512, 128), jnp.float32)
        _a = jax.random.bernoulli(jax.random.fold_in(_gk, 2), 0.015625, (512, 512))
        _a = jnp.logical_or(_a, jnp.swapaxes(_a, -1, -2))
        _a = jnp.logical_or(_a, jnp.eye(512, dtype=bool))
        _af = _a.astype(jnp.float32)
        _af = _af * jax.random.uniform(jax.random.fold_in(_gk, 3), (512, 512), jnp.float32, 0.05, 0.000976562)
        adj = _af
        return (x, adj)
    x, adj = _rec_inputs()

    def _L0_gnn_setup():
        import jax, jax.numpy as jnp
        import numpy as np
        N_STEPS = 8
        SPATIAL_SCALE = 1.0
        key = jax.random.key(seed)
        ks = jax.random.split(key, 6)
        B, N, D = (32, 512, 128)
        x = jax.random.normal(ks[0], (B, N, D), dtype=jnp.float32)
        adj_mx = jax.random.uniform(ks[1], (N, N), dtype=jnp.float32) / N
        alpha_train = jnp.ones((N,), dtype=jnp.float32)
        w = jnp.eye(D, dtype=jnp.float32) + 0.01 * jax.random.normal(ks[2], (D, D), dtype=jnp.float32)
        d = jax.random.uniform(ks[3], (D,), dtype=jnp.float32)
        fc_in_w = jax.random.normal(ks[4], (D, D), dtype=jnp.float32) * (1.0 / np.sqrt(D))
        fc_in_b = jnp.zeros((D,), dtype=jnp.float32)
        return {'x': x, 'adj_mx': adj_mx, 'alpha_train': alpha_train, 'w': w, 'd': d, 'fc_in_w': fc_in_w, 'fc_in_b': fc_in_b, 'vt': 0}
    _L0_gnn_all = _L0_gnn_setup()
    _L0_gnn_in = {k: v for k, v in _L0_gnn_all.items() if k in ('alpha_train', 'w', 'd', 'fc_in_w', 'fc_in_b')}
    del _L0_gnn_all

    def _L1_gnn_setup():
        import jax, jax.numpy as jnp
        import numpy as np
        EPS = 1e-05

        def _batchnorm(x, gamma, beta):
            mu = jnp.mean(x, axis=0)
            var = jnp.var(x, axis=0)
            return (x - mu) * jax.lax.rsqrt(var + EPS) * gamma + beta
        key = jax.random.key(seed)
        ks = jax.random.split(key, 4)
        b, n, d, h, o = (32, 1024, 128, 256, 128)
        features = jax.random.normal(ks[0], (b, n, d), dtype=jnp.float32)
        A = jax.random.uniform(ks[1], (n, n), dtype=jnp.float32)
        lim1 = float(np.sqrt(6.0 / (d + h)))
        W1 = jax.random.uniform(ks[2], (h, d), minval=-lim1, maxval=lim1, dtype=jnp.float32)
        b1 = jnp.zeros((h,), jnp.float32)
        lim2 = float(np.sqrt(6.0 / (h + o)))
        W2 = jax.random.uniform(ks[3], (o, h), minval=-lim2, maxval=lim2, dtype=jnp.float32)
        b2 = jnp.zeros((o,), jnp.float32)
        g1 = jnp.ones((h,), jnp.float32)
        be1 = jnp.zeros((h,), jnp.float32)
        g2 = jnp.ones((o,), jnp.float32)
        be2 = jnp.zeros((o,), jnp.float32)
        return {'features': features, 'A': A, 'W1': W1, 'b1': b1, 'g1': g1, 'be1': be1, 'W2': W2, 'b2': b2, 'g2': g2, 'be2': be2}
    _L1_gnn_all = _L1_gnn_setup()
    _L1_gnn_in = {k: v for k, v in _L1_gnn_all.items() if k in ('W1', 'b1', 'g1', 'be1', 'W2', 'b2', 'g2', 'be2')}
    del _L1_gnn_all

    def _L2_gnn_setup():
        import jax, jax.numpy as jnp
        import numpy as np
        B, N, IN_DIM, OUT_DIM, H = (2, 2048, 128, 128, 4)
        HEAD_DIM = OUT_DIM // H
        EDGE_P = 0.01
        key = jax.random.key(seed)
        k1, k2, k3 = jax.random.split(key, 3)
        h = jax.random.normal(k1, (B, N, IN_DIM), dtype=jnp.float32)
        W = jax.random.normal(k2, (IN_DIM, 3 * OUT_DIM), dtype=jnp.float32) / np.sqrt(IN_DIM)
        adj = (jax.random.uniform(k3, (N, N)) < EDGE_P).astype(jnp.float32)
        adj = jnp.maximum(adj, jnp.eye(N, dtype=jnp.float32))
        return {'h': h, 'W': W, 'adj': adj}
    _L2_gnn_all = _L2_gnn_setup()
    _L2_gnn_in = {k: v for k, v in _L2_gnn_all.items() if k in ('W',)}
    del _L2_gnn_all

    def _L3_gnn_setup():
        import jax, jax.numpy as jnp
        import numpy as np
        ALPHA = 0.2
        key = jax.random.key(seed)
        k1, k2, k3, k4 = jax.random.split(key, 4)
        B, N, Fin, Fout = (8, 1024, 128, 128)
        h = jax.random.normal(k1, (B, N, Fin), dtype=jnp.float32)
        adj = jax.random.randint(k2, (N, N), 0, 2).astype(jnp.float32)
        adj = jnp.maximum(adj, jnp.eye(N, dtype=jnp.float32))

        def xavier(k, shape, gain=1.414):
            fan_in, fan_out = (shape[0], shape[1])
            a = gain * np.sqrt(6.0 / (fan_in + fan_out))
            return jax.random.uniform(k, shape, dtype=jnp.float32, minval=-a, maxval=a)
        W = xavier(k3, (Fin, Fout))
        a = xavier(k4, (2 * Fout, 1))
        return {'h': h, 'adj_matrix': adj, 'W': W, 'a': a}
    _L3_gnn_all = _L3_gnn_setup()
    _L3_gnn_in = {k: v for k, v in _L3_gnn_all.items() if k in ('W', 'a')}
    del _L3_gnn_all
    return {'x': x, 'adj': adj, 'L0_gnn_alpha_train': _L0_gnn_in['alpha_train'], 'L0_gnn_w': _L0_gnn_in['w'], 'L0_gnn_d': _L0_gnn_in['d'], 'L0_gnn_fc_in_w': _L0_gnn_in['fc_in_w'], 'L0_gnn_fc_in_b': _L0_gnn_in['fc_in_b'], 'L1_gnn_W1': _L1_gnn_in['W1'], 'L1_gnn_b1': _L1_gnn_in['b1'], 'L1_gnn_g1': _L1_gnn_in['g1'], 'L1_gnn_be1': _L1_gnn_in['be1'], 'L1_gnn_W2': _L1_gnn_in['W2'], 'L1_gnn_b2': _L1_gnn_in['b2'], 'L1_gnn_g2': _L1_gnn_in['g2'], 'L1_gnn_be2': _L1_gnn_in['be2'], 'L2_gnn_W': _L2_gnn_in['W'], 'L3_gnn_W': _L3_gnn_in['W'], 'L3_gnn_a': _L3_gnn_in['a']}

def reference(x, adj, L0_gnn_alpha_train, L0_gnn_w, L0_gnn_d, L0_gnn_fc_in_w, L0_gnn_fc_in_b, L1_gnn_W1, L1_gnn_b1, L1_gnn_g1, L1_gnn_be1, L1_gnn_W2, L1_gnn_b2, L1_gnn_g2, L1_gnn_be2, L2_gnn_W, L3_gnn_W, L3_gnn_a):
    import jax
    import jax.numpy as jnp

    def _L0_gnn_ref(x, adj_mx, alpha_train, w, d, fc_in_w, fc_in_b, vt):
        import jax, jax.numpy as jnp
        import numpy as np
        N_STEPS = 8
        SPATIAL_SCALE = 1.0
        x0 = jax.lax.stop_gradient(x)
        h = jnp.einsum('bnd,ed->bne', x, fc_in_w) + fc_in_b
        alph = jax.nn.sigmoid(alpha_train)[:, None]
        d_clamped = jnp.clip(d, 0.0, 1.0)
        w_eff = w * d_clamped @ w.T
        dt = jnp.float32(SPATIAL_SCALE / N_STEPS)

        def euler_step(h, _):
            ax = jnp.einsum('nm,bmd->bnd', adj_mx, h)
            f = alph * 0.5 * (ax - h) + h @ w_eff - h + x0
            return (h + dt * f, None)
        h, _ = jax.lax.scan(euler_step, h, None, length=N_STEPS)
        return h

    def _L1_gnn_ref(features, A, W1, b1, g1, be1, W2, b2, g2, be2):
        import jax, jax.numpy as jnp
        import numpy as np
        EPS = 1e-05

        def _batchnorm(x, gamma, beta):
            mu = jnp.mean(x, axis=0)
            var = jnp.var(x, axis=0)
            return (x - mu) * jax.lax.rsqrt(var + EPS) * gamma + beta
        b, n, d = features.shape
        A_norm = A + jnp.eye(n, dtype=A.dtype)
        deg = jnp.sum(A_norm, axis=0) + jnp.sum(A_norm, axis=1) - jnp.diagonal(A_norm)
        dinv = jax.lax.rsqrt(deg)
        A_hat = A_norm * dinv[:, None] * dinv[None, :]
        agg = jnp.einsum('nm,bmd->bnd', A_hat, features)
        x = agg.reshape(-1, d)
        h = jax.nn.relu(_batchnorm(x @ W1.T + b1, g1, be1))
        out = h @ W2.T + b2
        out = _batchnorm(out, g2, be2)
        return out.reshape(b, n, -1)

    def _L2_gnn_ref(h, W, adj):
        import jax, jax.numpy as jnp
        import numpy as np
        B, N, IN_DIM, OUT_DIM, H = (2, 2048, 128, 128, 4)
        HEAD_DIM = OUT_DIM // H
        EDGE_P = 0.01
        Bn, Nn, _ = h.shape
        qkv = h @ W
        qkv = qkv.reshape(Bn, Nn, 3, H, HEAD_DIM).transpose(2, 0, 3, 1, 4)
        q, k, v = (qkv[0], qkv[1], qkv[2])
        mask = jnp.where(adj == 0, -jnp.inf, 0.0)
        scores = jnp.einsum('bhid,bhjd->bhij', q, k) / np.sqrt(HEAD_DIM) + mask
        attn = jax.nn.softmax(scores, axis=-1)
        out = jnp.einsum('bhij,bhjd->bhid', attn, v)
        return out.transpose(0, 2, 1, 3).reshape(Bn, Nn, OUT_DIM)

    def _L3_gnn_ref(h, adj_matrix, W, a):
        import jax, jax.numpy as jnp
        import numpy as np
        ALPHA = 0.2
        Fout = W.shape[1]
        Wh = jnp.einsum('bnf,fo->bno', h, W)
        a1, a2 = (a[:Fout, 0], a[Fout:, 0])
        s1 = Wh @ a1
        s2 = Wh @ a2
        e = s1[:, :, None] + s2[:, None, :]
        e = jnp.where(e >= 0, e, ALPHA * e)
        e = jnp.where(adj_matrix[None] == 0, -jnp.inf, e)
        attention = jax.nn.softmax(e, axis=-1)
        h_prime = jnp.einsum('bij,bjo->bio', attention, Wh)
        return h_prime
    x = _layernorm(x + _L0_gnn_ref(x, adj, L0_gnn_alpha_train, L0_gnn_w, L0_gnn_d, L0_gnn_fc_in_w, L0_gnn_fc_in_b, 0), axis=-1)
    x = _layernorm(x + _L1_gnn_ref(x, adj, L1_gnn_W1, L1_gnn_b1, L1_gnn_g1, L1_gnn_be1, L1_gnn_W2, L1_gnn_b2, L1_gnn_g2, L1_gnn_be2), axis=-1)
    x = _layernorm(x + _L2_gnn_ref(x, L2_gnn_W, adj), axis=-1)
    x = _layernorm(x + _L3_gnn_ref(x, adj, L3_gnn_W, L3_gnn_a), axis=-1)
    return x

_drawn_inputs = setup_inputs


def setup_inputs(seed=0):
    import zlib

    import numpy as np

    out = dict(_drawn_inputs(seed))
    spreads = {'L0_gnn_alpha_train': (1.0, 0.2),
     'L0_gnn_fc_in_b': (0.0, 0.1),
     'L1_gnn_b1': (0.0, 0.1),
     'L1_gnn_g1': (1.0, 0.2),
     'L1_gnn_be1': (0.0, 0.1),
     'L1_gnn_b2': (0.0, 0.1),
     'L1_gnn_g2': (1.0, 0.2),
     'L1_gnn_be2': (0.0, 0.1)}
    factors = {}
    for name, (base, spread) in spreads.items():
        noise = np.random.default_rng([zlib.crc32(name.encode()), seed]).standard_normal(out[name].shape)
        drawn = base * np.exp(spread * noise) if base else spread * noise
        out[name] = jnp.asarray(drawn.astype(out[name].dtype))
    for name, factor in factors.items():
        out[name] = (out[name] * factor).astype(out[name].dtype)
    return out
```

```python
from contextlib import ExitStack
from math import comb

import concourse.bass as bass
from concourse import mybir

F32 = mybir.dt.float32
F32R = mybir.dt.float32r
BF16 = mybir.dt.bfloat16
ALU = mybir.AluOpType
ACT = mybir.ActivationFunctionType
AX = mybir.AxisListType

P = 128
B, N, D = 16, 512, 128
NT = N // P
STEPS = 8
DT = 1.0 / STEPS
BABY = 3
H, HD = 4, D // 4
CH = 256 // P
EPS = 1e-5
MASKED = -1.0e30
CREDIT = 2


def after(b, per, k=None):
    return (b + CREDIT) * per + (per if k is None else k)


def hold(eng, gate):
    eng.sem_inc(gate, 1)


def flat(ap):
    return ap.rearrange("p a b -> p (a b)")


def three_pass(pe, out, stat, mov, start=True, stop=True):
    pe.matmul(out, stat[0], mov[0], start=start, stop=False)
    pe.matmul(out, stat[0], mov[1], start=False, stop=False)
    return pe.matmul(out, stat[1], mov[0], start=False, stop=stop)


class Memory:
    pass


def setup_constants(nc, ctx, m, ins, bank):
    def sb(name, shape, dt=F32):
        return ctx.enter_context(nc.sbuf_tensor(name, shape, dt))

    m.X = sb("X", [P, B, NT, D])
    m.ident = sb("ident", [P, P])
    m.identb = sb("identb", [P, P], BF16)
    m.neg_half = sb("neg_half", [P, 16])
    m.mask_ij = sb("mask_ij", [P, NT, N], BF16)
    m.mask_ji = sb("mask_ji", [P, NT, N], BF16)
    m.AhT = [sb("AhT_hi", [P, NT, N], F32R), sb("AhT_lo", [P, NT, N], F32R)]


def layer0_setup(nc, ctx, m, ins, bank):
    def keep(name, shape, dt=F32):
        return ctx.enter_context(nc.sbuf_tensor(name, shape, dt))

    m.LT = [keep("LT_hi", [P, NT, N], F32R), keep("LT_lo", [P, NT, N], F32R)]
    m.L2T = [keep("L2T_hi", [P, NT, N], F32R), keep("L2T_lo", [P, NT, N], F32R)]
    m.L3T = [keep("L3T_hi", [P, NT, N], F32R), keep("L3T_lo", [P, NT, N], F32R)]
    m.Pj = [keep("Pj_hi", [P, 9, D], F32R), keep("Pj_lo", [P, 9, D], F32R)]
    m.bias = keep("bias_field", [P, NT, BABY, D])

    with ExitStack() as own:
        def sb(name, shape, dt=F32):
            return own.enter_context(nc.sbuf_tensor(name, shape, dt))

        sems = []

        def sem(name):
            sems.append(nc.alloc_semaphore(name))
            return sems[-1]

        A = sb("A", [P, NT, N])
        A1 = sb("A1", [P, NT, N])
        L = sb("L", [P, NT, N])
        LTf = sb("LTf", [P, NT, N])
        Lr = [sb("L_hi", [P, NT, N], F32R), sb("L_lo", [P, NT, N], F32R)]
        w_sb = sb("w_sb", [P, D])
        fc = sb("fc", [P, D])
        d_col = sb("d_col", [P, 1])
        b_col = sb("b_col", [P, 1])
        al = sb("al", [P, NT])
        ea = sb("ea", [P, NT])
        col = sb("col", [P, 8, NT])
        ones = sb("ones", [P, P])
        wT = sb("wT", [P, D])
        wTs = sb("wTs", [P, D])
        RP = sb("RP", [P, 9, D])
        Pf = sb("Pf", [P, 9, D])
        cB = sb("cB", [P, 9, D])
        bB = sb("bB", [P, P])
        Y = sb("Y", [P, 2, NT])
        junk = sb("junk", [P, P])
        diag = sb("diag", [P, NT])
        deg = sb("deg", [P, 3, NT])
        dinv = sb("dinv", [P, NT])

        a_in = sem("a_in"); small_in = sem("small_in"); x_in = sem("x_in")
        pool_c = sem("pool_c"); ident_b = sem("ident_b")
        exp_a = sem("exp_a"); v_col = sem("v_col"); v_L = sem("v_L"); v_Lhi = sem("v_Lhi"); v_Llo = sem("v_Llo")
        t_AT = sem("t_AT"); v_mji = sem("v_mji"); v_mij = sem("v_mij")
        t_LT = sem("t_LT"); c_LTf = sem("c_LTf"); c_LTh = sem("c_LTh"); v_LTl = sem("v_LTl")
        t_L2 = sem("t_L2"); c_L2h = sem("c_L2h"); v_L2l = sem("v_L2l")
        t_L3 = sem("t_L3"); c_L3h = sem("c_L3h"); v_L3l = sem("v_L3l")
        t_Ah = sem("t_Ah"); c_Ahh = sem("c_Ahh"); v_Ahl = sem("v_Ahl")
        v_A1 = sem("v_A1"); t_cs = sem("t_cs"); v_deg = sem("v_deg"); p_dinv = sem("p_dinv"); v_As = sem("v_As")
        t_wT = sem("t_wT"); v_dc = sem("v_dc"); v_wT = sem("v_wT"); t_R = sem("t_R"); v_R = sem("v_R")
        t_Q = sem("t_Q"); v_P = sem("v_P"); t_cB = sem("t_cB"); v_cB = sem("v_cB")
        v_Y1 = sem("v_Y1"); t_Y2 = sem("t_Y2"); v_Y2 = sem("v_Y2"); v_bias = sem("v_bias"); v_bB = sem("v_bB")

        c_c, c_d, c_rs = (col[:, k, :] for k in range(3))
        block = own.enter_context(nc.Block())

        @block.sync
        def _(sp):
            sp.dma_start(A[:], ins["adj"].rearrange("(t p) m -> p t m", p=P)).then_inc(a_in, 16)
            sp.dma_start(w_sb[:], ins["L0_gnn_w"]).then_inc(small_in, 16)
            sp.dma_start(fc[:], ins["L0_gnn_fc_in_w"]).then_inc(small_in, 16)
            sp.dma_start(d_col[:], ins["L0_gnn_d"].rearrange("(p a) -> p a", a=1)).then_inc(small_in, 16)
            sp.dma_start(b_col[:], ins["L0_gnn_fc_in_b"].rearrange("(p a) -> p a", a=1)).then_inc(small_in, 16)
            with nc.allow_non_contiguous_dma(reason="512 words once"):
                sp.dma_start(al[:], ins["L0_gnn_alpha_train"].rearrange("(t p) -> p t", p=P)).then_inc(small_in, 16)
            for b in range(0, B, 4):
                sp.dma_start(m.X[:, b:b + 4].rearrange("p b t d -> p (b t) d"),
                             ins["x"][b:b + 4].rearrange("b (t p) d -> p (b t) d", p=P)).then_inc(x_in, 16)
            sp.wait_ge(x_in, 16 * (B // 4))

        @block.gpsimd
        def _(pool):
            pool.memset(m.ident[:], 0.0).then_inc(pool_c, 1)
            pool.memset(ones[:], 1.0).then_inc(pool_c, 1)
            pool.memset(m.neg_half[:], -0.5).then_inc(pool_c, 1)
            pool.wait_ge(pool_c, 3)
            pool.affine_select(out=m.ident[:], in_=m.ident[:], compare_op=ALU.not_equal, fill=1.0, base=0,
                               pattern=[[-1, P]], channel_multiplier=1).then_inc(pool_c, 1)
            pool.wait_ge(v_deg, 4)
            pool.tensor_tensor(dinv[:], deg[:, 2], m.neg_half[:, 0:NT], ALU.pow).then_inc(p_dinv, 1)

        @block.scalar
        def _(act):
            act.wait_ge(small_in, 80)
            act.activation(ea[:], al[:], ACT.Exp, scale=-1.0).then_inc(exp_a, 1)
            for q in range(NT):
                act.wait_ge(t_LT, q + 1)
                act.copy(LTf[:, q], bank[q][:]).then_inc(c_LTf, 1)
            for q in range(NT):
                act.wait_ge(c_LTf, q + 1)
                act.copy(m.LT[0][:, q], LTf[:, q]).then_inc(c_LTh, 1)
            act.wait_ge(p_dinv, 1)
            for q in range(NT):
                act.wait_ge(t_Ah, q + 1)
                act.activation(m.AhT[0][:, q], bank[q][:], ACT.Copy, scale=dinv[:, q:q + 1]).then_inc(c_Ahh, 1)
            for q in range(NT):
                act.wait_ge(t_L2, q + 1)
                act.copy(m.L2T[0][:, q], bank[q][:]).then_inc(c_L2h, 1)
            for q in range(NT):
                act.wait_ge(t_L3, q + 1)
                act.copy(m.L3T[0][:, q], bank[q][:]).then_inc(c_L3h, 1)

        @block.vector
        def _(dve):
            dve.wait_ge(pool_c, 4)
            dve.tensor_copy(m.identb[:], m.ident[:]).then_inc(ident_b, 1)
            dve.wait_ge(small_in, 80)
            dve.tensor_scalar(d_col[:], d_col[:], 0.0, 1.0, ALU.max, ALU.min).then_inc(v_dc, 1)
            dve.tensor_scalar(bB[:], ones[:], b_col[:], None, ALU.mult).then_inc(v_bB, 1)
            dve.wait_ge(exp_a, 1)
            dve.tensor_scalar(col[:, 3, :], ea[:], 1.0, None, ALU.add).then_inc(v_col, 1)
            dve.wait_ge(v_col, 1)
            dve.reciprocal(col[:, 4, :], col[:, 3, :]).then_inc(v_col, 1)
            dve.wait_ge(v_col, 2)
            dve.tensor_scalar(c_c, col[:, 4, :], DT / 2, None, ALU.mult).then_inc(v_col, 1)
            dve.wait_ge(v_col, 3)
            dve.tensor_scalar(c_d, c_c, -1.0, 1.0 - DT, ALU.mult, ALU.add).then_inc(v_col, 1)
            dve.wait_ge(v_col, 4)
            dve.wait_ge(a_in, 16)
            for t in range(NT):
                dve.tensor_scalar(L[:, t], A[:, t], c_c[:, t:t + 1], None, ALU.mult).then_inc(v_L, 1)
            dve.wait_ge(v_L, NT)
            for t in range(NT):
                s = slice(t * P, t * P + P)
                dve.scalar_tensor_tensor(out=L[:, t, s], in0=m.ident[:], scalar=c_d[:, t:t + 1], in1=L[:, t, s],
                                         op0=ALU.mult, op1=ALU.add).then_inc(v_L, 1)
            dve.wait_ge(t_wT, 1)
            dve.tensor_copy(wT[:], bank[4][:, 0:D]).then_inc(v_wT, 1)
            dve.wait_ge(v_dc, 1)
            dve.wait_ge(v_wT, 1)
            dve.tensor_scalar(wTs[:], wT[:], d_col[:], DT, ALU.mult, ALU.mult).then_inc(v_wT, 1)
            dve.wait_ge(v_L, 2 * NT)
            dve.tensor_copy(flat(Lr[0][:]), flat(L[:])).then_inc(v_Lhi, 1)
            dve.wait_ge(v_Lhi, 1)
            dve.tensor_tensor(flat(Lr[1][:]), flat(L[:]), flat(Lr[0][:].bitcast(F32)), ALU.subtract).then_inc(v_Llo, 1)
            dve.tensor_scalar(flat(m.mask_ij[:]), flat(A[:]), 0.0, MASKED, ALU.is_equal, ALU.mult).then_inc(v_mij, 1)
            for q in range(NT):
                dve.wait_ge(t_AT, q + 1)
                dve.tensor_scalar(m.mask_ji[:, q], bank[q][:], 0.0, MASKED, ALU.is_equal, ALU.mult).then_inc(v_mji, 1)
            dve.tensor_copy(flat(A1[:]), flat(A[:])).then_inc(v_A1, 1)
            dve.wait_ge(v_A1, 1)
            for t in range(NT):
                s = slice(t * P, t * P + P)
                dve.tensor_tensor(A1[:, t, s], A[:, t, s], m.ident[:], ALU.add).then_inc(v_A1, 1)
            dve.wait_ge(v_A1, 1 + NT)
            for t in range(NT):
                s = slice(t * P, t * P + P)
                dve.tensor_tensor_reduce(out=junk[:], in0=A1[:, t, s], in1=m.ident[:], scale=1.0, scalar=0.0,
                                         op0=ALU.mult, op1=ALU.add, accum_out=diag[:, t:t + 1]).then_inc(v_A1, 1)
                dve.wait_ge(v_A1, 2 + NT + t)
            dve.tensor_reduce(deg[:, 0], A1[:], AX.X, ALU.add).then_inc(v_deg, 1)
            dve.wait_ge(v_deg, 1)
            dve.tensor_tensor(deg[:, 1], deg[:, 0], diag[:], ALU.subtract).then_inc(v_deg, 1)
            dve.tensor_copy(RP[:, 0], m.ident[:]).then_inc(v_R, 1)
            for k, (a, n) in enumerate(((1, 1), (2, 1), (3, 2), (5, 4))):
                dve.wait_ge(t_R, k + 1)
                dve.tensor_copy(flat(RP[:, a:a + n]), bank[5 + k % 2][:, 0:n * D]).then_inc(v_R, 1)
            dve.wait_ge(v_deg, 2)
            dve.wait_ge(t_cs, 1)
            dve.tensor_tensor(deg[:, 2], deg[:, 1], bank[7][:, 0:NT], ALU.add).then_inc(v_deg, 2)
            for q in range(NT):
                dve.wait_ge(c_LTh, q + 1)
                dve.tensor_tensor(m.LT[1][:, q], LTf[:, q], m.LT[0][:, q].bitcast(F32), ALU.subtract).then_inc(v_LTl, 1)
            dve.tensor_reduce(Y[:, 0], L[:], AX.X, ALU.add).then_inc(v_Y1, 1)
            dve.wait_ge(p_dinv, 1)
            for t in range(NT):
                dve.tensor_scalar(A1[:, t], A1[:, t], dinv[:, t:t + 1], None, ALU.mult).then_inc(v_As, 1)
            for q in range(NT):
                dve.wait_ge(c_Ahh, q + 1)
                dve.scalar_tensor_tensor(out=m.AhT[1][:, q], in0=bank[q][:], scalar=dinv[:, q:q + 1],
                                         in1=m.AhT[0][:, q].bitcast(F32), op0=ALU.mult,
                                         op1=ALU.subtract).then_inc(v_Ahl, 1)
            for q in range(NT):
                dve.wait_ge(c_L2h, q + 1)
                dve.tensor_tensor(m.L2T[1][:, q], bank[q][:], m.L2T[0][:, q].bitcast(F32), ALU.subtract).then_inc(v_L2l, 1)
            dve.wait_ge(t_Q, 3)

            def in_bank(first, k):
                return bank[first + 2][:, 0:D] if k == 0 else bank[first + (k - 1) // 4][:, (k - 1) % 4 * D:(k - 1) % 4 * D + D]

            for j in range(9):
                dve.tensor_scalar(Pf[:, j], in_bank(4, 8 - j), float(comb(8, j)), None, ALU.mult).then_inc(v_P, 1)
            nP = 9
            for k in range(8):
                dve.wait_ge(v_P, nP)
                for j in range(8 - k):
                    dve.scalar_tensor_tensor(out=Pf[:, j], in0=RP[:, k], scalar=DT * comb(j + k, j), in1=Pf[:, j],
                                             op0=ALU.mult, op1=ALU.add).then_inc(v_P, 1)
                    nP += 1
            dve.wait_ge(v_P, nP)
            dve.tensor_tensor(Pf[:, 0], Pf[:, 0], m.ident[:], ALU.add).then_inc(v_P, 1)
            dve.wait_ge(v_P, nP + 1)
            dve.tensor_copy(flat(m.Pj[0][:]), flat(Pf[:])).then_inc(v_P, 1)
            dve.wait_ge(v_P, nP + 2)
            dve.tensor_tensor(flat(m.Pj[1][:]), flat(Pf[:]), flat(m.Pj[0][:].bitcast(F32)), ALU.subtract).then_inc(v_P, 1)
            dve.wait_ge(t_cB, 3)
            for j in range(9):
                dve.tensor_scalar(cB[:, j], in_bank(4, 8 - j), float(comb(8, j)), None, ALU.mult).then_inc(v_cB, 1)
            dve.wait_ge(t_Y2, 1)
            dve.tensor_copy(Y[:, 1], bank[7][:, 8:8 + NT]).then_inc(v_Y2, 1)
            dve.wait_ge(v_Y2, 1)
            dve.wait_ge(v_cB, 9)
            c_view = cB[:].rearrange("p (g i) d -> p g i d", i=BABY)
            for i in (1, 2):
                for t in range(NT):
                    dve.scalar_tensor_tensor(out=m.bias[:, t], in0=c_view[:, :, i], scalar=Y[:, i - 1, t:t + 1],
                                             in1=c_view[:, :, 0] if i == 1 else m.bias[:, t],
                                             op0=ALU.mult, op1=ALU.add).then_inc(v_bias, 1)
                dve.wait_ge(v_bias, NT * i)
            for q in range(NT):
                dve.wait_ge(c_L3h, q + 1)
                dve.tensor_tensor(m.L3T[1][:, q], bank[q][:], m.L3T[0][:, q].bitcast(F32), ALU.subtract).then_inc(v_L3l, 1)

        @block.tensor
        def _(pe):
            def transposes(src, done):
                for q in range(NT):
                    for t in range(NT):
                        last = pe.transpose(bank[q][:, t * P:t * P + P], src[:, t, q * P:q * P + P], m.ident[:])
                    last.then_inc(done, 1)

            pe.wait_ge(pool_c, 4)
            pe.wait_ge(a_in, 16)
            transposes(A, t_AT)
            pe.wait_ge(small_in, 80)
            pe.transpose(bank[4][:, 0:D], w_sb[:], m.ident[:]).then_inc(t_wT, 1)
            pe.wait_ge(v_mji, NT)
            pe.wait_ge(v_L, 2 * NT)
            transposes(L, t_LT)
            pe.wait_ge(v_wT, 2)
            pe.matmul(bank[5][:, 0:D], wTs[:], wT[:], start=True, stop=True).then_inc(t_R, 1)
            pe.wait_ge(v_R, 2)
            pe.matmul(bank[6][:, 0:D], RP[:, 1], RP[:, 1], start=True, stop=True).then_inc(t_R, 1)
            pe.wait_ge(v_A1, 1 + NT)
            for q in range(NT):
                for t in range(NT):
                    last = pe.matmul(bank[7][:, q:q + 1], A1[:, t, q * P:q * P + P], ones[:, 0:1],
                                     start=(t == 0), stop=(t == NT - 1))
            last.then_inc(t_cs, 1)
            pe.wait_ge(v_R, 3)
            pe.matmul(bank[5][:, 0:2 * D], RP[:, 2], flat(RP[:, 1:3]), start=True, stop=True).then_inc(t_R, 1)
            pe.wait_ge(v_R, 4)
            pe.matmul(bank[6][:, 0:4 * D], RP[:, 4], flat(RP[:, 1:5]), start=True, stop=True).then_inc(t_R, 1)
            pe.wait_ge(c_LTf, NT)
            pe.wait_ge(v_As, NT)
            transposes(A1, t_Ah)
            pe.wait_ge(v_Y1, 1)
            for t in range(NT):
                for q in range(NT):
                    last = pe.matmul(bank[7][:, 8 + t:9 + t], LTf[:, q, t * P:t * P + P], Y[:, 0, q:q + 1],
                                     start=(q == 0), stop=(q == NT - 1))
            last.then_inc(t_Y2, 1)

            def against_powers(stationary, done):
                for k, r in enumerate((RP[:, 1:5], RP[:, 5:9], RP[:, 0:1])):
                    pe.matmul(bank[4 + k][:, 0:r.shape[1] * D], stationary, flat(r), start=True, stop=True).then_inc(done, 1)

            pe.wait_ge(v_R, 5)
            against_powers(fc[:], t_Q)
            pe.wait_ge(v_Llo, 1)
            for power, (mov, done, ready, freed) in enumerate(((m.LT, t_L2, v_LTl, v_Ahl), (m.L2T, t_L3, v_L2l, v_L2l))):
                pe.wait_ge(ready, NT)
                for q in range(NT):
                    pe.wait_ge(freed, q + 1)
                    for k in range(NT):
                        s = slice(q * P, q * P + P)
                        last = three_pass(pe, bank[q][:], (Lr[0][:, k, s], Lr[1][:, k, s]),
                                          (mov[0][:, k], mov[1][:, k]), start=(k == 0), stop=(k == NT - 1))
                    last.then_inc(done, 1)
                if power == 0:
                    pe.wait_ge(v_P, 9)
                    pe.wait_ge(v_bB, 1)
                    against_powers(bB[:], t_cB)

    nc.clear_and_free_semaphores(sems)
    nc.all_engine_barrier()


def pairs(eng, steps, depth, step):
    def alive(s):
        return [0 <= s - k < steps for k in range(depth)]

    lead = (depth - 1) + (depth - 1) % 2
    for s in range(lead):
        step(s, s % 2, alive(s), s // 2)
    with eng.Fori(lead // 2, steps // 2) as r:
        for parity in range(2):
            step(r * 2 + parity, parity, [True] * depth, r)
    for s in range(steps, steps + depth - 1):
        step(s, s % 2, alive(s), s // 2)


def tile_of(X, b, t):
    return X[:, bass.ds(b, 1), t].rearrange("p a d -> p (a d)")


def batch_of(X, b):
    return X[:, bass.ds(b, 1)].rearrange("p a t d -> p (a t) d")


def batch_flat(X, b):
    return X[:, bass.ds(b, 1)].rearrange("p a t d -> p (a t d)")


class Norm:

    def __init__(self, nc, ctx, m, name):
        self.m = m
        self.stats = [ctx.enter_context(nc.sbuf_tensor(f"{name}_stats{k}", [P, 4, 6], F32)) for k in range(2)]
        self.aggr = [ctx.enter_context(nc.sbuf_tensor(f"{name}_aggr{k}", [P, 4, 2], F32)) for k in range(2)]
        self.rstd = [ctx.enter_context(nc.sbuf_tensor(f"{name}_rstd{k}", [P, 4], F32)) for k in range(2)]
        self.gate = ctx.enter_context(nc.semaphore(f"{name}_gate"))
        self.s_stats, self.s_aggr, self.s_eps, self.s_rstd, self.s_x = (
            ctx.enter_context(nc.semaphore(f"{name}_{x}")) for x in ("stats", "aggr", "eps", "rstd", "x"))

    def credit_dve(self, dve, per=1):
        dve.sem_inc(self.s_stats, 4 * CREDIT * per)
        dve.sem_inc(self.s_aggr, 4 * CREDIT * per)
        dve.sem_inc(self.s_x, 4 * CREDIT * per)

    def credit_pool(self, pool, per=1):
        pool.sem_inc(self.s_eps, CREDIT * per)
        pool.sem_inc(self.s_rstd, CREDIT * per)

    def statistics(self, dve, i, parity, r):
        dve.wait_ge(self.s_eps, i - 1)
        for k in range(4):
            dve.bn_stats(self.stats[parity][:, k], r[:, k]).then_inc(self.s_stats, 1)
        dve.wait_ge(self.s_stats, i * 4 + 4)
        hold(dve, self.gate)
        for k in range(4):
            dve.bn_aggr(self.aggr[parity][:, k], self.stats[parity][:, k]).then_inc(self.s_aggr, 1)

    def root(self, pool, i, parity):
        rstd = self.rstd[parity]
        pool.wait_ge(self.s_aggr, i * 4 + 4)
        pool.wait_ge(self.s_x, (i - 1) * 4)
        hold(pool, self.gate)
        pool.tensor_scalar(rstd[:], self.aggr[parity][:, :, 1], EPS, 1.0, ALU.add, ALU.mult).then_inc(self.s_eps, 1)
        pool.wait_ge(self.s_eps, i + 1)
        pool.tensor_tensor(rstd[:], rstd[:], self.m.neg_half[:, 0:4], ALU.pow).then_inc(self.s_rstd, 1)

    def apply(self, dve, i, parity, r, out):
        dve.wait_ge(self.s_rstd, i + 1)
        for k in range(4):
            dve.tensor_scalar(out(k), r[:, k], self.aggr[parity][:, k, 0:1], self.rstd[parity][:, k:k + 1],
                              ALU.subtract, ALU.mult).then_inc(self.s_x, 1)


def layer0(nc, m, bank):
    GB = 4
    groups = B // GB
    with ExitStack() as own:
        def sb(name, shape, dt=F32):
            return own.enter_context(nc.sbuf_tensor(name, shape, dt))

        def sem(name):
            return own.enter_context(nc.semaphore(name))

        Xf = [sb(f"Xf{k}", [P, NT, D]) for k in range(2)]
        Xr = [[sb(f"Xr{k}{h}", [P, NT, D], F32R) for h in range(2)] for k in range(2)]
        yT = [[[sb(f"yT{k}{i}{h}", [P, N], F32R) for h in range(2)] for i in range(BABY)] for k in range(2)]
        G = sb("G", [P, BABY, NT, GB * D])
        z = [sb(f"z{h}", [P, NT, GB * D], F32R) for h in range(2)]
        zf = [sb(f"zf{k}", [P, GB * D]) for k in range(2)]
        norm = Norm(nc, own, m, "n0")

        gate = sem("gate")
        x_st = [sem(f"x_staged{k}") for k in range(2)]
        x_hi = sem("x_high")
        x_lo = sem("x_low")
        y_ps = sem("y_in_psum")
        y_hi = sem("y_high")
        y_lo = sem("y_low")
        g_ps = sem("g_in_psum")
        g_sb = sem("g_out")
        z_hi = sem("z_high")
        z_lo = sem("z_low")
        h_ps = sem("h_in_psum")
        h_sb = sem("h_out")
        psum_y, psum_g, psum_h = bank[0:3], bank[3:5], bank[5:7]
        P_of = [p[:].rearrange("p (g i) d -> p g i d", i=BABY) for p in m.Pj]
        block = own.enter_context(nc.Block())

        @block.sync
        def _(sp):
            with sp.Fori(0, B // 2) as r:
                for par in range(2):
                    b = r * 2 + par
                    sp.wait_ge(x_lo, after(b - 2, 1))
                    sp.wait_ge(y_ps, after(b - 2, BABY, 1))
                    hold(sp, gate)
                    sp.dma_start(Xf[par][:], batch_of(m.X, b)).then_inc(x_st[par], 16)

        @block.scalar
        def _(act):
            act.sem_inc(x_hi, CREDIT)
            act.sem_inc(y_hi, CREDIT * BABY)
            act.sem_inc(z_hi, CREDIT * 2 * NT)

            def x_high(b, par, nth):
                act.wait_ge(x_st[par], 16 * nth + 16)
                act.wait_ge(y_ps, after(b - 2, BABY))
                act.copy(flat(Xr[par][0][:]), flat(Xf[par][:])).then_inc(x_hi, 1)

            with act.Fori(0, groups) as g:
                for bb in range(GB):
                    b, par = g * GB + bb, bb % 2
                    if bb == 0:
                        x_high(b, par, g * (GB // 2))
                    for i in range(BABY):
                        act.wait_ge(y_ps, after(b, BABY, i + 1))
                        act.wait_ge(g_ps, after(b - 2, NT))
                        act.copy(yT[par][i][0][:], psum_y[i][:]).then_inc(y_hi, 1)
                    if bb + 1 < GB:
                        x_high(b + 1, 1 - par, g * (GB // 2) + (bb + 1) // 2)
                for t in range(NT):
                    act.wait_ge(g_sb, after(g * GB + GB - 1, NT, t + 1))
                    act.wait_ge(h_ps, after(g - 1, 2 * NT))
                    act.copy(z[0][:, t], G[:, 2, t]).then_inc(z_hi, 1)
                act.wait_ge(h_ps, after(g, 2 * NT, NT))
                for t in range(NT):
                    act.wait_ge(h_sb, after(g, 2 * NT, t + 1))
                    act.copy(z[0][:, t], zf[t % 2][:]).then_inc(z_hi, 1)

        @block.gpsimd
        def _(pool):
            norm.credit_pool(pool, NT)
            with pool.Fori(0, groups) as g:
                for t in range(NT):
                    norm.root(pool, (g + CREDIT) * NT + t, t % 2)

        @block.vector
        def _(dve):
            dve.sem_inc(x_lo, CREDIT)
            dve.sem_inc(y_lo, CREDIT * BABY)
            dve.sem_inc(g_sb, CREDIT * NT)
            dve.sem_inc(z_lo, CREDIT * 2 * NT)
            dve.sem_inc(h_sb, CREDIT * 2 * NT)
            norm.credit_dve(dve, NT)

            def x_low(b, par):
                dve.wait_ge(x_hi, after(b, 1))
                dve.tensor_tensor(flat(Xr[par][1][:]), flat(Xf[par][:]), flat(Xr[par][0][:].bitcast(F32)),
                                  ALU.subtract).then_inc(x_lo, 1)

            def z_low(g, t, src, k):
                dve.wait_ge(z_hi, after(g, 2 * NT, k))
                dve.tensor_tensor(z[1][:, t], src, z[0][:, t].bitcast(F32), ALU.subtract).then_inc(z_lo, 1)

            with dve.Fori(0, groups) as g:
                for bb in range(GB):
                    b, par = g * GB + bb, bb % 2
                    if bb == 0:
                        x_low(b, par)
                    for i in range(BABY):
                        dve.wait_ge(y_hi, after(b, BABY, i + 1))
                        dve.tensor_tensor(yT[par][i][1][:], psum_y[i][:], yT[par][i][0][:].bitcast(F32),
                                          ALU.subtract).then_inc(y_lo, 1)
                    if bb + 1 < GB:
                        x_low(b + 1, 1 - par)
                    for t in range(NT):
                        dve.wait_ge(g_ps, after(b, NT, t + 1))
                        dve.tensor_tensor(G[:, :, t, bb * D:bb * D + D],
                                          psum_g[t % 2][:, 0:BABY * D].rearrange("p (g d) -> p g d", g=BABY),
                                          m.bias[:, t], ALU.add).then_inc(g_sb, 1)
                for t in range(NT):
                    z_low(g, t, G[:, 2, t], t + 1)
                for t in range(NT):
                    dve.wait_ge(h_ps, after(g, 2 * NT, t + 1))
                    if t >= 2:
                        dve.wait_ge(z_lo, after(g, 2 * NT, NT + t - 1))
                    dve.tensor_tensor(zf[t % 2][:], psum_h[t % 2][:], G[:, 1, t], ALU.add).then_inc(h_sb, 1)
                    if t >= 1:
                        z_low(g, t - 1, zf[(t - 1) % 2][:], NT + t)
                z_low(g, NT - 1, zf[(NT - 1) % 2][:], 2 * NT)
                for t in range(NT):
                    i = (g + CREDIT) * NT + t
                    dve.wait_ge(h_ps, after(g, 2 * NT, NT + t + 1))
                    if t < 2:
                        dve.wait_ge(z_lo, after(g, 2 * NT, 2 * NT - 1 + t))
                    else:
                        dve.wait_ge(norm.s_x, (i - 1) * 4)
                    dve.tensor_tensor(zf[t % 2][:], psum_h[t % 2][:], G[:, 0, t], ALU.add).then_inc(h_sb, 1)
                    dve.wait_ge(h_sb, after(g, 2 * NT, NT + t + 1))
                    norm.statistics(dve, i, t % 2, zf[t % 2][:].rearrange("p (b d) -> p b d", b=GB))
                    if t >= 1:
                        norm.apply(dve, i - 1, (t - 1) % 2, zf[(t - 1) % 2][:].rearrange("p (b d) -> p b d", b=GB),
                                   lambda k: tile_of(m.X, g * GB + k, t - 1))
                norm.apply(dve, i, t % 2, zf[t % 2][:].rearrange("p (b d) -> p b d", b=GB),
                           lambda k: tile_of(m.X, g * GB + k, t))

        @block.tensor
        def _(pe):
            pe.sem_inc(y_ps, CREDIT * BABY)
            pe.sem_inc(g_ps, CREDIT * NT)
            pe.sem_inc(h_ps, CREDIT * 2 * NT)
            with pe.Fori(0, groups) as g:
                for bb in range(GB):
                    b, par = g * GB + bb, bb % 2
                    pe.wait_ge(x_st[par], (g * (GB // 2) + bb // 2) * 16 + 16)
                    pe.wait_ge(y_lo, after(b - 1, BABY, 1))
                    for t in range(NT):
                        last = pe.transpose(psum_y[0][:, t * P:t * P + P], Xf[par][:, t], m.ident[:])
                    last.then_inc(y_ps, 1)
                    pe.wait_ge(x_lo, after(b, 1))
                    for i, mat in ((1, m.LT), (2, m.L2T)):
                        pe.wait_ge(y_lo, after(b - 1, BABY, i + 1))
                        for k in range(NT):
                            last = three_pass(pe, psum_y[i][:], [h[:, k] for h in Xr[par]], [h[:, k] for h in mat],
                                              start=(k == 0), stop=(k == NT - 1))
                        last.then_inc(y_ps, 1)
                    for t in range(NT):
                        pe.wait_ge(y_lo, after(b, BABY))
                        pe.wait_ge(g_sb, after(b, NT, t - 1))
                        for i in range(BABY):
                            last = three_pass(pe, psum_g[t % 2][:, 0:BABY * D],
                                              [h[:, t * P:t * P + P] for h in yT[par][i]],
                                              [h[:, :, i] for h in P_of], start=(i == 0), stop=(i == BABY - 1))
                        last.then_inc(g_ps, 1)
                for k in range(2 * NT):
                    t = k % NT
                    pe.wait_ge(z_lo, after(g, 2 * NT, NT if k < NT else 2 * NT))
                    pe.wait_ge(h_sb, after(g, 2 * NT, k - 1))
                    for q in range(NT):
                        last = three_pass(pe, psum_h[k % 2][:], [h[:, q, t * P:t * P + P] for h in m.L3T],
                                          [h[:, q] for h in z], start=(q == 0), stop=(q == NT - 1))
                    last.then_inc(h_ps, 1)


def split(dve, high, low, src, s_high, n_high, s_low):
    dve.tensor_copy(high, src).then_inc(s_high, 1)
    dve.wait_ge(s_high, n_high)
    return dve.tensor_tensor(low, src, high.bitcast(F32), ALU.subtract).then_inc(s_low, 1)


def layer1(nc, m, ins, bank):
    with ExitStack() as own:
        def sb(name, shape, dt=F32):
            return own.enter_context(nc.sbuf_tensor(name, shape, dt))

        W1T = [sb(f"W1T{h}", [P, CH, P], F32R) for h in range(2)]
        W2T = [sb(f"W2T{h}", [P, CH, P], F32R) for h in range(2)]
        par1 = sb("par1", [P, 3, CH])
        par2 = sb("par2", [P, 3, 1])
        Hb = sb("Hb", [P, CH, B, N])
        O = sb("O", [P, B, N])
        st1 = sb("st1", [P, CH, B, 6])
        st2 = sb("st2", [P, 1, B, 6])
        aff1 = sb("aff1", [P, 2, CH])
        aff2 = sb("aff2", [P, 2, 1])
        layer1_first(nc, m, ins, bank, W1T, W2T, par1, par2, Hb, st1)
        batch_norm_affine(nc, m, "bn1", st1, par1, aff1, CH)
        layer1_second(nc, m, bank, W2T, par2, Hb, aff1, O, st2)
        batch_norm_affine(nc, m, "bn2", st2, par2, aff2, 1)
        layer1_last(nc, m, bank, O, aff2)


def layer1_first(nc, m, ins, bank, W1T, W2T, par1, par2, Hb, st1):
    with ExitStack() as own:
        def sb(name, shape, dt=F32):
            return own.enter_context(nc.sbuf_tensor(name, shape, dt))

        def sem(name):
            return own.enter_context(nc.semaphore(name))

        w1 = sb("w1", [P, CH, D])
        w2 = sb("w2", [P, CH, P])
        wf = sb("wf", [P, 2, CH, P])
        Xr = [[sb(f"Xa{k}{h}", [P, NT, D], F32R) for h in range(2)] for k in range(2)]
        agT = [[sb(f"agT{k}{h}", [P, N], F32R) for h in range(2)] for k in range(2)]
        w_in = sem("w_in")
        w_ps = sem("w_in_psum"); w_sb = sem("w_out"); w_hi = sem("w_high"); w_lo = sem("w_low")
        x_hi = sem("x_high"); x_lo = sem("x_low")
        a_ps = sem("agg_in_psum"); a_hi = sem("agg_high"); a_lo = sem("agg_low")
        h_ps = sem("h_in_psum"); h_sb = sem("h_out"); h_st = sem("h_stats")
        block = own.enter_context(nc.Block())

        @block.sync
        def _(sp):
            sp.dma_start(w1[:], ins["L1_gnn_W1"].rearrange("(c p) d -> p c d", p=P)).then_inc(w_in, 16)
            sp.dma_start(flat(w2[:]), ins["L1_gnn_W2"]).then_inc(w_in, 16)
            with nc.allow_non_contiguous_dma(reason="a few hundred words once"):
                for k, n in enumerate(("b1", "g1", "be1")):
                    sp.dma_start(par1[:, k], ins[f"L1_gnn_{n}"].rearrange("(c p) -> p c", p=P)).then_inc(w_in, 16)
                for k, n in enumerate(("b2", "g2", "be2")):
                    sp.dma_start(par2[:, k], ins[f"L1_gnn_{n}"].rearrange("(p a) -> p a", a=1)).then_inc(w_in, 16)
            sp.wait_ge(w_in, 8 * 16)

        @block.scalar
        def _(act):
            for s in (x_hi, a_hi):
                act.sem_inc(s, CREDIT)
            act.sem_inc(h_sb, CREDIT * CH)
            act.wait_ge(w_in, 8 * 16)

            def step(s, par, alive, nth):
                if alive[0]:
                    act.wait_ge(a_ps, after(s - 2, 1))
                    act.copy(flat(Xr[par][0][:]), batch_flat(m.X, s)).then_inc(x_hi, 1)
                    act.wait_ge(a_ps, after(s, 1))
                    act.wait_ge(h_ps, after(s - 2, CH))
                    act.copy(agT[par][0][:], bank[par][:]).then_inc(a_hi, 1)
                if alive[1]:
                    b = s - 1
                    for c in range(CH):
                        act.wait_ge(h_ps, after(b, CH, c + 1))
                        act.activation(Hb[:, c, bass.ds(b, 1)].rearrange("p a n -> p (a n)"),
                                       bank[2 + 2 * (1 - par) + c][:], ACT.Identity,
                                       bias=par1[:, 0, c:c + 1]).then_inc(h_sb, 1)

            pairs(act, B, 2, step)

        @block.vector
        def _(dve):
            for s in (x_lo, a_lo):
                dve.sem_inc(s, CREDIT)
            dve.sem_inc(h_st, CREDIT * CH)
            dve.wait_ge(w_ps, 2 * CH)
            dve.tensor_copy(wf[:].rearrange("p a c o -> p (a c o)"), bank[7][:, 0:2 * CH * P]).then_inc(w_sb, 1)
            dve.wait_ge(w_sb, 1)
            split(dve, flat(W1T[0][:]), flat(W1T[1][:]), flat(wf[:, 0]), w_hi, 1, w_lo)
            split(dve, flat(W2T[0][:]), flat(W2T[1][:]), flat(wf[:, 1]), w_hi, 2, w_lo)

            def step(s, par, alive, nth):
                if alive[0]:
                    dve.wait_ge(x_hi, after(s, 1))
                    dve.tensor_tensor(flat(Xr[par][1][:]), batch_flat(m.X, s), flat(Xr[par][0][:].bitcast(F32)),
                                      ALU.subtract).then_inc(x_lo, 1)
                    dve.wait_ge(a_hi, after(s, 1))
                    dve.tensor_tensor(agT[par][1][:], bank[par][:], agT[par][0][:].bitcast(F32),
                                      ALU.subtract).then_inc(a_lo, 1)
                if alive[1]:
                    b = s - 1
                    for c in range(CH):
                        dve.wait_ge(h_sb, after(b, CH, c + 1))
                        dve.bn_stats(st1[:, c, bass.ds(b, 1)].rearrange("p a n -> p (a n)"),
                                     Hb[:, c, bass.ds(b, 1)].rearrange("p a n -> p (a n)")).then_inc(h_st, 1)

            pairs(dve, B, 2, step)

        @block.tensor
        def _(pe):
            pe.sem_inc(a_ps, CREDIT)
            pe.sem_inc(h_ps, CREDIT * CH)
            pe.wait_ge(w_in, 8 * 16)
            for k, w in enumerate((w1, w2)):
                for c in range(CH):
                    pe.transpose(bank[7][:, (k * CH + c) * P:(k * CH + c + 1) * P], w[:, c], m.ident[:]).then_inc(w_ps, 1)

            def step(s, par, alive, nth):
                if alive[0]:
                    pe.wait_ge(x_lo, after(s, 1))
                    pe.wait_ge(a_lo, after(s - 2, 1))
                    for k in range(NT):
                        last = three_pass(pe, bank[par][:], [h[:, k] for h in Xr[par]], [h[:, k] for h in m.AhT],
                                          start=(k == 0), stop=(k == NT - 1))
                    last.then_inc(a_ps, 1)
                if alive[1]:
                    b = s - 1
                    pe.wait_ge(a_lo, after(b, 1))
                    pe.wait_ge(w_lo, 2)
                    for c in range(CH):
                        pe.wait_ge(h_sb, after(b - 2, CH, c + 1))
                        three_pass(pe, bank[2 + 2 * (1 - par) + c][:], [h[:, c] for h in W1T],
                                   [h[:] for h in agT[1 - par]]).then_inc(h_ps, 1)

            pairs(pe, B, 2, step)


def batch_norm_affine(nc, m, name, st, par, aff, channels):
    with ExitStack() as own:
        mv = own.enter_context(nc.sbuf_tensor(f"{name}_mv", [P, channels, 2], F32))
        ve = own.enter_context(nc.sbuf_tensor(f"{name}_ve", [P, channels], F32))
        ms = own.enter_context(nc.sbuf_tensor(f"{name}_ms", [P, channels], F32))
        agg = own.enter_context(nc.semaphore(f"{name}_agg"))
        root = own.enter_context(nc.semaphore(f"{name}_root"))
        out = own.enter_context(nc.semaphore(f"{name}_out"))
        block = own.enter_context(nc.Block())

        @block.vector
        def _(dve):
            for c in range(channels):
                dve.bn_aggr(mv[:, c], st[:, c].rearrange("p b s -> p (b s)")).then_inc(agg, 1)
            dve.wait_ge(root, 2)
            dve.tensor_tensor(aff[:, 0], ve[:], par[:, 1], ALU.mult).then_inc(out, 1)
            dve.wait_ge(out, 1)
            dve.tensor_tensor(ms[:], mv[:, :, 0], aff[:, 0], ALU.mult).then_inc(out, 1)
            dve.wait_ge(out, 2)
            dve.tensor_tensor(aff[:, 1], par[:, 2], ms[:], ALU.subtract).then_inc(out, 1)

        @block.gpsimd
        def _(pool):
            pool.wait_ge(agg, channels)
            pool.tensor_scalar(ve[:], mv[:, :, 1], EPS, 1.0, ALU.add, ALU.mult).then_inc(root, 1)
            pool.wait_ge(root, 1)
            pool.tensor_tensor(ve[:], ve[:], m.neg_half[:, 0:channels], ALU.pow).then_inc(root, 1)


def layer1_second(nc, m, bank, W2T, par2, Hb, aff1, O, st2):
    with ExitStack() as own:
        def sb(name, shape, dt=F32):
            return own.enter_context(nc.sbuf_tensor(name, shape, dt))

        def sem(name):
            return own.enter_context(nc.semaphore(name))

        hf = [sb(f"hf{k}", [P, CH, N]) for k in range(2)]
        hr = [[sb(f"hr{k}{h}", [P, CH, N], F32R) for h in range(2)] for k in range(2)]
        relu = sem("relu"); h_hi = sem("h_high"); h_lo = sem("h_low")
        o_ps = sem("o_in_psum"); o_sb = sem("o_out"); o_st = sem("o_stats")
        block = own.enter_context(nc.Block())

        @block.scalar
        def _(act):
            act.sem_inc(relu, CREDIT * CH)
            act.sem_inc(o_sb, CREDIT)

            def step(s, par, alive, nth):
                if alive[0]:
                    for c in range(CH):
                        act.wait_ge(h_lo, after(s - 2, CH, c + 1))
                        act.activation(hf[par][:, c], Hb[:, c, bass.ds(s, 1)].rearrange("p a n -> p (a n)"), ACT.Relu,
                                       scale=aff1[:, 0, c:c + 1], bias=aff1[:, 1, c:c + 1]).then_inc(relu, 1)
                if alive[1]:
                    b = s - 1
                    act.wait_ge(o_ps, after(b, 1))
                    act.activation(O[:, bass.ds(b, 1)].rearrange("p a n -> p (a n)"), bank[1 - par][:], ACT.Identity,
                                   bias=par2[:, 0, 0:1]).then_inc(o_sb, 1)

            pairs(act, B, 2, step)

        @block.vector
        def _(dve):
            dve.sem_inc(h_hi, CREDIT * CH)
            dve.sem_inc(h_lo, CREDIT * CH)
            dve.sem_inc(o_st, CREDIT)

            def step(s, par, alive, nth):
                if alive[0]:
                    dve.wait_ge(o_ps, after(s - 2, 1))
                    for c in range(CH):
                        dve.wait_ge(relu, after(s, CH, c + 1))
                        split(dve, hr[par][0][:, c], hr[par][1][:, c], hf[par][:, c], h_hi, after(s, CH, c + 1), h_lo)
                if alive[1]:
                    b = s - 1
                    dve.wait_ge(o_sb, after(b, 1))
                    dve.bn_stats(st2[:, 0, bass.ds(b, 1)].rearrange("p a n -> p (a n)"),
                                 O[:, bass.ds(b, 1)].rearrange("p a n -> p (a n)")).then_inc(o_st, 1)

            pairs(dve, B, 2, step)

        @block.tensor
        def _(pe):
            pe.sem_inc(o_ps, CREDIT)

            def step(s, par, alive, nth):
                pe.wait_ge(o_sb, after(s - 2, 1))
                for c in range(CH):
                    pe.wait_ge(h_lo, after(s, CH, c + 1))
                    last = three_pass(pe, bank[par][:], [h[:, c] for h in W2T], [h[:, c] for h in hr[par]],
                                      start=(c == 0), stop=(c == CH - 1))
                last.then_inc(o_ps, 1)

            pairs(pe, B, 1, step)


def layer1_last(nc, m, bank, O, aff2):
    with ExitStack() as own:
        def sb(name, shape, dt=F32):
            return own.enter_context(nc.sbuf_tensor(name, shape, dt))

        def sem(name):
            return own.enter_context(nc.semaphore(name))

        on = [sb(f"on{k}", [P, N]) for k in range(2)]
        r = [sb(f"r{k}", [P, NT, D]) for k in range(2)]
        norm = Norm(nc, own, m, "n1")
        bn = sem("normed"); t_ps = sem("turned"); res = sem("residual")
        block = own.enter_context(nc.Block())

        @block.scalar
        def _(act):
            act.sem_inc(bn, CREDIT)

            def step(s, par, alive, nth):
                act.wait_ge(t_ps, after(s - 2, 1))
                act.activation(on[par][:], O[:, bass.ds(s, 1)].rearrange("p a n -> p (a n)"), ACT.Identity,
                               scale=aff2[:, 0, 0:1], bias=aff2[:, 1, 0:1]).then_inc(bn, 1)

            pairs(act, B, 1, step)

        @block.tensor
        def _(pe):
            pe.sem_inc(t_ps, CREDIT)

            def step(s, par, alive, nth):
                pe.wait_ge(bn, after(s, 1))
                pe.wait_ge(res, after(s - 2, 1))
                for t in range(NT):
                    last = pe.transpose(bank[par][:, t * P:t * P + P], on[par][:, t * P:t * P + P], m.ident[:])
                last.then_inc(t_ps, 1)

            pairs(pe, B, 1, step)

        @block.gpsimd
        def _(pool):
            norm.credit_pool(pool)
            pairs(pool, B, 1, lambda s, par, alive, nth: norm.root(pool, s + CREDIT, par))

        @block.vector
        def _(dve):
            dve.sem_inc(res, CREDIT)
            norm.credit_dve(dve)

            def step(s, par, alive, nth):
                if alive[0]:
                    dve.wait_ge(t_ps, after(s, 1))
                    dve.wait_ge(norm.s_x, after(s - 2, 4))
                    dve.tensor_tensor(flat(r[par][:]), bank[par][:], batch_flat(m.X, s), ALU.add).then_inc(res, 1)
                    dve.wait_ge(res, after(s, 1))
                    norm.statistics(dve, s + CREDIT, par, r[par])
                if alive[1]:
                    norm.apply(dve, s - 1 + CREDIT, 1 - par, r[1 - par], lambda k: tile_of(m.X, s - 1, k))

            pairs(dve, B, 2, step)


def layer2(nc, m, ins, bank, wide):
    SCALE = float(HD) ** -0.5
    JP = NT // 2
    TILES = H * NT
    with ExitStack() as own:
        def sb(name, shape, dt=F32):
            return own.enter_context(nc.sbuf_tensor(name, shape, dt))

        def sem(name):
            return own.enter_context(nc.semaphore(name))

        W = sb("W", [P, 3 * D])
        Wr = [sb(f"Wr{h}", [P, 2 * D], F32R) for h in range(2)]
        ones = sb("ones_hd", [P, HD])
        Xf = [sb(f"Xb{k}", [P, NT, D]) for k in range(2)]
        xT = [sb(f"xT{k}", [P, N]) for k in range(2)]
        xTr = [[sb(f"xT{k}{h}", [P, N], F32R) for h in range(2)] for k in range(2)]
        qkT = [sb(f"qkT{k}", [P, 4, N], F32R) for k in range(2)]
        Q_LO, Q_HI, K_HI, K_LO = range(4)
        qk_st = [sb(f"qk_st{k}", [P, 2, H, N], F32R) for k in range(2)]
        q_st = [s[:, 0] for s in qk_st]
        k_st = [s[:, 1] for s in qk_st]
        v = [sb(f"v{k}", [P, NT, D]) for k in range(2)]
        junk = [sb(f"junk{k}", [P, N], BF16) for k in range(2)]
        mx = [sb(f"mx{k}", [P, TILES]) for k in range(2)]
        neg = [sb(f"neg{k}", [P, TILES]) for k in range(2)]
        neg_row = [sb(f"neg_row{k}", [TILES, P], F32R) for k in range(2)]
        prob = [[sb(f"prob{k}{h}", [P, 2, N]) for h in range(H)] for k in range(JP)]
        rec = sb("rec", [P, N])
        oT = [sb(f"oT{k}", [P, N]) for k in range(2)]
        r = [sb(f"rb{k}", [P, NT, D]) for k in range(2)]
        norm = Norm(nc, own, m, "n2")

        w_in = sem("w_in"); w_hi = sem("w_high"); w_lo = sem("w_low"); const = sem("const")
        x_f = sem("x_copied")
        x_ps = sem("x_turned"); x_c = sem("xT_out"); x_hi = sem("xT_high"); x_lo = sem("xT_low")
        q_ps = sem("q_in_psum"); q_hi = sem("q_high"); q_lo = sem("q_low")
        k_ps = sem("k_in_psum"); k_hi = sem("k_high"); k_lo = sem("k_low")
        v_ps = sem("v_in_psum"); v_c = sem("v_out")
        stacked = [sem(f"stacked{k}") for k in range(2)]
        s_ps = sem("scores"); s_mx = sem("row_max")
        n_sb = sem("negated"); n_ps = sem("neg_turned"); n_row = sem("neg_row_out")
        row_in = [sem(f"row_in{k}") for k in range(2)]
        t_ps = sem("scores_t"); t_exp = sem("exp_done")
        av = sem("values")
        rcp = sem("reciprocal"); o_n = sem("out_normed"); o_ps = sem("out_turned"); o_r = sem("residual")
        gate = sem("gate")
        psO, psD = bank[4], bank[5]
        even, odd = bank[6], bank[7]
        score_bank = [odd, even]
        STACKED = 3 * H * 16
        block = own.enter_context(nc.Block())

        def before(par, nth):
            return nth if par else nth - 1

        @block.sync
        def _(sp):
            sp.dma_start(W[:], ins["L2_gnn_W"]).then_inc(w_in, 16)

            def step(s, par, alive, nth):
                if alive[0]:
                    sp.wait_ge(t_ps, after(s - 2, JP * H))
                    hold(sp, gate)
                    sp.wait_ge(k_lo, after(s, 1))
                    for g, (q, k) in enumerate(((Q_HI, K_HI), (Q_HI, K_LO), (Q_LO, K_HI))):
                        for h in range(H):
                            sp.dma_start(qk_st[par][g * HD:(g + 1) * HD, :, h].bitcast(F32),
                                         qkT[par][h * HD:(h + 1) * HD, q:k + 1:k - q].bitcast(F32)
                                         ).then_inc(stacked[par], 16)
                if alive[1]:
                    sp.wait_ge(n_row, after(s - 1, 1))
                    sp.dma_start(q_st[1 - par][3 * HD:3 * HD + 1].bitcast(F32).rearrange("a h (t p) -> a (h t) p", p=P),
                                 neg_row[1 - par][:].bitcast(F32)).then_inc(row_in[1 - par], 16)

            pairs(sp, B, 4, step)

        @block.gpsimd
        def _(pool):
            pool.sem_inc(x_f, CREDIT)
            norm.credit_pool(pool)
            pool.memset(ones[:], 1.0).then_inc(const, 1)
            for n, (buf, end, value) in enumerate([(b, e, x) for e, x, bufs in
                                                   ((P, 0.0, q_st + k_st), (3 * HD + 1, 1.0, k_st)) for b in bufs]):
                pool.wait_ge(const, n + 1)
                pool.memset(buf[3 * HD:end].bitcast(F32), value).then_inc(const, 1)
            pool.wait_ge(const, 7)

            def step(s, par, alive, nth):
                if alive[0]:
                    pool.wait_ge(x_ps, after(s - 2, 1))
                    if alive[3]:
                        pool.wait_ge(norm.s_rstd, after(s - 4, 1))
                    pool.tensor_copy(flat(Xf[par][:]), batch_flat(m.X, s)).then_inc(x_f, 1)
                if alive[3]:
                    pool.wait_ge(x_f, after(s if alive[0] else B - 1, 1))
                    norm.root(pool, s - 3 + CREDIT, 1 - par)

            pairs(pool, B, 4, step)

        @block.scalar
        def _(act):
            for s in (x_c, q_hi, k_hi, v_c, n_row):
                act.sem_inc(s, CREDIT)
            act.sem_inc(t_exp, CREDIT * JP * H)

            def step(s, par, alive, nth):
                if alive[0]:
                    act.wait_ge(x_ps, after(s, 1))
                    act.wait_ge(v_ps, after(s - 2, 1))
                    act.copy(xT[par][:], even[:]).then_inc(x_c, 1)
                    act.wait_ge(stacked[par], nth * STACKED)
                    act.wait_ge(q_ps, after(s, 1))
                    act.copy(qkT[par][:, Q_HI], odd[:]).then_inc(q_hi, 1)
                    act.wait_ge(k_ps, after(s, 1))
                    act.copy(qkT[par][:, K_HI], even[:]).then_inc(k_hi, 1)
                if alive[1]:
                    act.wait_ge(v_ps, after(s - 1, 1))
                    act.wait_ge(av, after(s - 3, JP))
                    act.copy(flat(v[1 - par][:]), odd[:]).then_inc(v_c, 1)
                if alive[2]:
                    b = s - 2
                    for k in range(JP * H):
                        jp, h = divmod(k, H)
                        act.wait_ge(t_ps, after(b, JP * H, k + 1))
                        act.wait_ge(av, after(b - 1, JP, jp + 1))
                        act.activation(flat(prob[jp][h][:]), wide[k % 2][:], ACT.Exp, scale=SCALE).then_inc(t_exp, 1)
                if alive[1]:
                    act.wait_ge(n_ps, after(s - 1, 1))
                    act.wait_ge(row_in[1 - par], before(par, nth) * 16)
                    act.copy(neg_row[1 - par][:], odd[0:TILES, 0:P]).then_inc(n_row, 1)

            pairs(act, B, 4, step)

        @block.vector
        def _(dve):
            for s in (x_hi, x_lo, q_lo, k_lo, n_sb, rcp, o_n, o_r):
                dve.sem_inc(s, CREDIT)
            dve.sem_inc(s_mx, CREDIT * TILES)
            norm.credit_dve(dve)
            dve.wait_ge(w_in, 16)
            split(dve, Wr[0][:], Wr[1][:], W[:, 0:2 * D], w_hi, 1, w_lo)

            def row_max(b, par, k):
                dve.wait_ge(s_ps, after(b, TILES, k + 1))
                dve.wait_ge(s_mx, after(b, TILES, k - 1))
                hold(dve, gate)
                dve.tensor_tensor_reduce(out=junk[k % 2][:], in0=score_bank[k % 2][:], in1=m.mask_ij[:, k % NT],
                                         scale=1.0, scalar=3.0 * MASKED, op0=ALU.add, op1=ALU.max,
                                         accum_out=mx[par][:, k:k + 1]).then_inc(s_mx, 1)

            def step(s, par, alive, nth):
                if alive[0]:
                    dve.wait_ge(x_c, after(s, 1))
                    dve.wait_ge(k_ps, after(s - 2, 1))
                    split(dve, xTr[par][0][:], xTr[par][1][:], xT[par][:], x_hi, after(s, 1), x_lo)
                    for ps, high, low, done, mine in ((odd, Q_HI, Q_LO, q_hi, q_lo), (even, K_HI, K_LO, k_hi, k_lo)):
                        dve.wait_ge(done, after(s, 1))
                        dve.tensor_tensor(qkT[par][:, low], ps[:], qkT[par][:, high].bitcast(F32),
                                          ALU.subtract).then_inc(mine, 1)
                if alive[3]:
                    b = s - 3
                    dve.wait_ge(o_ps, after(b, 1))
                    dve.wait_ge(norm.s_x, after(b - 2, 4))
                    dve.tensor_tensor(flat(r[1 - par][:]), even[:], batch_flat(m.X, b), ALU.add).then_inc(o_r, 1)
                    dve.wait_ge(o_r, after(b, 1))
                    norm.statistics(dve, b + CREDIT, 1 - par, r[1 - par])
                if alive[1]:
                    for k in range(TILES // 2):
                        row_max(s - 1, 1 - par, k)
                if alive[3]:
                    norm.apply(dve, b + CREDIT, 1 - par, r[1 - par], lambda k: tile_of(m.X, b, k))
                if alive[1]:
                    for k in range(TILES // 2, TILES):
                        row_max(s - 1, 1 - par, k)
                    dve.wait_ge(s_mx, after(s - 1, TILES))
                    dve.wait_ge(n_ps, after(s - 3, 1))
                    dve.tensor_scalar(neg[1 - par][:], mx[1 - par][:], -1.0, None, ALU.mult).then_inc(n_sb, 1)
                if alive[2]:
                    b = s - 2
                    dve.wait_ge(av, after(b, JP))
                    dve.wait_ge(o_n, after(b - 1, 1))
                    dve.reciprocal(rec[:], psD[:]).then_inc(rcp, 1)
                    dve.wait_ge(rcp, after(b, 1))
                    dve.wait_ge(o_ps, after(b - 2, 1))
                    dve.tensor_tensor(oT[par][:], psO[:], rec[:], ALU.mult).then_inc(o_n, 1)

            pairs(dve, B, 4, step)

        @block.tensor
        def _(pe):
            for s in (x_ps, q_ps, k_ps, v_ps, n_ps, o_ps):
                pe.sem_inc(s, CREDIT)
            pe.sem_inc(s_ps, CREDIT * TILES)
            pe.sem_inc(t_ps, CREDIT * JP * H)
            pe.sem_inc(av, CREDIT * JP)
            pe.wait_ge(const, 7)
            pe.wait_ge(w_lo, 1)

            def scores(b, par, k, alive, of_batch):
                h, q = divmod(k, NT)
                if k == 0:
                    pe.wait_ge(stacked[par], (of_batch + 1) * STACKED)
                    pe.wait_ge(v_c, after(b, 1))
                elif k == 1:
                    if alive[0]:
                        pe.wait_ge(k_lo, after(b + 1, 1))
                    if alive[3]:
                        pe.wait_ge(o_r, after(b - 2, 1))
                else:
                    pe.wait_ge(s_mx, after(b, TILES, k - 1))
                pe.matmul(score_bank[k % 2][:], q_st[par][0:3 * HD, h, q * P:q * P + P], k_st[par][0:3 * HD, h],
                          start=True, stop=True).then_inc(s_ps, 1)

            def scores_t(b, par, k):
                jp, h = divmod(k, H)
                pe.wait_ge(t_exp, after(b, JP * H, k - 1))
                for jj in range(2):
                    j = jp * 2 + jj
                    out = wide[k % 2][:, jj * N:jj * N + N]
                    pe.matmul(out, k_st[par][:, h, j * P:j * P + P], q_st[par][:, h], start=True, stop=False)
                    last = pe.matmul(out, m.identb[:], m.mask_ji[:, j], start=False, stop=True)
                last.then_inc(t_ps, 1)

            def values(b, par, jp):
                pe.wait_ge(t_exp, after(b, JP * H, (jp + 1) * H))
                pe.wait_ge(o_n, after(b - 1, 1))
                for jj in range(2):
                    j = jp * 2 + jj
                    for out, stat in ((psO, None), (psD, ones)):
                        for h in range(H):
                            s = slice(h * HD, (h + 1) * HD)
                            last = pe.matmul(out[s, :], v[par][:, j, s] if stat is None else stat[:],
                                             prob[jp][h][:, jj], start=(j == 0), stop=(j == NT - 1),
                                             skip_group_check=True)
                last.then_inc(av, 1)

            ORDER = (["t", "s"] * 6 + ["v"] + ["t", "s"] * 2 + ["s"] * 4 + ["v"] + ["s"] * 4)

            def step(s, par, alive, nth):
                if alive[0]:
                    pe.wait_ge(x_f, after(s, 1))
                    pe.wait_ge(s_mx, after(s - 2, TILES))
                    pe.wait_ge(k_lo, after(s - 1, 1))
                    for t in range(NT):
                        last = pe.transpose(even[:, t * P:t * P + P], Xf[par][:, t], m.ident[:])
                    last.then_inc(x_ps, 1)
                    pe.wait_ge(x_lo, after(s, 1))
                    pe.wait_ge(n_row, after(s - 2, 1))
                    three_pass(pe, odd[:], [h[:, 0:D] for h in Wr], [h[:] for h in xTr[par]]).then_inc(q_ps, 1)
                    three_pass(pe, even[:], [h[:, D:2 * D] for h in Wr], [h[:] for h in xTr[par]]).then_inc(k_ps, 1)
                if alive[1]:
                    if alive[0]:
                        pe.wait_ge(q_lo, after(s, 1))
                    else:
                        pe.wait_ge(n_row, after(s - 2, 1))
                    for t in range(NT):
                        last = pe.matmul(odd[:, t * P:t * P + P], xT[1 - par][:, t * P:t * P + P], W[:, 2 * D:],
                                         start=True, stop=True)
                    last.then_inc(v_ps, 1)
                if alive[3]:
                    b = s - 3
                    if alive[0]:
                        pe.wait_ge(k_lo, after(s, 1))
                    elif alive[1]:
                        pe.wait_ge(s_mx, after(s - 2, TILES))
                    else:
                        pe.wait_ge(s_mx, after(B - 1, TILES))
                        pe.wait_ge(o_r, after(b - 1, 1))
                    pe.wait_ge(o_n, after(b, 1))
                    for t in range(NT):
                        last = pe.transpose(even[:, t * P:t * P + P], oT[1 - par][:, t * P:t * P + P], m.ident[:])
                    last.then_inc(o_ps, 1)
                if alive[2]:
                    pe.wait_ge(row_in[par], nth * 16)
                count = dict.fromkeys("tsv", 0)
                for what in ORDER:
                    k = count[what]
                    count[what] += 1
                    if what == "t" and alive[2]:
                        scores_t(s - 2, par, k)
                    if what == "s" and alive[1]:
                        scores(s - 1, 1 - par, k, alive, before(par, nth))
                    if what == "v" and alive[2]:
                        values(s - 2, par, k)
                if alive[1]:
                    pe.wait_ge(n_sb, after(s - 1, 1))
                    pe.wait_ge(s_mx, after(s - 1, TILES))
                    pe.transpose(odd[0:TILES, 0:P], neg[1 - par][:], m.ident[:]).then_inc(n_ps, 1)

            pairs(pe, B, 4, step)


def layer3(nc, m, ins, bank):
    SLOPE = 0.2
    with ExitStack() as own:
        def sb(name, shape, dt=F32):
            return own.enter_context(nc.sbuf_tensor(name, shape, dt))

        def sem(name):
            return own.enter_context(nc.semaphore(name))

        WX = sb("WX", [P, D + 2])
        a_sb = sb("a_sb", [P, 2])
        WT = sb("WT", [P, D])
        ones = sb("ones3", [P, P])
        onesb = sb("onesb", [P, P], BF16)
        wB = [sb(f"wB{k}", [P, P]) for k in range(2)]
        Xf = [sb(f"Xc{k}", [P, NT, D]) for k in range(2)]
        xT = [sb(f"xTc{k}", [P, N]) for k in range(2)]
        Wh = [sb(f"Wh{k}", [P, NT, D + 2]) for k in range(2)]
        s12 = [sb(f"s12{k}", [P, NT, 2]) for k in range(2)]
        s2s = [sb(f"s2s{k}", [P, 2, NT]) for k in range(2)]
        junk = [sb(f"junk3{k}", [P, N], BF16) for k in range(2)]
        mx = [sb(f"mx3{k}", [P, NT]) for k in range(2)]
        em = [sb(f"em{k}", [P, 3, NT]) for k in range(2)]
        dg = [sb(f"dg{k}", [P, NT, P], BF16) for k in range(2)]
        rl = [sb(f"rl{k}", [P, NT, N]) for k in range(2)]
        pr = [sb(f"pr{k}", [P, NT, N]) for k in range(2)]
        rec = [sb(f"rec3{k}", [P, NT]) for k in range(2)]
        r = [sb(f"rc{k}", [P, NT, D]) for k in range(2)]
        norm = Norm(nc, own, m, "n3")

        w_in = sem("w_in"); const = sem("const"); wt_ps = sem("WT_in_psum"); wt_c = sem("WT_out")
        wa_ps = sem("Wa_in_psum"); wa_c = sem("Wa_out"); wb_c = sem("Wa_spread")
        x_f = sem("x_copied")
        x_ps = sem("x_turned"); x_c = sem("xT_out")
        wh_ps = sem("Wh_in_psum"); s_c = sem("s_out"); wh_c = sem("Wh_out")
        ss = sem("s2_scaled")
        s2_ps = sem("s2_rows"); s1_ps = sem("s1_rows")
        s_mx = sem("row_max")
        e_m = sem("max_terms")
        d_g = sem("diagonals")
        relu = sem("relu")
        r_ps = sem("mask_and_rows"); e_s = sem("e_summed")
        ex = sem("exp_done"); av = sem("values")
        rcp = sem("reciprocal")
        res = sem("residual")
        gate = sem("gate")
        half = [bank[3], bank[0]]
        out_bank = [bank[6], bank[7]]
        block = own.enter_context(nc.Block())

        @block.sync
        def _(sp):
            sp.dma_start(WX[:, 0:D], ins["L3_gnn_W"]).then_inc(w_in, 16)
            with nc.allow_non_contiguous_dma(reason="256 words once"):
                sp.dma_start(a_sb[:], ins["L3_gnn_a"].rearrange("(k p) a -> p (k a)", p=P)).then_inc(w_in, 16)
            sp.wait_ge(w_in, 32)

        @block.gpsimd
        def _(pool):
            pool.sem_inc(x_f, CREDIT)
            norm.credit_pool(pool)
            for n, ap in enumerate((ones[:], onesb[:], Wh[0][:, :, D:D + 1], Wh[1][:, :, D:D + 1])):
                pool.wait_ge(const, n)
                pool.memset(ap, 1.0).then_inc(const, 1)
            pool.wait_ge(const, 4)

            def step(s, par, alive, nth):
                if alive[0]:
                    pool.wait_ge(x_ps, after(s - 2, 1))
                    pool.wait_ge(norm.s_rstd, s)
                    pool.tensor_copy(flat(Xf[par][:]), batch_flat(m.X, s)).then_inc(x_f, 1)
                if alive[2]:
                    pool.wait_ge(x_f, after(s if alive[0] else B - 1, 1))
                    norm.root(pool, s - 2 + CREDIT, par)

            pairs(pool, B, 3, step)

        @block.scalar
        def _(act):
            for s in (x_c, ex):
                act.sem_inc(s, CREDIT)
            act.sem_inc(wh_c, CREDIT * 2)
            act.sem_inc(relu, CREDIT * NT)

            def step(s, par, alive, nth):
                if alive[0]:
                    act.wait_ge(x_ps, after(s, 1))
                    act.wait_ge(s1_ps, after(s - 2, 1))
                    act.copy(xT[par][:], bank[0][:]).then_inc(x_c, 1)
                    act.wait_ge(s1_ps, after(s, 1))
                    act.wait_ge(ss, after(s, 2))
                    act.wait_ge(e_s, after(s - 2, NT))
                    for j in range(NT):
                        act.activation(rl[par][:, j], bank[1][:], ACT.Relu, scale=1.0 - SLOPE,
                                       bias=s2s[par][:, 0, j:j + 1]).then_inc(relu, 1)
                    act.wait_ge(av, after(s - 2, 1))
                    for k in range(2):
                        act.wait_ge(s_c, after(s, 2, k + 1))
                        act.copy(Wh[par][:, 2 * k:2 * k + 2, 0:D],
                                 half[k][:, 0:2 * (D + 2)].rearrange("p (t d) -> p t d", t=2)[:, :, 0:D]).then_inc(wh_c, 1)
                if alive[1]:
                    b = s - 1
                    act.wait_ge(e_s, after(b, NT))
                    act.activation(flat(pr[1 - par][:]), flat(pr[1 - par][:]), ACT.Exp).then_inc(ex, 1)

            pairs(act, B, 3, step)

        @block.vector
        def _(dve):
            dve.sem_inc(s_c, CREDIT * 2)
            dve.sem_inc(ss, CREDIT * 2)
            dve.sem_inc(s_mx, CREDIT * NT)
            dve.sem_inc(e_m, CREDIT * 3)
            dve.sem_inc(d_g, CREDIT * NT)
            dve.sem_inc(e_s, CREDIT * NT)
            dve.sem_inc(rcp, CREDIT * 2)
            dve.sem_inc(res, CREDIT * NT)
            norm.credit_dve(dve)
            dve.wait_ge(wt_ps, 1)
            dve.tensor_copy(WT[:], bank[0][:, 0:D]).then_inc(wt_c, 1)
            dve.wait_ge(wa_ps, 1)
            dve.tensor_copy(WX[:, D:D + 2], bank[1][:, 0:2]).then_inc(wa_c, 1)
            dve.wait_ge(wa_c, 1)
            dve.wait_ge(const, 1)
            for k in range(2):
                dve.tensor_scalar(wB[k][:], ones[:], WX[:, D + k:D + k + 1], None, ALU.mult).then_inc(wb_c, 1)

            def step(s, par, alive, nth):
                if alive[0]:
                    dve.wait_ge(relu, after(s - 2, NT))
                    dve.wait_ge(e_m, after(s - 2, 3))
                    for k in range(2):
                        dve.wait_ge(wh_ps, after(s, 2, k + 1))
                        dve.tensor_copy(s12[par][:, 2 * k:2 * k + 2],
                                        half[k][:, 0:2 * (D + 2)].rearrange("p (t d) -> p t d", t=2)[:, :, D:]).then_inc(s_c, 1)
                    dve.wait_ge(s_c, after(s, 2))
                    for k, f in enumerate((1.0 - SLOPE, SLOPE)):
                        dve.tensor_scalar(s2s[par][:, k], s12[par][:, :, 1], f, None, ALU.mult).then_inc(ss, 1)
                    dve.wait_ge(s2_ps, after(s, 1))
                    for t in range(NT):
                        dve.wait_ge(s_mx, after(s, NT, t - 1))
                        hold(dve, gate)
                        dve.tensor_tensor_reduce(out=junk[t % 2][:], in0=bank[2][:], in1=m.mask_ij[:, t],
                                                 scale=1.0, scalar=3.0 * MASKED, op0=ALU.add, op1=ALU.max,
                                                 accum_out=mx[par][:, t:t + 1]).then_inc(s_mx, 1)
                if alive[1]:
                    b = s - 1
                    dve.wait_ge(av, after(b - 2, 1))
                    dve.wait_ge(relu, after(b, NT))
                    for j in range(NT):
                        dve.wait_ge(r_ps, after(b, NT, j + 1))
                        dve.scalar_tensor_tensor(out=pr[1 - par][:, j], in0=bank[4 + j % 2][:],
                                                 scalar=s2s[1 - par][:, 1, j:j + 1], in1=rl[1 - par][:, j],
                                                 op0=ALU.add, op1=ALU.add).then_inc(e_s, 1)
                if alive[0]:
                    s1 = s12[par][:, :, 0]
                    dve.wait_ge(s_mx, after(s, NT))
                    dve.tensor_tensor(em[par][:, 0], s1, mx[par][:], ALU.add).then_inc(e_m, 1)
                    dve.wait_ge(e_m, after(s, 3, 1))
                    dve.scalar_tensor_tensor(out=em[par][:, 1], in0=em[par][:, 0], scalar=SLOPE, in1=em[par][:, 0],
                                             op0=ALU.mult, op1=ALU.max).then_inc(e_m, 1)
                    dve.wait_ge(e_m, after(s, 3, 2))
                    dve.wait_ge(d_g, after(s - 2, NT))
                    dve.scalar_tensor_tensor(out=em[par][:, 2], in0=s1, scalar=SLOPE, in1=em[par][:, 1],
                                             op0=ALU.mult, op1=ALU.subtract).then_inc(e_m, 1)
                    dve.wait_ge(e_m, after(s, 3))
                    dve.wait_ge(r_ps, after(s - 2, NT))
                    for t in range(NT):
                        dve.tensor_scalar(dg[par][:, t], m.identb[:], em[par][:, 2, t:t + 1], None,
                                          ALU.mult).then_inc(d_g, 1)
                if alive[2]:
                    b = s - 2
                    dve.wait_ge(av, after(b, 1))
                    dve.wait_ge(res, after(b - 2, NT))
                    for k in range(2):
                        dve.reciprocal(rec[par][:, 2 * k:2 * k + 2],
                                       out_bank[k][:, 0:2 * (D + 2)].rearrange("p (t d) -> p t d", t=2)[:, :, D]).then_inc(rcp, 1)
                    dve.wait_ge(rcp, after(b, 2))
                    dve.wait_ge(norm.s_x, after(b - 2, 4))
                    for t in range(NT):
                        o = (t % 2) * (D + 2)
                        dve.scalar_tensor_tensor(out=r[par][:, t], in0=out_bank[t // 2][:, o:o + D],
                                                 scalar=rec[par][:, t:t + 1], in1=tile_of(m.X, b, t),
                                                 op0=ALU.mult, op1=ALU.add).then_inc(res, 1)
                    dve.wait_ge(res, after(b, NT))
                    norm.statistics(dve, b + CREDIT, par, r[par])
                    norm.apply(dve, b + CREDIT, par, r[par], lambda k: tile_of(m.X, b, k))

            pairs(dve, B, 3, step)

        @block.tensor
        def _(pe):
            for s in (x_ps, s2_ps, s1_ps, av):
                pe.sem_inc(s, CREDIT)
            pe.sem_inc(wh_ps, CREDIT * 2)
            pe.sem_inc(r_ps, CREDIT * NT)
            pe.wait_ge(w_in, 32)
            pe.transpose(bank[0][:, 0:D], WX[:, 0:D], m.ident[:]).then_inc(wt_ps, 1)
            pe.wait_ge(wt_c, 1)
            pe.matmul(bank[1][:, 0:2], WT[:], a_sb[:], start=True, stop=True).then_inc(wa_ps, 1)
            pe.wait_ge(wb_c, 2)
            pe.wait_ge(const, 4)

            def step(s, par, alive, nth):
                if alive[0]:
                    pe.wait_ge(x_f, after(s, 1))
                    pe.wait_ge(wh_c, after(s - 1, 2))
                    for t in range(NT):
                        last = pe.transpose(bank[0][:, t * P:t * P + P], Xf[par][:, t], m.ident[:])
                    last.then_inc(x_ps, 1)
                    pe.wait_ge(x_c, after(s, 1))
                    for t in range(NT):
                        o = (t % 2) * (D + 2)
                        last = pe.matmul(half[t // 2][:, o:o + D + 2], xT[par][:, t * P:t * P + P], WX[:],
                                         start=True, stop=True)
                        if t % 2:
                            last.then_inc(wh_ps, 1)
                    pe.wait_ge(s_mx, after(s - 1, NT))
                    pe.matmul(bank[2][:], wB[1][:], xT[par][:], start=True, stop=True).then_inc(s2_ps, 1)
                    pe.wait_ge(relu, after(s - 1, NT))
                    pe.matmul(bank[1][:], wB[0][:], xT[par][:], start=True, stop=True).then_inc(s1_ps, 1)
                if alive[2]:
                    b = s - 2
                    pe.wait_ge(ex, after(b, 1))
                    pe.wait_ge(res, after(b - 1, NT))
                    for t in range(NT):
                        o = (t % 2) * (D + 2)
                        for j in range(NT):
                            last = pe.matmul(out_bank[t // 2][:, o:o + D + 1], pr[par][:, j, t * P:t * P + P],
                                             Wh[par][:, j, 0:D + 1], start=(j == 0), stop=(j == NT - 1))
                    last.then_inc(av, 1)
                if alive[1]:
                    b = s - 1
                    pe.wait_ge(d_g, after(b, NT))
                    for j in range(NT):
                        pe.wait_ge(e_s, after(b, NT, j - 1))
                        pe.matmul(bank[4 + j % 2][:], m.identb[:], m.mask_ji[:, j], start=True, stop=False)
                        pe.matmul(bank[4 + j % 2][:], onesb[:], flat(dg[1 - par][:]), start=False, stop=True).then_inc(r_ps, 1)

            pairs(pe, B, 3, step)


def store(nc, m, out):
    with ExitStack() as own:
        s = own.enter_context(nc.semaphore("stored"))
        block = own.enter_context(nc.Block())

        @block.sync
        def _(sp):
            for b in range(0, B, 4):
                sp.dma_start(out[b:b + 4].rearrange("b (t p) d -> p (b t) d", p=P),
                             m.X[:, b:b + 4].rearrange("p b t d -> p (b t) d")).then_inc(s, 16)
            sp.wait_ge(s, 16 * (B // 4))


def build(nc, ins, out, stop=9):
    with ExitStack() as ctx:
        wide = [ctx.enter_context(nc.psum_tensor(f"wide{k}", [P, 1024], F32)) for k in range(2)]
        bank = [w[:, k * 512:k * 512 + 512] for w in wide for k in range(2)]
        bank += [ctx.enter_context(nc.psum_tensor(f"bank{k}", [P, 512], F32))[:] for k in range(4, 8)]
        m = Memory()
        setup_constants(nc, ctx, m, ins, bank)
        with ExitStack() as first:
            layer0_setup(nc, first, m, ins, bank)
            layer0(nc, m, bank)
        if stop >= 1:
            layer1(nc, m, ins, bank)
        if stop >= 2:
            layer2(nc, m, ins, bank, wide)
        if stop >= 3:
            layer3(nc, m, ins, bank)
        store(nc, m, out)


_INS = ["x", "adj", "L0_gnn_alpha_train", "L0_gnn_w", "L0_gnn_d", "L0_gnn_fc_in_w", "L0_gnn_fc_in_b",
        "L1_gnn_W1", "L1_gnn_b1", "L1_gnn_g1", "L1_gnn_be1", "L1_gnn_W2", "L1_gnn_b2", "L1_gnn_g2", "L1_gnn_be2",
        "L2_gnn_W", "L3_gnn_W", "L3_gnn_a"]


def kernel(**inputs):
    import numpy as _np
    import concourse.bacc as _bacc
    from concourse.bass_utils import run_bass_kernel_spmd as _run

    nc = _bacc.Bacc("TRN2", target_bir_lowering=False, num_devices=1)
    arrays, ins = {}, {}
    for name in _INS:
        a = _np.ascontiguousarray(inputs[name])
        arrays[f"in_{name}_dram"] = a
        ins[name] = nc.dram_tensor(f"in_{name}_dram", a.shape, mybir.dt.from_np(a.dtype), kind="ExternalInput").ap()
    out = nc.dram_tensor("out_0_dram", (B, N, D), F32, kind="ExternalOutput").ap()
    build(nc, ins, out)
    r = _run(nc, [arrays], core_ids=[0])
    return r.results[0]["out_0_dram"]
```

```python
from contextlib import ExitStack
from math import comb

import concourse.bass as bass
from concourse import mybir

F32 = mybir.dt.float32
F32R = mybir.dt.float32r
BF16 = mybir.dt.bfloat16
ALU = mybir.AluOpType
ACT = mybir.ActivationFunctionType
AX = mybir.AxisListType

P = 128
B, N, D = 16, 512, 128
NT = N // P
STEPS = 8
DT = 1.0 / STEPS
BABY = 3
H, HD = 4, D // 4
CH = 256 // P
EPS = 1e-5
MASKED = -1.0e30
CREDIT = 2


def after(b, per, k=None):
    return (b + CREDIT) * per + (per if k is None else k)


def hold(eng, gate):
    eng.sem_inc(gate, 1)


def flat(ap):
    return ap.rearrange("p a b -> p (a b)")


def three_pass(pe, out, stat, mov, start=True, stop=True):
    pe.matmul(out, stat[0], mov[0], start=start, stop=False)
    pe.matmul(out, stat[0], mov[1], start=False, stop=False)
    return pe.matmul(out, stat[1], mov[0], start=False, stop=stop)


class Memory:
    pass


def setup_constants(nc, ctx, m, ins, bank):
    def sb(name, shape, dt=F32):
        return ctx.enter_context(nc.sbuf_tensor(name, shape, dt))

    m.X = sb("X", [P, B, NT, D])
    m.ident = sb("ident", [P, P])
    m.identb = sb("identb", [P, P], BF16)
    m.neg_half = sb("neg_half", [P, 16])
    m.mask_ij = sb("mask_ij", [P, NT, N], BF16)
    m.mask_ji = sb("mask_ji", [P, NT, N], BF16)
    m.AhT = [sb("AhT_hi", [P, NT, N], F32R), sb("AhT_lo", [P, NT, N], F32R)]


def layer0_setup(nc, ctx, m, ins, bank):
    def keep(name, shape, dt=F32):
        return ctx.enter_context(nc.sbuf_tensor(name, shape, dt))

    m.LT = [keep("LT_hi", [P, NT, N], F32R), keep("LT_lo", [P, NT, N], F32R)]
    m.L2T = [keep("L2T_hi", [P, NT, N], F32R), keep("L2T_lo", [P, NT, N], F32R)]
    m.L3T = [keep("L3T_hi", [P, NT, N], F32R), keep("L3T_lo", [P, NT, N], F32R)]
    m.Pj = [keep("Pj_hi", [P, 9, D], F32R), keep("Pj_lo", [P, 9, D], F32R)]
    m.bias = keep("bias_field", [P, NT, BABY, D])

    with ExitStack() as own:
        def sb(name, shape, dt=F32):
            return own.enter_context(nc.sbuf_tensor(name, shape, dt))

        sems = []

        def sem(name):
            sems.append(nc.alloc_semaphore(name))
            return sems[-1]

        A = sb("A", [P, NT, N])
        A1 = sb("A1", [P, NT, N])
        L = sb("L", [P, NT, N])
        LTf = sb("LTf", [P, NT, N])
        Lr = [sb("L_hi", [P, NT, N], F32R), sb("L_lo", [P, NT, N], F32R)]
        w_sb = sb("w_sb", [P, D])
        fc = sb("fc", [P, D])
        d_col = sb("d_col", [P, 1])
        b_col = sb("b_col", [P, 1])
        al = sb("al", [P, NT])
        ea = sb("ea", [P, NT])
        col = sb("col", [P, 8, NT])
        ones = sb("ones", [P, P])
        wT = sb("wT", [P, D])
        wTs = sb("wTs", [P, D])
        RP = sb("RP", [P, 9, D])
        Pf = sb("Pf", [P, 9, D])
        cB = sb("cB", [P, 9, D])
        bB = sb("bB", [P, P])
        Y = sb("Y", [P, 2, NT])
        junk = sb("junk", [P, P])
        diag = sb("diag", [P, NT])
        deg = sb("deg", [P, 3, NT])
        dinv = sb("dinv", [P, NT])

        a_in = sem("a_in"); small_in = sem("small_in"); x_in = sem("x_in")
        pool_c = sem("pool_c"); ident_b = sem("ident_b")
        exp_a = sem("exp_a"); v_col = sem("v_col"); v_L = sem("v_L"); v_Lhi = sem("v_Lhi"); v_Llo = sem("v_Llo")
        t_AT = sem("t_AT"); v_mji = sem("v_mji"); v_mij = sem("v_mij")
        t_LT = sem("t_LT"); c_LTf = sem("c_LTf"); c_LTh = sem("c_LTh"); v_LTl = sem("v_LTl")
        t_L2 = sem("t_L2"); c_L2h = sem("c_L2h"); v_L2l = sem("v_L2l")
        t_L3 = sem("t_L3"); c_L3h = sem("c_L3h"); v_L3l = sem("v_L3l")
        t_Ah = sem("t_Ah"); c_Ahh = sem("c_Ahh"); v_Ahl = sem("v_Ahl")
        v_A1 = sem("v_A1"); t_cs = sem("t_cs"); v_deg = sem("v_deg"); p_dinv = sem("p_dinv"); v_As = sem("v_As")
        t_wT = sem("t_wT"); v_dc = sem("v_dc"); v_wT = sem("v_wT"); t_R = sem("t_R"); v_R = sem("v_R")
        t_Q = sem("t_Q"); v_P = sem("v_P"); t_cB = sem("t_cB"); v_cB = sem("v_cB")
        v_Y1 = sem("v_Y1"); t_Y2 = sem("t_Y2"); v_Y2 = sem("v_Y2"); v_bias = sem("v_bias"); v_bB = sem("v_bB")

        c_c, c_d, c_rs = (col[:, k, :] for k in range(3))
        block = own.enter_context(nc.Block())

        @block.sync
        def _(sp):
            sp.dma_start(A[:], ins["adj"].rearrange("(t p) m -> p t m", p=P)).then_inc(a_in, 16)
            sp.dma_start(w_sb[:], ins["L0_gnn_w"]).then_inc(small_in, 16)
            sp.dma_start(fc[:], ins["L0_gnn_fc_in_w"]).then_inc(small_in, 16)
            sp.dma_start(d_col[:], ins["L0_gnn_d"].rearrange("(p a) -> p a", a=1)).then_inc(small_in, 16)
            sp.dma_start(b_col[:], ins["L0_gnn_fc_in_b"].rearrange("(p a) -> p a", a=1)).then_inc(small_in, 16)
            with nc.allow_non_contiguous_dma(reason="512 words once"):
                sp.dma_start(al[:], ins["L0_gnn_alpha_train"].rearrange("(t p) -> p t", p=P)).then_inc(small_in, 16)
            for b in range(0, B, 4):
                sp.dma_start(m.X[:, b:b + 4].rearrange("p b t d -> p (b t) d"),
                             ins["x"][b:b + 4].rearrange("b (t p) d -> p (b t) d", p=P)).then_inc(x_in, 16)
            sp.wait_ge(x_in, 16 * (B // 4))

        @block.gpsimd
        def _(pool):
            pool.memset(m.ident[:], 0.0).then_inc(pool_c, 1)
            pool.memset(ones[:], 1.0).then_inc(pool_c, 1)
            pool.memset(m.neg_half[:], -0.5).then_inc(pool_c, 1)
            pool.wait_ge(pool_c, 3)
            pool.affine_select(out=m.ident[:], in_=m.ident[:], compare_op=ALU.not_equal, fill=1.0, base=0,
                               pattern=[[-1, P]], channel_multiplier=1).then_inc(pool_c, 1)
            pool.wait_ge(v_deg, 4)
            pool.tensor_tensor(dinv[:], deg[:, 2], m.neg_half[:, 0:NT], ALU.pow).then_inc(p_dinv, 1)

        @block.scalar
        def _(act):
            act.wait_ge(small_in, 80)
            act.activation(ea[:], al[:], ACT.Exp, scale=-1.0).then_inc(exp_a, 1)
            for q in range(NT):
                act.wait_ge(t_LT, q + 1)
                act.copy(LTf[:, q], bank[q][:]).then_inc(c_LTf, 1)
            for q in range(NT):
                act.wait_ge(c_LTf, q + 1)
                act.copy(m.LT[0][:, q], LTf[:, q]).then_inc(c_LTh, 1)
            act.wait_ge(p_dinv, 1)
            for q in range(NT):
                act.wait_ge(t_Ah, q + 1)
                act.activation(m.AhT[0][:, q], bank[q][:], ACT.Copy, scale=dinv[:, q:q + 1]).then_inc(c_Ahh, 1)
            for q in range(NT):
                act.wait_ge(t_L2, q + 1)
                act.copy(m.L2T[0][:, q], bank[q][:]).then_inc(c_L2h, 1)
            for q in range(NT):
                act.wait_ge(t_L3, q + 1)
                act.copy(m.L3T[0][:, q], bank[q][:]).then_inc(c_L3h, 1)

        @block.vector
        def _(dve):
            dve.wait_ge(pool_c, 4)
            dve.tensor_copy(m.identb[:], m.ident[:]).then_inc(ident_b, 1)
            dve.wait_ge(small_in, 80)
            dve.tensor_scalar(d_col[:], d_col[:], 0.0, 1.0, ALU.max, ALU.min).then_inc(v_dc, 1)
            dve.tensor_scalar(bB[:], ones[:], b_col[:], None, ALU.mult).then_inc(v_bB, 1)
            dve.wait_ge(exp_a, 1)
            dve.tensor_scalar(col[:, 3, :], ea[:], 1.0, None, ALU.add).then_inc(v_col, 1)
            dve.wait_ge(v_col, 1)
            dve.reciprocal(col[:, 4, :], col[:, 3, :]).then_inc(v_col, 1)
            dve.wait_ge(v_col, 2)
            dve.tensor_scalar(c_c, col[:, 4, :], DT / 2, None, ALU.mult).then_inc(v_col, 1)
            dve.wait_ge(v_col, 3)
            dve.tensor_scalar(c_d, c_c, -1.0, 1.0 - DT, ALU.mult, ALU.add).then_inc(v_col, 1)
            dve.wait_ge(v_col, 4)
            dve.wait_ge(a_in, 16)
            for t in range(NT):
                dve.tensor_scalar(L[:, t], A[:, t], c_c[:, t:t + 1], None, ALU.mult).then_inc(v_L, 1)
            dve.wait_ge(v_L, NT)
            for t in range(NT):
                s = slice(t * P, t * P + P)
                dve.scalar_tensor_tensor(out=L[:, t, s], in0=m.ident[:], scalar=c_d[:, t:t + 1], in1=L[:, t, s],
                                         op0=ALU.mult, op1=ALU.add).then_inc(v_L, 1)
            dve.wait_ge(t_wT, 1)
            dve.tensor_copy(wT[:], bank[4][:, 0:D]).then_inc(v_wT, 1)
            dve.wait_ge(v_dc, 1)
            dve.wait_ge(v_wT, 1)
            dve.tensor_scalar(wTs[:], wT[:], d_col[:], DT, ALU.mult, ALU.mult).then_inc(v_wT, 1)
            dve.wait_ge(v_L, 2 * NT)
            dve.tensor_copy(flat(Lr[0][:]), flat(L[:])).then_inc(v_Lhi, 1)
            dve.wait_ge(v_Lhi, 1)
            dve.tensor_tensor(flat(Lr[1][:]), flat(L[:]), flat(Lr[0][:].bitcast(F32)), ALU.subtract).then_inc(v_Llo, 1)
            dve.tensor_scalar(flat(m.mask_ij[:]), flat(A[:]), 0.0, MASKED, ALU.is_equal, ALU.mult).then_inc(v_mij, 1)
            for q in range(NT):
                dve.wait_ge(t_AT, q + 1)
                dve.tensor_scalar(m.mask_ji[:, q], bank[q][:], 0.0, MASKED, ALU.is_equal, ALU.mult).then_inc(v_mji, 1)
            dve.tensor_copy(flat(A1[:]), flat(A[:])).then_inc(v_A1, 1)
            dve.wait_ge(v_A1, 1)
            for t in range(NT):
                s = slice(t * P, t * P + P)
                dve.tensor_tensor(A1[:, t, s], A[:, t, s], m.ident[:], ALU.add).then_inc(v_A1, 1)
            dve.wait_ge(v_A1, 1 + NT)
            for t in range(NT):
                s = slice(t * P, t * P + P)
                dve.tensor_tensor_reduce(out=junk[:], in0=A1[:, t, s], in1=m.ident[:], scale=1.0, scalar=0.0,
                                         op0=ALU.mult, op1=ALU.add, accum_out=diag[:, t:t + 1]).then_inc(v_A1, 1)
                dve.wait_ge(v_A1, 2 + NT + t)
            dve.tensor_reduce(deg[:, 0], A1[:], AX.X, ALU.add).then_inc(v_deg, 1)
            dve.wait_ge(v_deg, 1)
            dve.tensor_tensor(deg[:, 1], deg[:, 0], diag[:], ALU.subtract).then_inc(v_deg, 1)
            dve.tensor_copy(RP[:, 0], m.ident[:]).then_inc(v_R, 1)
            for k, (a, n) in enumerate(((1, 1), (2, 1), (3, 2), (5, 4))):
                dve.wait_ge(t_R, k + 1)
                dve.tensor_copy(flat(RP[:, a:a + n]), bank[5 + k % 2][:, 0:n * D]).then_inc(v_R, 1)
            dve.wait_ge(v_deg, 2)
            dve.wait_ge(t_cs, 1)
            dve.tensor_tensor(deg[:, 2], deg[:, 1], bank[7][:, 0:NT], ALU.add).then_inc(v_deg, 2)
            for q in range(NT):
                dve.wait_ge(c_LTh, q + 1)
                dve.tensor_tensor(m.LT[1][:, q], LTf[:, q], m.LT[0][:, q].bitcast(F32), ALU.subtract).then_inc(v_LTl, 1)
            dve.tensor_reduce(Y[:, 0], L[:], AX.X, ALU.add).then_inc(v_Y1, 1)
            dve.wait_ge(p_dinv, 1)
            for t in range(NT):
                dve.tensor_scalar(A1[:, t], A1[:, t], dinv[:, t:t + 1], None, ALU.mult).then_inc(v_As, 1)
            for q in range(NT):
                dve.wait_ge(c_Ahh, q + 1)
                dve.scalar_tensor_tensor(out=m.AhT[1][:, q], in0=bank[q][:], scalar=dinv[:, q:q + 1],
                                         in1=m.AhT[0][:, q].bitcast(F32), op0=ALU.mult,
                                         op1=ALU.subtract).then_inc(v_Ahl, 1)
            for q in range(NT):
                dve.wait_ge(c_L2h, q + 1)
                dve.tensor_tensor(m.L2T[1][:, q], bank[q][:], m.L2T[0][:, q].bitcast(F32), ALU.subtract).then_inc(v_L2l, 1)
            dve.wait_ge(t_Q, 3)

            def in_bank(first, k):
                return bank[first + 2][:, 0:D] if k == 0 else bank[first + (k - 1) // 4][:, (k - 1) % 4 * D:(k - 1) % 4 * D + D]

            for j in range(9):
                dve.tensor_scalar(Pf[:, j], in_bank(4, 8 - j), float(comb(8, j)), None, ALU.mult).then_inc(v_P, 1)
            nP = 9
            for k in range(8):
                dve.wait_ge(v_P, nP)
                for j in range(8 - k):
                    dve.scalar_tensor_tensor(out=Pf[:, j], in0=RP[:, k], scalar=DT * comb(j + k, j), in1=Pf[:, j],
                                             op0=ALU.mult, op1=ALU.add).then_inc(v_P, 1)
                    nP += 1
            dve.wait_ge(v_P, nP)
            dve.tensor_tensor(Pf[:, 0], Pf[:, 0], m.ident[:], ALU.add).then_inc(v_P, 1)
            dve.wait_ge(v_P, nP + 1)
            dve.tensor_copy(flat(m.Pj[0][:]), flat(Pf[:])).then_inc(v_P, 1)
            dve.wait_ge(v_P, nP + 2)
            dve.tensor_tensor(flat(m.Pj[1][:]), flat(Pf[:]), flat(m.Pj[0][:].bitcast(F32)), ALU.subtract).then_inc(v_P, 1)
            dve.wait_ge(t_cB, 3)
            for j in range(9):
                dve.tensor_scalar(cB[:, j], in_bank(4, 8 - j), float(comb(8, j)), None, ALU.mult).then_inc(v_cB, 1)
            dve.wait_ge(t_Y2, 1)
            dve.tensor_copy(Y[:, 1], bank[7][:, 8:8 + NT]).then_inc(v_Y2, 1)
            dve.wait_ge(v_Y2, 1)
            dve.wait_ge(v_cB, 9)
            c_view = cB[:].rearrange("p (g i) d -> p g i d", i=BABY)
            for i in (1, 2):
                for t in range(NT):
                    dve.scalar_tensor_tensor(out=m.bias[:, t], in0=c_view[:, :, i], scalar=Y[:, i - 1, t:t + 1],
                                             in1=c_view[:, :, 0] if i == 1 else m.bias[:, t],
                                             op0=ALU.mult, op1=ALU.add).then_inc(v_bias, 1)
                dve.wait_ge(v_bias, NT * i)
            for q in range(NT):
                dve.wait_ge(c_L3h, q + 1)
                dve.tensor_tensor(m.L3T[1][:, q], bank[q][:], m.L3T[0][:, q].bitcast(F32), ALU.subtract).then_inc(v_L3l, 1)

        @block.tensor
        def _(pe):
            def transposes(src, done):
                for q in range(NT):
                    for t in range(NT):
                        last = pe.transpose(bank[q][:, t * P:t * P + P], src[:, t, q * P:q * P + P], m.ident[:])
                    last.then_inc(done, 1)

            pe.wait_ge(pool_c, 4)
            pe.wait_ge(a_in, 16)
            transposes(A, t_AT)
            pe.wait_ge(small_in, 80)
            pe.transpose(bank[4][:, 0:D], w_sb[:], m.ident[:]).then_inc(t_wT, 1)
            pe.wait_ge(v_mji, NT)
            pe.wait_ge(v_L, 2 * NT)
            transposes(L, t_LT)
            pe.wait_ge(v_wT, 2)
            pe.matmul(bank[5][:, 0:D], wTs[:], wT[:], start=True, stop=True).then_inc(t_R, 1)
            pe.wait_ge(v_R, 2)
            pe.matmul(bank[6][:, 0:D], RP[:, 1], RP[:, 1], start=True, stop=True).then_inc(t_R, 1)
            pe.wait_ge(v_A1, 1 + NT)
            for q in range(NT):
                for t in range(NT):
                    last = pe.matmul(bank[7][:, q:q + 1], A1[:, t, q * P:q * P + P], ones[:, 0:1],
                                     start=(t == 0), stop=(t == NT - 1))
            last.then_inc(t_cs, 1)
            pe.wait_ge(v_R, 3)
            pe.matmul(bank[5][:, 0:2 * D], RP[:, 2], flat(RP[:, 1:3]), start=True, stop=True).then_inc(t_R, 1)
            pe.wait_ge(v_R, 4)
            pe.matmul(bank[6][:, 0:4 * D], RP[:, 4], flat(RP[:, 1:5]), start=True, stop=True).then_inc(t_R, 1)
            pe.wait_ge(c_LTf, NT)
            pe.wait_ge(v_As, NT)
            transposes(A1, t_Ah)
            pe.wait_ge(v_Y1, 1)
            for t in range(NT):
                for q in range(NT):
                    last = pe.matmul(bank[7][:, 8 + t:9 + t], LTf[:, q, t * P:t * P + P], Y[:, 0, q:q + 1],
                                     start=(q == 0), stop=(q == NT - 1))
            last.then_inc(t_Y2, 1)

            def against_powers(stationary, done):
                for k, r in enumerate((RP[:, 1:5], RP[:, 5:9], RP[:, 0:1])):
                    pe.matmul(bank[4 + k][:, 0:r.shape[1] * D], stationary, flat(r), start=True, stop=True).then_inc(done, 1)

            pe.wait_ge(v_R, 5)
            against_powers(fc[:], t_Q)
            pe.wait_ge(v_Llo, 1)
            for power, (mov, done, ready, freed) in enumerate(((m.LT, t_L2, v_LTl, v_Ahl), (m.L2T, t_L3, v_L2l, v_L2l))):
                pe.wait_ge(ready, NT)
                for q in range(NT):
                    pe.wait_ge(freed, q + 1)
                    for k in range(NT):
                        s = slice(q * P, q * P + P)
                        last = three_pass(pe, bank[q][:], (Lr[0][:, k, s], Lr[1][:, k, s]),
                                          (mov[0][:, k], mov[1][:, k]), start=(k == 0), stop=(k == NT - 1))
                    last.then_inc(done, 1)
                if power == 0:
                    pe.wait_ge(v_P, 9)
                    pe.wait_ge(v_bB, 1)
                    against_powers(bB[:], t_cB)

    nc.clear_and_free_semaphores(sems)
    nc.all_engine_barrier()


def pairs(eng, steps, depth, step):
    def alive(s):
        return [0 <= s - k < steps for k in range(depth)]

    lead = (depth - 1) + (depth - 1) % 2
    for s in range(lead):
        step(s, s % 2, alive(s), s // 2)
    with eng.Fori(lead // 2, steps // 2) as r:
        for parity in range(2):
            step(r * 2 + parity, parity, [True] * depth, r)
    for s in range(steps, steps + depth - 1):
        step(s, s % 2, alive(s), s // 2)


def tile_of(X, b, t):
    return X[:, bass.ds(b, 1), t].rearrange("p a d -> p (a d)")


def batch_of(X, b):
    return X[:, bass.ds(b, 1)].rearrange("p a t d -> p (a t) d")


def batch_flat(X, b):
    return X[:, bass.ds(b, 1)].rearrange("p a t d -> p (a t d)")


class Norm:

    def __init__(self, nc, ctx, m, name):
        self.m = m
        self.stats = [ctx.enter_context(nc.sbuf_tensor(f"{name}_stats{k}", [P, 4, 6], F32)) for k in range(2)]
        self.aggr = [ctx.enter_context(nc.sbuf_tensor(f"{name}_aggr{k}", [P, 4, 2], F32)) for k in range(2)]
        self.rstd = [ctx.enter_context(nc.sbuf_tensor(f"{name}_rstd{k}", [P, 4], F32)) for k in range(2)]
        self.gate = ctx.enter_context(nc.semaphore(f"{name}_gate"))
        self.s_stats, self.s_aggr, self.s_eps, self.s_rstd, self.s_x = (
            ctx.enter_context(nc.semaphore(f"{name}_{x}")) for x in ("stats", "aggr", "eps", "rstd", "x"))

    def credit_dve(self, dve, per=1):
        dve.sem_inc(self.s_stats, 4 * CREDIT * per)
        dve.sem_inc(self.s_aggr, 4 * CREDIT * per)

    def credit_apply(self, eng, per=1):
        eng.sem_inc(self.s_x, 4 * CREDIT * per)

    def credit_pool(self, pool, per=1):
        pool.sem_inc(self.s_eps, CREDIT * per)
        pool.sem_inc(self.s_rstd, CREDIT * per)

    def statistics(self, dve, i, parity, r):
        dve.wait_ge(self.s_eps, i - 1)
        for k in range(4):
            dve.bn_stats(self.stats[parity][:, k], r[:, k]).then_inc(self.s_stats, 1)
        dve.wait_ge(self.s_stats, i * 4 + 4)
        hold(dve, self.gate)
        for k in range(4):
            dve.bn_aggr(self.aggr[parity][:, k], self.stats[parity][:, k]).then_inc(self.s_aggr, 1)

    def root(self, pool, i, parity):
        rstd = self.rstd[parity]
        pool.wait_ge(self.s_aggr, i * 4 + 4)
        pool.wait_ge(self.s_x, (i - 1) * 4)
        hold(pool, self.gate)
        pool.tensor_scalar(rstd[:], self.aggr[parity][:, :, 1], EPS, 1.0, ALU.add, ALU.mult).then_inc(self.s_eps, 1)
        pool.wait_ge(self.s_eps, i + 1)
        pool.tensor_tensor(rstd[:], rstd[:], self.m.neg_half[:, 0:4], ALU.pow).then_inc(self.s_rstd, 1)

    def apply(self, eng, i, parity, r, out):
        eng.wait_ge(self.s_rstd, i + 1)
        hold(eng, self.gate)
        for k in range(4):
            eng.tensor_scalar(out(k), r[:, k], self.aggr[parity][:, k, 0:1], self.rstd[parity][:, k:k + 1],
                              ALU.subtract, ALU.mult).then_inc(self.s_x, 1)


def layer0(nc, m, bank):
    GB = 2
    groups = B // GB
    with ExitStack() as own:
        def sb(name, shape, dt=F32):
            return own.enter_context(nc.sbuf_tensor(name, shape, dt))

        def sem(name):
            return own.enter_context(nc.semaphore(name))

        Xf = [sb(f"Xf{k}", [P, NT, D]) for k in range(GB)]
        Xr = [[sb(f"Xr{k}{h}", [P, NT, D], F32R) for h in range(2)] for k in range(GB)]
        yT = [[[sb(f"yT{k}{i}{h}", [P, N], F32R) for h in range(2)] for i in range(BABY)] for k in range(GB)]
        G = [sb(f"G{k}", [P, BABY, NT, GB * D]) for k in range(2)]
        z = [sb(f"z{h}", [P, NT, GB * D], F32R) for h in range(2)]
        zf = sb("zf", [P, NT, GB * D])
        norm = Norm(nc, own, m, "n0")

        gate = sem("gate")
        x_st = [sem(f"x_staged{k}") for k in range(GB)]
        x_hi = sem("x_high")
        x_lo = sem("x_low")
        y_ps = sem("y_in_psum")
        y_hi = sem("y_high")
        y_lo = sem("y_low")
        g_ps = sem("g_in_psum")
        g_sb = sem("g_out")
        z_hi = sem("z_high")
        z_lo = sem("z_low")
        h_ps = sem("h_in_psum")
        h_sb = sem("h_out")
        psum_y, psum_g, psum_h = bank[0:3], bank[3:5], bank[5:7]
        P_of = [p[:].rearrange("p (g i) d -> p g i d", i=BABY) for p in m.Pj]
        block = own.enter_context(nc.Block())

        STAGE = dict(h=0, y=0, g=0, z=1, p=1, n=1, a=1, N=2, A=2)
        ORDER = []
        for what in ("h h y z z N y z z y A p p g p g g p g y z z y z z y p p g g n p p g g a").split():
            ORDER.append((what, sum(w == what for w, _ in ORDER)))

        def four(u):
            return zf[:, 2 * u:2 * u + 2].rearrange("p t (b d) -> p (t b) d", b=GB)

        @block.sync
        def _(sp):
            with sp.Fori(0, groups) as g:
                for bb in range(GB):
                    b = g * GB + bb
                    sp.wait_ge(x_lo, after(b - 2, 1))
                    sp.wait_ge(y_ps, after(b - 2, BABY, 1))
                    hold(sp, gate)
                    sp.dma_start(Xf[bb][:], batch_of(m.X, b)).then_inc(x_st[bb], 16)

        @block.scalar
        def _(act):
            act.sem_inc(x_hi, CREDIT)
            act.sem_inc(y_hi, CREDIT * BABY)
            act.sem_inc(z_hi, CREDIT * 2 * NT)

            def step(s, par, alive, nth):
                for what, k in ORDER:
                    if not alive[STAGE[what]]:
                        continue
                    if what == "h":
                        act.wait_ge(x_st[k], s * 16 + 16)
                        act.wait_ge(y_ps, after(s * GB + k - 2, BABY))
                        act.copy(flat(Xr[k][0][:]), flat(Xf[k][:])).then_inc(x_hi, 1)
                    elif what == "y":
                        bb, i = divmod(k, BABY)
                        act.wait_ge(y_ps, after(s * GB + bb, BABY, i + 1))
                        act.wait_ge(g_ps, after(s * GB + bb - 2, NT))
                        act.copy(yT[bb][i][0][:], psum_y[i][:]).then_inc(y_hi, 1)
                    elif what == "z":
                        t = k % NT
                        if k < NT:
                            act.wait_ge(g_sb, after(s * GB - 1, NT, t + 1))
                            act.wait_ge(h_ps, after(s - 2, 2 * NT))
                            act.copy(z[0][:, t], G[1 - par][:, 2, t]).then_inc(z_hi, 1)
                        else:
                            act.wait_ge(h_ps, after(s - 1, 2 * NT, NT))
                            act.wait_ge(h_sb, after(s - 1, 2 * NT, t + 1))
                            act.copy(z[0][:, t], zf[:, t]).then_inc(z_hi, 1)

            pairs(act, groups, 3, step)

        @block.gpsimd
        def _(pool):
            norm.credit_pool(pool, 2)
            pool.sem_inc(x_lo, CREDIT)

            def step(s, par, alive, nth):
                if alive[0]:
                    for k in range(GB):
                        pool.wait_ge(x_hi, after(s * GB + k, 1))
                        pool.tensor_tensor(flat(Xr[k][1][:]), flat(Xf[k][:]), flat(Xr[k][0][:].bitcast(F32)),
                                           ALU.subtract).then_inc(x_lo, 1)
                if alive[2]:
                    for u in range(2):
                        norm.root(pool, (s - 2 + CREDIT) * 2 + u, u)

            pairs(pool, groups, 3, step)

        @block.vector
        def _(dve):
            dve.sem_inc(y_lo, CREDIT * BABY)
            dve.sem_inc(g_sb, CREDIT * NT)
            dve.sem_inc(z_lo, CREDIT * 2 * NT)
            dve.sem_inc(h_sb, CREDIT * 2 * NT)
            norm.credit_dve(dve, 2)
            norm.credit_apply(dve, 2)

            def step(s, par, alive, nth):
                for what, k in ORDER:
                    if not alive[STAGE[what]]:
                        continue
                    if what == "y":
                        bb, i = divmod(k, BABY)
                        dve.wait_ge(y_hi, after(s * GB + bb, BABY, i + 1))
                        dve.tensor_tensor(yT[bb][i][1][:], psum_y[i][:], yT[bb][i][0][:].bitcast(F32),
                                          ALU.subtract).then_inc(y_lo, 1)
                    elif what == "g":
                        bb, t = divmod(k, NT)
                        if k == 0:
                            dve.wait_ge(z_lo, after(s - 2, 2 * NT, NT))
                            dve.wait_ge(h_sb, after(s - 2, 2 * NT))
                        dve.wait_ge(g_ps, after(s * GB + bb, NT, t + 1))
                        dve.tensor_tensor(G[par][:, :, t, bb * D:bb * D + D],
                                          psum_g[t % 2][:, 0:BABY * D].rearrange("p (g d) -> p g d", g=BABY),
                                          m.bias[:, t], ALU.add).then_inc(g_sb, 1)
                    elif what == "z":
                        t = k % NT
                        dve.wait_ge(z_hi, after(s - 1, 2 * NT, k + 1))
                        dve.tensor_tensor(z[1][:, t], G[1 - par][:, 2, t] if k < NT else zf[:, t],
                                          z[0][:, t].bitcast(F32), ALU.subtract).then_inc(z_lo, 1)
                    elif what == "p":
                        t = k % NT
                        dve.wait_ge(h_ps, after(s - 1, 2 * NT, k + 1))
                        if k < NT:
                            dve.wait_ge(norm.s_x, after(s - 2, 8))
                        else:
                            dve.wait_ge(z_lo, after(s - 1, 2 * NT, k + 1))
                        dve.tensor_tensor(zf[:, t], psum_h[k % 2][:, 0:GB * D],
                                          G[1 - par][:, 1 if k < NT else 0, t], ALU.add).then_inc(h_sb, 1)
                    elif what in "nN":
                        u = "nN".index(what)
                        b = s - STAGE[what]
                        dve.wait_ge(h_sb, after(b, 2 * NT, NT + 2 * u + 2))
                        norm.statistics(dve, (b + CREDIT) * 2 + u, u, four(u))
                    elif what in "aA":
                        u = "aA".index(what)
                        b = s - STAGE[what]
                        norm.apply(dve, (b + CREDIT) * 2 + u, u, four(u),
                                   lambda n: tile_of(m.X, b * GB + n % GB, 2 * u + n // GB))

            pairs(dve, groups, 3, step)

        @block.tensor
        def _(pe):
            pe.sem_inc(y_ps, CREDIT * BABY)
            pe.sem_inc(g_ps, CREDIT * NT)
            pe.sem_inc(h_ps, CREDIT * 2 * NT)

            def step(s, par, alive, nth):
                for what, k in ORDER:
                    if not alive[STAGE[what]]:
                        continue
                    if what == "y":
                        bb, i = divmod(k, BABY)
                        b = s * GB + bb
                        pe.wait_ge(y_lo, after(b - 1, BABY, i + 1))
                        if i == 0:
                            pe.wait_ge(x_st[bb], s * 16 + 16)
                            for t in range(NT):
                                last = pe.transpose(psum_y[0][:, t * P:t * P + P], Xf[bb][:, t], m.ident[:])
                        else:
                            pe.wait_ge(x_lo, after(b, 1))
                            mat = (None, m.LT, m.L2T)[i]
                            for q in range(NT):
                                last = three_pass(pe, psum_y[i][:], [h[:, q] for h in Xr[bb]], [h[:, q] for h in mat],
                                                  start=(q == 0), stop=(q == NT - 1))
                        last.then_inc(y_ps, 1)
                    elif what == "g":
                        bb, t = divmod(k, NT)
                        b = s * GB + bb
                        pe.wait_ge(y_lo, after(b, BABY))
                        pe.wait_ge(g_sb, after(b, NT, t - 1))
                        for i in range(BABY):
                            last = three_pass(pe, psum_g[t % 2][:, 0:BABY * D],
                                              [h[:, t * P:t * P + P] for h in yT[bb][i]],
                                              [h[:, :, i] for h in P_of], start=(i == 0), stop=(i == BABY - 1))
                        last.then_inc(g_ps, 1)
                    elif what == "p":
                        t = k % NT
                        pe.wait_ge(z_lo, after(s - 1, 2 * NT, NT if k < NT else 2 * NT))
                        pe.wait_ge(h_sb, after(s - 1, 2 * NT, k - 1))
                        for q in range(NT):
                            last = three_pass(pe, psum_h[k % 2][:, 0:GB * D], [h[:, q, t * P:t * P + P] for h in m.L3T],
                                              [h[:, q] for h in z], start=(q == 0), stop=(q == NT - 1))
                        last.then_inc(h_ps, 1)

            pairs(pe, groups, 3, step)


def split(dve, high, low, src, s_high, n_high, s_low):
    dve.tensor_copy(high, src).then_inc(s_high, 1)
    dve.wait_ge(s_high, n_high)
    return dve.tensor_tensor(low, src, high.bitcast(F32), ALU.subtract).then_inc(s_low, 1)


def layer1(nc, m, ins, bank):
    with ExitStack() as own:
        def sb(name, shape, dt=F32):
            return own.enter_context(nc.sbuf_tensor(name, shape, dt))

        W1T = [sb(f"W1T{h}", [P, CH, P], F32R) for h in range(2)]
        W2T = [sb(f"W2T{h}", [P, CH, P], F32R) for h in range(2)]
        par1 = sb("par1", [P, 3, CH])
        par2 = sb("par2", [P, 3, 1])
        Hb = sb("Hb", [P, CH, B, N])
        O = sb("O", [P, B, N])
        st1 = sb("st1", [P, CH, B, 6])
        st2 = sb("st2", [P, 1, B, 6])
        aff1 = sb("aff1", [P, 2, CH])
        aff2 = sb("aff2", [P, 2, 1])
        layer1_first(nc, m, ins, bank, W1T, W2T, par1, par2, Hb, st1)
        batch_norm_affine(nc, m, "bn1", st1, par1, aff1, CH)
        layer1_second(nc, m, bank, W2T, par2, Hb, aff1, O, st2)
        batch_norm_affine(nc, m, "bn2", st2, par2, aff2, 1)
        layer1_last(nc, m, bank, O, aff2)


def layer1_first(nc, m, ins, bank, W1T, W2T, par1, par2, Hb, st1):
    with ExitStack() as own:
        def sb(name, shape, dt=F32):
            return own.enter_context(nc.sbuf_tensor(name, shape, dt))

        def sem(name):
            return own.enter_context(nc.semaphore(name))

        w1 = sb("w1", [P, CH, D])
        w2 = sb("w2", [P, CH, P])
        wf = sb("wf", [P, 2, CH, P])
        Xr = [[sb(f"Xa{k}{h}", [P, NT, D], F32R) for h in range(2)] for k in range(2)]
        agT = [[sb(f"agT{k}{h}", [P, N], F32R) for h in range(2)] for k in range(2)]
        w_in = sem("w_in")
        w_ps = sem("w_in_psum"); w_sb = sem("w_out"); w_hi = sem("w_high"); w_lo = sem("w_low")
        x_hi = sem("x_high"); x_lo = sem("x_low")
        a_ps = sem("agg_in_psum"); a_hi = sem("agg_high"); a_lo = sem("agg_low")
        h_ps = sem("h_in_psum"); h_sb = sem("h_out"); h_st = sem("h_stats")
        block = own.enter_context(nc.Block())

        @block.sync
        def _(sp):
            sp.dma_start(w1[:], ins["L1_gnn_W1"].rearrange("(c p) d -> p c d", p=P)).then_inc(w_in, 16)
            sp.dma_start(flat(w2[:]), ins["L1_gnn_W2"]).then_inc(w_in, 16)
            with nc.allow_non_contiguous_dma(reason="a few hundred words once"):
                for k, n in enumerate(("b1", "g1", "be1")):
                    sp.dma_start(par1[:, k], ins[f"L1_gnn_{n}"].rearrange("(c p) -> p c", p=P)).then_inc(w_in, 16)
                for k, n in enumerate(("b2", "g2", "be2")):
                    sp.dma_start(par2[:, k], ins[f"L1_gnn_{n}"].rearrange("(p a) -> p a", a=1)).then_inc(w_in, 16)
            sp.wait_ge(w_in, 8 * 16)

        @block.scalar
        def _(act):
            for s in (x_hi, a_hi):
                act.sem_inc(s, CREDIT)
            act.sem_inc(h_sb, CREDIT * CH)
            act.wait_ge(w_in, 8 * 16)

            def step(s, par, alive, nth):
                if alive[0]:
                    act.wait_ge(a_ps, after(s - 2, 1))
                    act.copy(flat(Xr[par][0][:]), batch_flat(m.X, s)).then_inc(x_hi, 1)
                    act.wait_ge(a_ps, after(s, 1))
                    act.wait_ge(h_ps, after(s - 2, CH))
                    act.copy(agT[par][0][:], bank[par][:]).then_inc(a_hi, 1)
                if alive[1]:
                    b = s - 1
                    for c in range(CH):
                        act.wait_ge(h_ps, after(b, CH, c + 1))
                        act.activation(Hb[:, c, bass.ds(b, 1)].rearrange("p a n -> p (a n)"),
                                       bank[2 + 2 * (1 - par) + c][:], ACT.Identity,
                                       bias=par1[:, 0, c:c + 1]).then_inc(h_sb, 1)

            pairs(act, B, 2, step)

        @block.vector
        def _(dve):
            for s in (x_lo, a_lo):
                dve.sem_inc(s, CREDIT)
            dve.sem_inc(h_st, CREDIT * CH)
            dve.wait_ge(w_ps, 2 * CH)
            dve.tensor_copy(wf[:].rearrange("p a c o -> p (a c o)"), bank[7][:, 0:2 * CH * P]).then_inc(w_sb, 1)
            dve.wait_ge(w_sb, 1)
            split(dve, flat(W1T[0][:]), flat(W1T[1][:]), flat(wf[:, 0]), w_hi, 1, w_lo)
            split(dve, flat(W2T[0][:]), flat(W2T[1][:]), flat(wf[:, 1]), w_hi, 2, w_lo)

            def step(s, par, alive, nth):
                if alive[0]:
                    dve.wait_ge(x_hi, after(s, 1))
                    dve.tensor_tensor(flat(Xr[par][1][:]), batch_flat(m.X, s), flat(Xr[par][0][:].bitcast(F32)),
                                      ALU.subtract).then_inc(x_lo, 1)
                    dve.wait_ge(a_hi, after(s, 1))
                    dve.tensor_tensor(agT[par][1][:], bank[par][:], agT[par][0][:].bitcast(F32),
                                      ALU.subtract).then_inc(a_lo, 1)
                if alive[1]:
                    b = s - 1
                    for c in range(CH):
                        dve.wait_ge(h_sb, after(b, CH, c + 1))
                        dve.bn_stats(st1[:, c, bass.ds(b, 1)].rearrange("p a n -> p (a n)"),
                                     Hb[:, c, bass.ds(b, 1)].rearrange("p a n -> p (a n)")).then_inc(h_st, 1)

            pairs(dve, B, 2, step)

        @block.tensor
        def _(pe):
            pe.sem_inc(a_ps, CREDIT)
            pe.sem_inc(h_ps, CREDIT * CH)
            pe.wait_ge(w_in, 8 * 16)
            for k, w in enumerate((w1, w2)):
                for c in range(CH):
                    pe.transpose(bank[7][:, (k * CH + c) * P:(k * CH + c + 1) * P], w[:, c], m.ident[:]).then_inc(w_ps, 1)

            def step(s, par, alive, nth):
                if alive[0]:
                    pe.wait_ge(x_lo, after(s, 1))
                    pe.wait_ge(a_lo, after(s - 2, 1))
                    for k in range(NT):
                        last = three_pass(pe, bank[par][:], [h[:, k] for h in Xr[par]], [h[:, k] for h in m.AhT],
                                          start=(k == 0), stop=(k == NT - 1))
                    last.then_inc(a_ps, 1)
                if alive[1]:
                    b = s - 1
                    pe.wait_ge(a_lo, after(b, 1))
                    pe.wait_ge(w_lo, 2)
                    for c in range(CH):
                        pe.wait_ge(h_sb, after(b - 2, CH, c + 1))
                        three_pass(pe, bank[2 + 2 * (1 - par) + c][:], [h[:, c] for h in W1T],
                                   [h[:] for h in agT[1 - par]]).then_inc(h_ps, 1)

            pairs(pe, B, 2, step)


def batch_norm_affine(nc, m, name, st, par, aff, channels):
    with ExitStack() as own:
        mv = own.enter_context(nc.sbuf_tensor(f"{name}_mv", [P, channels, 2], F32))
        ve = own.enter_context(nc.sbuf_tensor(f"{name}_ve", [P, channels], F32))
        ms = own.enter_context(nc.sbuf_tensor(f"{name}_ms", [P, channels], F32))
        agg = own.enter_context(nc.semaphore(f"{name}_agg"))
        root = own.enter_context(nc.semaphore(f"{name}_root"))
        out = own.enter_context(nc.semaphore(f"{name}_out"))
        block = own.enter_context(nc.Block())

        @block.vector
        def _(dve):
            for c in range(channels):
                dve.bn_aggr(mv[:, c], st[:, c].rearrange("p b s -> p (b s)")).then_inc(agg, 1)
            dve.wait_ge(root, 2)
            dve.tensor_tensor(aff[:, 0], ve[:], par[:, 1], ALU.mult).then_inc(out, 1)
            dve.wait_ge(out, 1)
            dve.tensor_tensor(ms[:], mv[:, :, 0], aff[:, 0], ALU.mult).then_inc(out, 1)
            dve.wait_ge(out, 2)
            dve.tensor_tensor(aff[:, 1], par[:, 2], ms[:], ALU.subtract).then_inc(out, 1)

        @block.gpsimd
        def _(pool):
            pool.wait_ge(agg, channels)
            pool.tensor_scalar(ve[:], mv[:, :, 1], EPS, 1.0, ALU.add, ALU.mult).then_inc(root, 1)
            pool.wait_ge(root, 1)
            pool.tensor_tensor(ve[:], ve[:], m.neg_half[:, 0:channels], ALU.pow).then_inc(root, 1)


def layer1_second(nc, m, bank, W2T, par2, Hb, aff1, O, st2):
    with ExitStack() as own:
        def sb(name, shape, dt=F32):
            return own.enter_context(nc.sbuf_tensor(name, shape, dt))

        def sem(name):
            return own.enter_context(nc.semaphore(name))

        hf = [sb(f"hf{k}", [P, CH, N]) for k in range(2)]
        hr = [[sb(f"hr{k}{h}", [P, CH, N], F32R) for h in range(2)] for k in range(2)]
        relu = sem("relu"); h_hi = sem("h_high"); h_lo = sem("h_low")
        o_ps = sem("o_in_psum"); o_sb = sem("o_out"); o_st = sem("o_stats")
        block = own.enter_context(nc.Block())

        @block.scalar
        def _(act):
            act.sem_inc(relu, CREDIT * CH)
            act.sem_inc(o_sb, CREDIT)

            def step(s, par, alive, nth):
                if alive[0]:
                    for c in range(CH):
                        act.wait_ge(h_lo, after(s - 2, CH, c + 1))
                        act.activation(hf[par][:, c], Hb[:, c, bass.ds(s, 1)].rearrange("p a n -> p (a n)"), ACT.Relu,
                                       scale=aff1[:, 0, c:c + 1], bias=aff1[:, 1, c:c + 1]).then_inc(relu, 1)
                if alive[1]:
                    b = s - 1
                    act.wait_ge(o_ps, after(b, 1))
                    act.activation(O[:, bass.ds(b, 1)].rearrange("p a n -> p (a n)"), bank[1 - par][:], ACT.Identity,
                                   bias=par2[:, 0, 0:1]).then_inc(o_sb, 1)

            pairs(act, B, 2, step)

        @block.vector
        def _(dve):
            dve.sem_inc(h_hi, CREDIT * CH)
            dve.sem_inc(h_lo, CREDIT * CH)
            dve.sem_inc(o_st, CREDIT)

            def step(s, par, alive, nth):
                if alive[0]:
                    dve.wait_ge(o_ps, after(s - 2, 1))
                    for c in range(CH):
                        dve.wait_ge(relu, after(s, CH, c + 1))
                        split(dve, hr[par][0][:, c], hr[par][1][:, c], hf[par][:, c], h_hi, after(s, CH, c + 1), h_lo)
                if alive[1]:
                    b = s - 1
                    dve.wait_ge(o_sb, after(b, 1))
                    dve.bn_stats(st2[:, 0, bass.ds(b, 1)].rearrange("p a n -> p (a n)"),
                                 O[:, bass.ds(b, 1)].rearrange("p a n -> p (a n)")).then_inc(o_st, 1)

            pairs(dve, B, 2, step)

        @block.tensor
        def _(pe):
            pe.sem_inc(o_ps, CREDIT)

            def step(s, par, alive, nth):
                pe.wait_ge(o_sb, after(s - 2, 1))
                for c in range(CH):
                    pe.wait_ge(h_lo, after(s, CH, c + 1))
                    last = three_pass(pe, bank[par][:], [h[:, c] for h in W2T], [h[:, c] for h in hr[par]],
                                      start=(c == 0), stop=(c == CH - 1))
                last.then_inc(o_ps, 1)

            pairs(pe, B, 1, step)


def layer1_last(nc, m, bank, O, aff2):
    with ExitStack() as own:
        def sb(name, shape, dt=F32):
            return own.enter_context(nc.sbuf_tensor(name, shape, dt))

        def sem(name):
            return own.enter_context(nc.semaphore(name))

        on = [sb(f"on{k}", [P, N]) for k in range(2)]
        r = [sb(f"r{k}", [P, NT, D]) for k in range(2)]
        norm = Norm(nc, own, m, "n1")
        bn = sem("normed"); t_ps = sem("turned"); res = sem("residual")
        block = own.enter_context(nc.Block())

        @block.scalar
        def _(act):
            act.sem_inc(bn, CREDIT)

            def step(s, par, alive, nth):
                act.wait_ge(t_ps, after(s - 2, 1))
                act.activation(on[par][:], O[:, bass.ds(s, 1)].rearrange("p a n -> p (a n)"), ACT.Identity,
                               scale=aff2[:, 0, 0:1], bias=aff2[:, 1, 0:1]).then_inc(bn, 1)

            pairs(act, B, 1, step)

        @block.tensor
        def _(pe):
            pe.sem_inc(t_ps, CREDIT)

            def step(s, par, alive, nth):
                pe.wait_ge(bn, after(s, 1))
                pe.wait_ge(res, after(s - 2, 1))
                for t in range(NT):
                    last = pe.transpose(bank[par][:, t * P:t * P + P], on[par][:, t * P:t * P + P], m.ident[:])
                last.then_inc(t_ps, 1)

            pairs(pe, B, 1, step)

        @block.gpsimd
        def _(pool):
            norm.credit_pool(pool)
            pairs(pool, B, 1, lambda s, par, alive, nth: norm.root(pool, s + CREDIT, par))

        @block.vector
        def _(dve):
            dve.sem_inc(res, CREDIT)
            norm.credit_dve(dve)
            norm.credit_apply(dve)

            def step(s, par, alive, nth):
                if alive[0]:
                    dve.wait_ge(t_ps, after(s, 1))
                    dve.wait_ge(norm.s_x, after(s - 2, 4))
                    dve.tensor_tensor(flat(r[par][:]), bank[par][:], batch_flat(m.X, s), ALU.add).then_inc(res, 1)
                    dve.wait_ge(res, after(s, 1))
                    norm.statistics(dve, s + CREDIT, par, r[par])
                if alive[1]:
                    norm.apply(dve, s - 1 + CREDIT, 1 - par, r[1 - par], lambda k: tile_of(m.X, s - 1, k))

            pairs(dve, B, 2, step)


def layer2(nc, m, ins, bank, wide):
    SCALE = float(HD) ** -0.5
    JP = NT // 2
    PAIRS = H * JP
    TILES = H * NT
    with ExitStack() as own:
        def sb(name, shape, dt=F32):
            return own.enter_context(nc.sbuf_tensor(name, shape, dt))

        def sem(name):
            return own.enter_context(nc.semaphore(name))

        W = sb("W", [P, 3 * D])
        Wr = [sb(f"Wr{h}", [P, 2 * D], F32R) for h in range(2)]
        ones = sb("ones_hd", [P, HD])
        Xf = [sb(f"Xb{k}", [P, NT, D]) for k in range(2)]
        xT = [sb(f"xT{k}", [P, N]) for k in range(2)]
        xTr = [[sb(f"xT{k}{h}", [P, N], F32R) for h in range(2)] for k in range(2)]
        qkT = [sb(f"qkT{k}", [P, 4, N], F32R) for k in range(2)]
        Q_LO, Q_HI, K_HI, K_LO = range(4)
        qk_st = [sb(f"qk_st{k}", [P, 2, H, N], F32R) for k in range(2)]
        q_st = [s[:, 0] for s in qk_st]
        k_st = [s[:, 1] for s in qk_st]
        v = [sb(f"v{k}", [P, NT, D]) for k in range(2)]
        junk = [sb(f"junk{k}", [P, N], BF16) for k in range(2)]
        mx = [sb(f"mx{k}", [P, TILES]) for k in range(2)]
        neg = [sb(f"neg{k}", [P, TILES]) for k in range(2)]
        neg_row = [sb(f"neg_row{k}", [TILES, P], F32R) for k in range(2)]
        prob = [[sb(f"prob{k}{h}", [P, 2, N]) for h in range(H)] for k in range(JP)]
        oT = sb("oT", [P, N])
        denT = sb("denT", [P, N])
        rec = sb("rec", [P, NT, H, 1])
        r = [sb(f"rb{k}", [P, NT, D]) for k in range(2)]
        norm = Norm(nc, own, m, "n2")

        w_in = sem("w_in"); w_hi = sem("w_high"); w_lo = sem("w_low"); const = sem("const")
        x_f = sem("x_copied")
        x_ps = sem("x_turned"); x_hi = sem("xT_high"); x_c = sem("xT_out"); x_lo = sem("xT_low")
        q_ps = sem("q_in_psum"); q_hi = sem("q_high"); q_lo = sem("q_low")
        k_ps = sem("k_in_psum"); k_hi = sem("k_high"); k_lo = sem("k_low")
        v_ps = sem("v_in_psum"); v_c = sem("v_out")
        stacked = [[sem(f"stacked{k}{h}") for h in range(H)] for k in range(2)]
        s_ps = sem("scores"); s_mx = sem("row_max")
        n_sb = sem("negated"); n_ps = sem("neg_turned"); n_row = sem("neg_row_out")
        row_in = [sem(f"row_in{k}") for k in range(2)]
        t_ps = sem("scores_t"); t_exp = sem("exp_done")
        av = sem("values")
        o_c = sem("outT_out"); d_c = sem("denominatorT_out")
        o_ps = sem("out_turned"); d_ps = sem("denominator_turned")
        rcp = sem("reciprocal"); o_n = sem("out_divided"); o_r = sem("residual")
        gate = sem("gate")
        psO, psD = bank[4], bank[5]
        STACKED = 3 * 16
        block = own.enter_context(nc.Block())

        STAGE = dict(x=0, q=0, k=0, v=1, s=1, g=2, n=2, t=2, a=3, e=3, o=3, d=3, m=3, r=3, b=3, y=3)
        ORDER = []
        for what in ("g x s a n s q a s k s a s s a s e s t s t s o d m t s r t s b v t s t s t s y t s").split():
            ORDER.append((what, sum(w == what for w, _ in ORDER)))
        RING = [item for item in ORDER if item[0] in "xqkvsno"]
        ring = {item: bank[6 + n % 2] for n, item in enumerate(RING)}

        def released(s, what, k):
            return {"x": (x_c, after(s, 1)), "q": (q_lo, after(s, 1)), "k": (k_lo, after(s, 1)),
                    "v": (v_c, after(s - 1, 1)), "s": (s_mx, after(s - 1, TILES, k + 1)),
                    "n": (n_row, after(s - 2, 1)), "o": (o_n, after(s - 3, 1))}[what]

        def before(par, nth):
            return nth if par else nth - 1

        @block.sync
        def _(sp):
            sp.dma_start(W[:], ins["L2_gnn_W"]).then_inc(w_in, 16)

            def step(s, par, alive, nth):
                if alive[2]:
                    sp.wait_ge(n_row, after(s - 2, 1))
                    hold(sp, gate)
                    sp.dma_start(q_st[par][3 * HD:3 * HD + 1].bitcast(F32).rearrange("a h (t p) -> a (h t) p", p=P),
                                 neg_row[par][:].bitcast(F32)).then_inc(row_in[par], 16)
                if alive[0]:
                    sp.wait_ge(k_lo, after(s, 1))
                    for h in range(H):
                        sp.wait_ge(t_ps, after(s - 2, PAIRS, (h + 1) * JP))
                        if h == 0:
                            hold(sp, gate)
                        for g, (q, k) in enumerate(((Q_HI, K_HI), (Q_HI, K_LO), (Q_LO, K_HI))):
                            sp.dma_start(qk_st[par][g * HD:(g + 1) * HD, :, h].bitcast(F32),
                                         qkT[par][h * HD:(h + 1) * HD, q:k + 1:k - q].bitcast(F32)
                                         ).then_inc(stacked[par][h], 16)

            pairs(sp, B, 4, step)

        @block.gpsimd
        def _(pool):
            pool.sem_inc(x_f, CREDIT)
            norm.credit_pool(pool)
            pool.memset(ones[:], 1.0).then_inc(const, 1)
            for n, (buf, end, value) in enumerate([(b, e, x) for e, x, bufs in
                                                   ((P, 0.0, q_st + k_st), (3 * HD + 1, 1.0, k_st)) for b in bufs]):
                pool.wait_ge(const, n + 1)
                pool.memset(buf[3 * HD:end].bitcast(F32), value).then_inc(const, 1)
            pool.wait_ge(const, 7)

            def step(s, par, alive, nth):
                if alive[0]:
                    pool.wait_ge(x_ps, after(s - 2, 1))
                    if alive[4]:
                        pool.wait_ge(norm.s_rstd, after(s - 5, 1))
                    pool.tensor_copy(flat(Xf[par][:]), batch_flat(m.X, s)).then_inc(x_f, 1)
                if alive[4]:
                    pool.wait_ge(x_f, after(s if alive[0] else B - 1, 1))
                    norm.root(pool, s - 4 + CREDIT, par)

            pairs(pool, B, 5, step)

        @block.scalar
        def _(act):
            for s in (x_hi, x_c, q_hi, k_hi, v_c, n_row, o_c, d_c):
                act.sem_inc(s, CREDIT)
            act.sem_inc(t_exp, CREDIT * PAIRS)

            def step(s, par, alive, nth):
                for what, k in ORDER:
                    if not alive[STAGE[what]]:
                        continue
                    src = ring.get((what, k))
                    b = s - STAGE[what]
                    if what == "x":
                        act.wait_ge(x_ps, after(s, 1))
                        act.wait_ge(k_ps, after(s - 2, 1))
                        act.copy(xTr[par][0][:], src[:]).then_inc(x_hi, 1)
                        act.wait_ge(v_ps, after(s - 2, 1))
                        act.copy(xT[par][:], src[:]).then_inc(x_c, 1)
                    elif what == "q":
                        for h in range(H):
                            act.wait_ge(stacked[par][h], nth * STACKED)
                        act.wait_ge(q_ps, after(s, 1))
                        act.copy(qkT[par][:, Q_HI], src[:]).then_inc(q_hi, 1)
                    elif what == "k":
                        act.wait_ge(k_ps, after(s, 1))
                        act.copy(qkT[par][:, K_HI], src[:]).then_inc(k_hi, 1)
                    elif what == "v":
                        act.wait_ge(v_ps, after(b, 1))
                        act.wait_ge(av, after(b - 2, NT))
                        act.copy(flat(v[1 - par][:]), src[:]).then_inc(v_c, 1)
                    elif what == "t":
                        h, jp = divmod(k, JP)
                        act.wait_ge(t_ps, after(b, PAIRS, k + 1))
                        if k == 0:
                            act.wait_ge(av, after(b - 1, NT))
                        act.activation(flat(prob[jp][h][:]), wide[k % 2][:], ACT.Exp, scale=SCALE).then_inc(t_exp, 1)
                    elif what == "n":
                        act.wait_ge(n_ps, after(b, 1))
                        act.wait_ge(row_in[par], (nth - 1) * 16)
                        act.copy(neg_row[par][:], src[0:TILES, 0:P]).then_inc(n_row, 1)
                    elif what == "e":
                        act.wait_ge(av, after(b, NT))
                        act.wait_ge(o_ps, after(b - 1, 1))
                        act.copy(oT[:], psO[:]).then_inc(o_c, 1)
                        act.wait_ge(d_ps, after(b - 1, 1))
                        act.copy(denT[:], psD[:]).then_inc(d_c, 1)

            pairs(act, B, 4, step)

        @block.vector
        def _(dve):
            for s in (x_lo, q_lo, k_lo, n_sb, rcp, o_n, o_r):
                dve.sem_inc(s, CREDIT)
            dve.sem_inc(s_mx, CREDIT * TILES)
            norm.credit_dve(dve)
            norm.credit_apply(dve)
            dve.wait_ge(w_in, 16)
            split(dve, Wr[0][:], Wr[1][:], W[:, 0:2 * D], w_hi, 1, w_lo)

            def step(s, par, alive, nth):
                for what, k in ORDER:
                    if not alive[STAGE[what]]:
                        continue
                    src = ring.get((what, k))
                    b = s - STAGE[what]
                    if what == "x":
                        dve.wait_ge(x_c, after(s, 1))
                        dve.wait_ge(k_ps, after(s - 2, 1))
                        dve.tensor_tensor(xTr[par][1][:], xT[par][:], xTr[par][0][:].bitcast(F32),
                                          ALU.subtract).then_inc(x_lo, 1)
                    elif what == "q":
                        dve.wait_ge(q_hi, after(s, 1))
                        dve.tensor_tensor(qkT[par][:, Q_LO], src[:], qkT[par][:, Q_HI].bitcast(F32),
                                          ALU.subtract).then_inc(q_lo, 1)
                    elif what == "k":
                        dve.wait_ge(k_hi, after(s, 1))
                        dve.tensor_tensor(qkT[par][:, K_LO], src[:], qkT[par][:, K_HI].bitcast(F32),
                                          ALU.subtract).then_inc(k_lo, 1)
                    elif what == "s":
                        dve.wait_ge(s_ps, after(b, TILES, k + 1))
                        dve.wait_ge(s_mx, after(b, TILES, k - 1))
                        hold(dve, gate)
                        dve.tensor_tensor_reduce(out=junk[k % 2][:], in0=src[:], in1=m.mask_ij[:, k % NT],
                                                 scale=1.0, scalar=3.0 * MASKED, op0=ALU.add, op1=ALU.max,
                                                 accum_out=mx[1 - par][:, k:k + 1]).then_inc(s_mx, 1)
                    elif what == "g":
                        dve.wait_ge(s_mx, after(b, TILES))
                        dve.wait_ge(n_ps, after(b - 2, 1))
                        dve.tensor_scalar(neg[par][:], mx[par][:], -1.0, None, ALU.mult).then_inc(n_sb, 1)
                    elif what == "m":
                        dve.wait_ge(d_ps, after(b, 1))
                        dve.wait_ge(o_n, after(b - 1, 1))
                        dve.reciprocal(rec[:, :, :, 0], psD[:].rearrange("p (t h d) -> p t h d", h=H, d=HD)[:, :, :, 0]
                                       ).then_inc(rcp, 1)
                        dve.wait_ge(o_ps, after(b, 1))
                        dve.wait_ge(rcp, after(b, 1))
                        dve.wait_ge(norm.s_x, after(b - 2, 4))
                        dve.tensor_tensor(r[1 - par][:].rearrange("p t (h d) -> p t h d", h=H),
                                          ring["o", 0][:].rearrange("p (t h d) -> p t h d", h=H, d=HD),
                                          rec[:].broadcast_to([P, NT, H, HD]), ALU.mult).then_inc(o_n, 1)
                    elif what == "r":
                        dve.wait_ge(o_n, after(b, 1))
                        dve.tensor_tensor(flat(r[1 - par][:]), flat(r[1 - par][:]), batch_flat(m.X, b),
                                          ALU.add).then_inc(o_r, 1)
                    elif what == "b":
                        dve.wait_ge(o_r, after(b, 1))
                        norm.statistics(dve, b + CREDIT, 1 - par, r[1 - par])
                    elif what == "y":
                        norm.apply(dve, b + CREDIT, 1 - par, r[1 - par], lambda k: tile_of(m.X, b, k))

            pairs(dve, B, 4, step)

        @block.tensor
        def _(pe):
            for s in (x_ps, q_ps, k_ps, v_ps, n_ps, o_ps, d_ps):
                pe.sem_inc(s, CREDIT)
            pe.sem_inc(s_ps, CREDIT * TILES)
            pe.sem_inc(t_ps, CREDIT * PAIRS)
            pe.sem_inc(av, CREDIT * NT)
            pe.wait_ge(const, 7)
            pe.wait_ge(w_lo, 1)

            def wait_for_bank(s, alive, item):
                was = [True] * 4 if alive[0] and not isinstance(s, int) else [0 <= s - 1 - k < B for k in range(4)]
                turns = [(s - 1, was, i) for i in RING] + [(s, alive, i) for i in RING]
                for at, live, (what, k) in turns[RING.index(item) + len(RING) - 2::-2]:
                    if live[STAGE[what]]:
                        pe.wait_ge(*released(at, what, k))
                        return

            def step(s, par, alive, nth):
                for what, k in ORDER:
                    if not alive[STAGE[what]]:
                        continue
                    out = ring.get((what, k))
                    b = s - STAGE[what]
                    if out is not None:
                        wait_for_bank(s, alive, (what, k))
                    if what == "x":
                        pe.wait_ge(x_f, after(s, 1))
                        for t in range(NT):
                            last = pe.transpose(out[:, t * P:t * P + P], Xf[par][:, t], m.ident[:])
                        last.then_inc(x_ps, 1)
                    elif what == "q":
                        pe.wait_ge(x_lo, after(s, 1))
                        three_pass(pe, out[:], [h[:, 0:D] for h in Wr], [h[:] for h in xTr[par]]).then_inc(q_ps, 1)
                    elif what == "k":
                        three_pass(pe, out[:], [h[:, D:2 * D] for h in Wr], [h[:] for h in xTr[par]]).then_inc(k_ps, 1)
                    elif what == "v":
                        for t in range(NT):
                            last = pe.matmul(out[:, t * P:t * P + P], xT[1 - par][:, t * P:t * P + P], W[:, 2 * D:],
                                             start=True, stop=True)
                        last.then_inc(v_ps, 1)
                    elif what == "s":
                        h, i = divmod(k, NT)
                        if i == 0:
                            pe.wait_ge(stacked[1 - par][h], (before(par, nth) + 1) * STACKED)
                        pe.matmul(out[:], q_st[1 - par][0:3 * HD, h, i * P:i * P + P], k_st[1 - par][0:3 * HD, h],
                                  start=True, stop=True).then_inc(s_ps, 1)
                    elif what == "n":
                        pe.wait_ge(n_sb, after(b, 1))
                        pe.transpose(out[0:TILES, 0:P], neg[par][:], m.ident[:]).then_inc(n_ps, 1)
                    elif what == "t":
                        h, jp = divmod(k, JP)
                        if k == 0:
                            pe.wait_ge(row_in[par], nth * 16)
                        pe.wait_ge(t_exp, after(b, PAIRS, k - 1))
                        for jj in range(2):
                            j = jp * 2 + jj
                            ps = wide[k % 2][:, jj * N:jj * N + N]
                            pe.matmul(ps, k_st[par][:, h, j * P:j * P + P], q_st[par][:, h], start=True, stop=False)
                            last = pe.matmul(ps, m.identb[:], m.mask_ji[:, j], start=False, stop=True)
                        last.then_inc(t_ps, 1)
                    elif what == "a":
                        if k == 0:
                            pe.wait_ge(t_exp, after(b, PAIRS))
                            pe.wait_ge(o_c, after(b - 1, 1))
                            pe.wait_ge(rcp, after(b - 1, 1))
                        jp, jj = divmod(k, 2)
                        for ps, stat in ((psO, None), (psD, ones)):
                            for h in range(H):
                                c = slice(h * HD, (h + 1) * HD)
                                last = pe.matmul(ps[c, :], v[1 - par][:, k, c] if stat is None else stat[:],
                                                 prob[jp][h][:, jj], start=(k == 0), stop=(k == NT - 1),
                                                 skip_group_check=True)
                        last.then_inc(av, 1)
                    elif what == "o":
                        pe.wait_ge(o_c, after(b, 1))
                        for t in range(NT):
                            last = pe.transpose(out[:, t * P:t * P + P], oT[:, t * P:t * P + P], m.ident[:])
                        last.then_inc(o_ps, 1)
                    elif what == "d":
                        pe.wait_ge(d_c, after(b, 1))
                        for t in range(NT):
                            last = pe.transpose(psD[:, t * P:t * P + P], denT[:, t * P:t * P + P], m.ident[:])
                        last.then_inc(d_ps, 1)

            pairs(pe, B, 4, step)


def layer3(nc, m, ins, bank, out):
    SLOPE = 0.2
    with ExitStack() as own:
        def sb(name, shape, dt=F32):
            return own.enter_context(nc.sbuf_tensor(name, shape, dt))

        def sem(name):
            return own.enter_context(nc.semaphore(name))

        WX = sb("WX", [P, D + 2])
        a_sb = sb("a_sb", [P, 2])
        WT = sb("WT", [P, D])
        ones = sb("ones3", [P, P])
        onesb = sb("onesb", [P, P], BF16)
        wB = [sb(f"wB{k}", [P, P]) for k in range(2)]
        Xf = [sb(f"Xc{k}", [P, NT, D]) for k in range(2)]
        xT = [sb(f"xTc{k}", [P, N]) for k in range(2)]
        Wh = [sb(f"Wh{k}", [P, NT, D + 2]) for k in range(2)]
        s12 = [sb(f"s12{k}", [P, NT, 2]) for k in range(2)]
        s2s = [sb(f"s2s{k}", [P, 2, NT]) for k in range(2)]
        junk = [sb(f"junk3{k}", [P, N], BF16) for k in range(2)]
        mx = [sb(f"mx3{k}", [P, NT]) for k in range(2)]
        em = [sb(f"em{k}", [P, 3, NT]) for k in range(2)]
        dg = [sb(f"dg{k}", [P, NT, P], BF16) for k in range(2)]
        rl = [sb(f"rl{k}", [P, NT, N]) for k in range(2)]
        pr = [sb(f"pr{k}", [P, NT, N]) for k in range(2)]
        rec = [sb(f"rec3{k}", [P, NT]) for k in range(2)]
        r = [sb(f"rc{k}", [P, NT, D]) for k in range(2)]
        norm = Norm(nc, own, m, "n3")

        w_in = sem("w_in"); const = sem("const"); wt_ps = sem("WT_in_psum"); wt_c = sem("WT_out")
        wa_ps = sem("Wa_in_psum"); wa_c = sem("Wa_out"); wb_c = sem("Wa_spread")
        x_f = sem("x_copied")
        x_ps = sem("x_turned"); x_c = sem("xT_out")
        wh_ps = sem("Wh_in_psum"); s_c = sem("s_out"); wh_c = sem("Wh_out")
        ss = sem("s2_scaled")
        s2_ps = sem("s2_rows"); s1_ps = sem("s1_rows")
        s_mx = sem("row_max")
        e_m = sem("max_terms")
        d_g = sem("diagonals")
        relu = sem("relu")
        r_ps = sem("mask_and_rows"); e_s = sem("e_summed")
        ex = sem("exp_done"); av = sem("values")
        rcp = sem("reciprocal")
        res = sem("residual")
        stored = [sem(f"stored{k}") for k in range(2)]
        gate = sem("gate")
        half = [bank[3], bank[0]]
        out_bank = [bank[6], bank[7]]
        block = own.enter_context(nc.Block())

        STAGE = dict(x=0, w=0, j=0, i=0, m=0, c=0, l=0, e=1, E=1, a=2, r=2, b=2)
        ORDER = []
        for what in "a a x a a e e w w r E e e r m r j i r E m l m m c l l l b".split():
            ORDER.append((what, sum(w == what for w, _ in ORDER)))

        @block.sync
        def _(sp):
            sp.dma_start(WX[:, 0:D], ins["L3_gnn_W"]).then_inc(w_in, 16)
            with nc.allow_non_contiguous_dma(reason="256 words once"):
                sp.dma_start(a_sb[:], ins["L3_gnn_a"].rearrange("(k p) a -> p (k a)", p=P)).then_inc(w_in, 16)
            sp.wait_ge(w_in, 32)
            for k in range(2):
                sp.sem_inc(stored[k], 16)

            def step(s, par, alive, nth):
                if alive[0]:
                    sp.wait_ge(norm.s_x, after(s, 4))
                    hold(sp, gate)
                    sp.dma_start(out[bass.ds(s, 1)].rearrange("a (t p) d -> p (a t) d", p=P),
                                 r[par][:]).then_inc(stored[par], 16)

            pairs(sp, B, 1, step)
            for k in range(2):
                sp.wait_ge(stored[k], 16 + 16 * (B // 2))

        @block.gpsimd
        def _(pool):
            pool.sem_inc(x_f, CREDIT)
            norm.credit_pool(pool)
            norm.credit_apply(pool)
            for n, ap in enumerate((ones[:], onesb[:], Wh[0][:, :, D:D + 1], Wh[1][:, :, D:D + 1])):
                pool.wait_ge(const, n)
                pool.memset(ap, 1.0).then_inc(const, 1)
            pool.wait_ge(const, 4)

            def step(s, par, alive, nth):
                if alive[0]:
                    pool.wait_ge(x_ps, after(s - 2, 1))
                    if alive[3]:
                        pool.wait_ge(norm.s_x, after(s - 4, 4))
                    pool.tensor_copy(flat(Xf[par][:]), batch_flat(m.X, s)).then_inc(x_f, 1)
                if alive[3]:
                    b = s - 3
                    pool.wait_ge(x_f, after(s if alive[0] else B - 1, 1))
                    norm.root(pool, b + CREDIT, 1 - par)
                    norm.apply(pool, b + CREDIT, 1 - par, r[1 - par], lambda k: r[1 - par][:, k])

            pairs(pool, B, 4, step)

        @block.scalar
        def _(act):
            act.sem_inc(x_c, CREDIT)
            act.sem_inc(ex, CREDIT * 2)
            act.sem_inc(wh_c, CREDIT * 2)
            act.sem_inc(relu, CREDIT * NT)

            def step(s, par, alive, nth):
                for what, k in ORDER:
                    if not alive[STAGE[what]]:
                        continue
                    b = s - STAGE[what]
                    if what == "x":
                        act.wait_ge(x_ps, after(s, 1))
                        act.wait_ge(s1_ps, after(s - 2, 1))
                        act.copy(xT[par][:], bank[0][:]).then_inc(x_c, 1)
                    elif what == "w":
                        act.wait_ge(av, after(s - 2, NT))
                        act.wait_ge(s_c, after(s, 2, k + 1))
                        act.copy(Wh[par][:, 2 * k:2 * k + 2, 0:D],
                                 half[k][:, 0:2 * (D + 2)].rearrange("p (t d) -> p t d", t=2)[:, :, 0:D]).then_inc(wh_c, 1)
                    elif what == "l":
                        if k == 0:
                            act.wait_ge(s1_ps, after(s, 1))
                            act.wait_ge(ss, after(s, 2))
                            act.wait_ge(e_s, after(s - 2, NT))
                        act.activation(rl[par][:, k], bank[1][:], ACT.Relu, scale=1.0 - SLOPE,
                                       bias=s2s[par][:, 0, k:k + 1]).then_inc(relu, 1)
                    elif what == "E":
                        act.wait_ge(e_s, after(b, NT, 2 * k + 2))
                        two = flat(pr[1 - par][:, 2 * k:2 * k + 2])
                        act.activation(two, two, ACT.Exp).then_inc(ex, 1)

            pairs(act, B, 3, step)

        @block.vector
        def _(dve):
            dve.sem_inc(s_c, CREDIT * 2)
            dve.sem_inc(ss, CREDIT * 2)
            dve.sem_inc(s_mx, CREDIT * NT)
            dve.sem_inc(e_m, CREDIT * 3)
            dve.sem_inc(d_g, CREDIT * NT)
            dve.sem_inc(e_s, CREDIT * NT)
            dve.sem_inc(rcp, CREDIT * 2)
            dve.sem_inc(res, CREDIT * NT)
            norm.credit_dve(dve)
            dve.wait_ge(wt_ps, 1)
            dve.tensor_copy(WT[:], bank[0][:, 0:D]).then_inc(wt_c, 1)
            dve.wait_ge(wa_ps, 1)
            dve.tensor_copy(WX[:, D:D + 2], bank[1][:, 0:2]).then_inc(wa_c, 1)
            dve.wait_ge(wa_c, 1)
            dve.wait_ge(const, 1)
            for k in range(2):
                dve.tensor_scalar(wB[k][:], ones[:], WX[:, D + k:D + k + 1], None, ALU.mult).then_inc(wb_c, 1)

            def step(s, par, alive, nth):
                for what, k in ORDER:
                    if not alive[STAGE[what]]:
                        continue
                    b = s - STAGE[what]
                    if what == "w":
                        dve.wait_ge(wh_ps, after(s, 2, k + 1))
                        dve.tensor_copy(s12[par][:, 2 * k:2 * k + 2],
                                        half[k][:, 0:2 * (D + 2)].rearrange("p (t d) -> p t d", t=2)[:, :, D:]).then_inc(s_c, 1)
                        if k == 1:
                            dve.wait_ge(s_c, after(s, 2))
                            dve.wait_ge(relu, after(s - 2, NT))
                            for n, f in enumerate((1.0 - SLOPE, SLOPE)):
                                dve.tensor_scalar(s2s[par][:, n], s12[par][:, :, 1], f, None, ALU.mult).then_inc(ss, 1)
                    elif what == "m":
                        dve.wait_ge(s2_ps, after(s, 1))
                        dve.wait_ge(s_mx, after(s, NT, k - 1))
                        hold(dve, gate)
                        dve.tensor_tensor_reduce(out=junk[k % 2][:], in0=bank[2][:], in1=m.mask_ij[:, k],
                                                 scale=1.0, scalar=3.0 * MASKED, op0=ALU.add, op1=ALU.max,
                                                 accum_out=mx[par][:, k:k + 1]).then_inc(s_mx, 1)
                    elif what == "e":
                        if k == 0:
                            dve.wait_ge(av, after(b - 2, NT))
                        dve.wait_ge(relu, after(b, NT, k + 1))
                        dve.wait_ge(r_ps, after(b, NT, k + 1))
                        dve.scalar_tensor_tensor(out=pr[1 - par][:, k], in0=bank[4 + k % 2][:],
                                                 scalar=s2s[1 - par][:, 1, k:k + 1], in1=rl[1 - par][:, k],
                                                 op0=ALU.add, op1=ALU.add).then_inc(e_s, 1)
                    elif what == "c":
                        s1 = s12[par][:, :, 0]
                        dve.wait_ge(s_mx, after(s, NT))
                        dve.tensor_tensor(em[par][:, 0], s1, mx[par][:], ALU.add).then_inc(e_m, 1)
                        dve.wait_ge(e_m, after(s, 3, 1))
                        dve.scalar_tensor_tensor(out=em[par][:, 1], in0=em[par][:, 0], scalar=SLOPE, in1=em[par][:, 0],
                                                 op0=ALU.mult, op1=ALU.max).then_inc(e_m, 1)
                        dve.wait_ge(e_m, after(s, 3, 2))
                        dve.wait_ge(d_g, after(s - 2, NT))
                        dve.scalar_tensor_tensor(out=em[par][:, 2], in0=s1, scalar=SLOPE, in1=em[par][:, 1],
                                                 op0=ALU.mult, op1=ALU.subtract).then_inc(e_m, 1)
                        dve.wait_ge(e_m, after(s, 3))
                        dve.wait_ge(r_ps, after(s - 2, NT))
                        for t in range(NT):
                            dve.tensor_scalar(dg[par][:, t], m.identb[:], em[par][:, 2, t:t + 1], None,
                                              ALU.mult).then_inc(d_g, 1)
                    elif what == "r":
                        h, t = divmod(k, 2)
                        if t == 0:
                            dve.wait_ge(av, after(b, NT, k + 2))
                            dve.wait_ge(res, after(b - 2, NT))
                            dve.reciprocal(rec[par][:, k:k + 2],
                                           out_bank[h][:, 0:2 * (D + 2)].rearrange("p (t d) -> p t d", t=2)[:, :, D]
                                           ).then_inc(rcp, 1)
                            dve.wait_ge(rcp, after(b, 2, h + 1))
                            dve.wait_ge(stored[par], nth * 16)
                        dve.scalar_tensor_tensor(out=r[par][:, k], in0=out_bank[h][:, t * (D + 2):t * (D + 2) + D],
                                                 scalar=rec[par][:, k:k + 1], in1=tile_of(m.X, b, k),
                                                 op0=ALU.mult, op1=ALU.add).then_inc(res, 1)
                    elif what == "b":
                        dve.wait_ge(res, after(b, NT))
                        norm.statistics(dve, b + CREDIT, par, r[par])

            pairs(dve, B, 3, step)

        @block.tensor
        def _(pe):
            for s in (x_ps, s2_ps, s1_ps):
                pe.sem_inc(s, CREDIT)
            pe.sem_inc(av, CREDIT * NT)
            pe.sem_inc(wh_ps, CREDIT * 2)
            pe.sem_inc(r_ps, CREDIT * NT)
            pe.wait_ge(w_in, 32)
            pe.transpose(bank[0][:, 0:D], WX[:, 0:D], m.ident[:]).then_inc(wt_ps, 1)
            pe.wait_ge(wt_c, 1)
            pe.matmul(bank[1][:, 0:2], WT[:], a_sb[:], start=True, stop=True).then_inc(wa_ps, 1)
            pe.wait_ge(wb_c, 2)
            pe.wait_ge(const, 4)

            def step(s, par, alive, nth):
                for what, k in ORDER:
                    if not alive[STAGE[what]]:
                        continue
                    b = s - STAGE[what]
                    if what == "x":
                        pe.wait_ge(x_f, after(s, 1))
                        pe.wait_ge(wh_c, after(s - 1, 2))
                        for t in range(NT):
                            last = pe.transpose(bank[0][:, t * P:t * P + P], Xf[par][:, t], m.ident[:])
                        last.then_inc(x_ps, 1)
                    elif what == "w":
                        pe.wait_ge(x_c, after(s, 1))
                        for t in range(2):
                            last = pe.matmul(half[k][:, t * (D + 2):(t + 1) * (D + 2)],
                                             xT[par][:, (2 * k + t) * P:(2 * k + t + 1) * P], WX[:],
                                             start=True, stop=True)
                        last.then_inc(wh_ps, 1)
                    elif what == "j":
                        pe.wait_ge(x_c, after(s, 1))
                        pe.wait_ge(s_mx, after(s - 1, NT))
                        pe.matmul(bank[2][:], wB[1][:], xT[par][:], start=True, stop=True).then_inc(s2_ps, 1)
                    elif what == "i":
                        pe.wait_ge(relu, after(s - 1, NT))
                        pe.matmul(bank[1][:], wB[0][:], xT[par][:], start=True, stop=True).then_inc(s1_ps, 1)
                    elif what == "a":
                        h, t = divmod(k, 2)
                        pe.wait_ge(ex, after(b, 2))
                        pe.wait_ge(res, after(b - 1, NT, 2 * h + 2))
                        for j in range(NT):
                            last = pe.matmul(out_bank[h][:, t * (D + 2):t * (D + 2) + D + 1],
                                             pr[par][:, j, k * P:k * P + P], Wh[par][:, j, 0:D + 1],
                                             start=(j == 0), stop=(j == NT - 1))
                        last.then_inc(av, 1)
                    elif what == "e":
                        pe.wait_ge(d_g, after(b, NT))
                        pe.wait_ge(e_s, after(b, NT, k - 1))
                        pe.matmul(bank[4 + k % 2][:], m.identb[:], m.mask_ji[:, k], start=True, stop=False)
                        pe.matmul(bank[4 + k % 2][:], onesb[:], flat(dg[1 - par][:]), start=False, stop=True).then_inc(r_ps, 1)

            pairs(pe, B, 3, step)


def build(nc, ins, out):
    with ExitStack() as ctx:
        wide = [ctx.enter_context(nc.psum_tensor(f"wide{k}", [P, 1024], F32)) for k in range(2)]
        bank = [w[:, k * 512:k * 512 + 512] for w in wide for k in range(2)]
        bank += [ctx.enter_context(nc.psum_tensor(f"bank{k}", [P, 512], F32))[:] for k in range(4, 8)]
        m = Memory()
        setup_constants(nc, ctx, m, ins, bank)
        with ExitStack() as first:
            layer0_setup(nc, first, m, ins, bank)
            layer0(nc, m, bank)
        layer1(nc, m, ins, bank)
        layer2(nc, m, ins, bank, wide)
        layer3(nc, m, ins, bank, out)


_INS = ["x", "adj", "L0_gnn_alpha_train", "L0_gnn_w", "L0_gnn_d", "L0_gnn_fc_in_w", "L0_gnn_fc_in_b",
        "L1_gnn_W1", "L1_gnn_b1", "L1_gnn_g1", "L1_gnn_be1", "L1_gnn_W2", "L1_gnn_b2", "L1_gnn_g2", "L1_gnn_be2",
        "L2_gnn_W", "L3_gnn_W", "L3_gnn_a"]


def kernel(**inputs):
    import numpy as _np
    import concourse.bacc as _bacc
    from concourse.bass_utils import run_bass_kernel_spmd as _run

    nc = _bacc.Bacc("TRN2", target_bir_lowering=False, num_devices=1)
    arrays, ins = {}, {}
    for name in _INS:
        a = _np.ascontiguousarray(inputs[name])
        arrays[f"in_{name}_dram"] = a
        ins[name] = nc.dram_tensor(f"in_{name}_dram", a.shape, mybir.dt.from_np(a.dtype), kind="ExternalInput").ap()
    out = nc.dram_tensor("out_0_dram", (B, N, D), F32, kind="ExternalOutput").ap()
    build(nc, ins, out)
    r = _run(nc, [arrays], core_ids=[0])
    return r.results[0]["out_0_dram"]
```

```python
from contextlib import ExitStack
from math import comb

import concourse.bass as bass
from concourse import mybir

F32 = mybir.dt.float32
F32R = mybir.dt.float32r
BF16 = mybir.dt.bfloat16
ALU = mybir.AluOpType
ACT = mybir.ActivationFunctionType
AX = mybir.AxisListType

P = 128
B, N, D = 16, 512, 128
NT = N // P
STEPS = 8
DT = 1.0 / STEPS
BABY = 3
H, HD = 4, D // 4
CH = 256 // P
EPS = 1e-5
MASKED = -1.0e30
CREDIT = 2


def after(b, per, k=None):
    return (b + CREDIT) * per + (per if k is None else k)


def hold(eng, gate):
    eng.sem_inc(gate, 1)


def flat(ap):
    return ap.rearrange("p a b -> p (a b)")


def three_pass(pe, out, stat, mov, start=True, stop=True):
    pe.matmul(out, stat[0], mov[0], start=start, stop=False)
    pe.matmul(out, stat[0], mov[1], start=False, stop=False)
    return pe.matmul(out, stat[1], mov[0], start=False, stop=stop)


class Memory:
    pass


def setup_constants(nc, ctx, m, ins, bank):
    def sb(name, shape, dt=F32):
        return ctx.enter_context(nc.sbuf_tensor(name, shape, dt))

    m.X = sb("X", [P, B, NT, D])
    m.ident = sb("ident", [P, P])
    m.identb = sb("identb", [P, P], BF16)
    m.neg_half = sb("neg_half", [P, 16])
    m.mask_ij = sb("mask_ij", [P, NT, N], BF16)
    m.mask_ji = sb("mask_ji", [P, NT, N], BF16)
    m.AhT = [sb("AhT_hi", [P, NT, N], F32R), sb("AhT_lo", [P, NT, N], F32R)]


def layer0_setup(nc, ctx, m, ins, bank):
    def keep(name, shape, dt=F32):
        return ctx.enter_context(nc.sbuf_tensor(name, shape, dt))

    m.LT = [keep("LT_hi", [P, NT, N], F32R), keep("LT_lo", [P, NT, N], F32R)]
    m.L2T = [keep("L2T_hi", [P, NT, N], F32R), keep("L2T_lo", [P, NT, N], F32R)]
    m.L3T = [keep("L3T_hi", [P, NT, N], F32R), keep("L3T_lo", [P, NT, N], F32R)]
    m.Pj = [keep("Pj_hi", [P, 9, D], F32R), keep("Pj_lo", [P, 9, D], F32R)]
    m.bias = keep("bias_field", [P, NT, BABY, D])

    with ExitStack() as own:
        def sb(name, shape, dt=F32):
            return own.enter_context(nc.sbuf_tensor(name, shape, dt))

        sems = []

        def sem(name):
            sems.append(nc.alloc_semaphore(name))
            return sems[-1]

        A = sb("A", [P, NT, N])
        A1 = sb("A1", [P, NT, N])
        L = sb("L", [P, NT, N])
        LTf = sb("LTf", [P, NT, N])
        ATf = sb("ATf", [P, NT, N])
        Lr = [sb("L_hi", [P, NT, N], F32R), sb("L_lo", [P, NT, N], F32R)]
        w_sb = sb("w_sb", [P, D])
        fc = sb("fc", [P, D])
        d_col = sb("d_col", [P, 1])
        b_col = sb("b_col", [P, 1])
        al = sb("al", [P, NT])
        ea = sb("ea", [P, NT])
        col = sb("col", [P, 8, NT])
        ones = sb("ones", [P, P])
        wT = sb("wT", [P, D])
        wTs = sb("wTs", [P, D])
        RP = sb("RP", [P, 9, D])
        Pf = sb("Pf", [P, 9, D])
        cB = sb("cB", [P, 9, D])
        bB = sb("bB", [P, P])
        Y = sb("Y", [P, 2, NT])
        junk = sb("junk", [P, P])
        diag = sb("diag", [P, NT])
        deg = sb("deg", [P, 4, NT])
        dinv = sb("dinv", [P, NT])

        a_in = sem("a_in"); small_in = sem("small_in"); x_in = sem("x_in")
        pool_c = sem("pool_c"); ident_b = sem("ident_b")
        exp_a = sem("exp_a"); v_col = sem("v_col"); v_L = sem("v_L"); v_Lhi = sem("v_Lhi"); v_Llo = sem("v_Llo")
        t_AT = sem("t_AT"); c_AT = sem("c_AT"); v_mji = sem("v_mji"); v_mij = sem("v_mij")
        t_LT = sem("t_LT"); c_LTf = sem("c_LTf"); c_LTh = sem("c_LTh"); v_LTl = sem("v_LTl")
        t_L2 = sem("t_L2"); c_L2h = sem("c_L2h"); v_L2l = sem("v_L2l")
        t_L3 = sem("t_L3"); c_L3h = sem("c_L3h"); v_L3l = sem("v_L3l")
        t_Ah = sem("t_Ah"); c_Ahh = sem("c_Ahh"); v_Ahl = sem("v_Ahl")
        v_A1 = sem("v_A1"); v_deg = sem("v_deg"); p_dinv = sem("p_dinv"); v_As = sem("v_As")
        t_wT = sem("t_wT"); v_dc = sem("v_dc"); v_wT = sem("v_wT"); t_R = sem("t_R"); v_R = sem("v_R")
        t_Q = sem("t_Q"); v_P = sem("v_P"); t_cB = sem("t_cB"); v_cB = sem("v_cB")
        v_Y1 = sem("v_Y1"); t_Y2 = sem("t_Y2"); v_Y2 = sem("v_Y2"); v_bias = sem("v_bias"); v_bB = sem("v_bB")

        c_c, c_d, c_rs = (col[:, k, :] for k in range(3))
        block = own.enter_context(nc.Block())

        @block.sync
        def _(sp):
            sp.dma_start(A[:], ins["adj"].rearrange("(t p) m -> p t m", p=P)).then_inc(a_in, 16)
            sp.dma_start(w_sb[:], ins["L0_gnn_w"]).then_inc(small_in, 16)
            sp.dma_start(fc[:], ins["L0_gnn_fc_in_w"]).then_inc(small_in, 16)
            sp.dma_start(d_col[:], ins["L0_gnn_d"].rearrange("(p a) -> p a", a=1)).then_inc(small_in, 16)
            sp.dma_start(b_col[:], ins["L0_gnn_fc_in_b"].rearrange("(p a) -> p a", a=1)).then_inc(small_in, 16)
            with nc.allow_non_contiguous_dma(reason="512 words once"):
                sp.dma_start(al[:], ins["L0_gnn_alpha_train"].rearrange("(t p) -> p t", p=P)).then_inc(small_in, 16)
            for b in range(0, B, 4):
                sp.dma_start(m.X[:, b:b + 4].rearrange("p b t d -> p (b t) d"),
                             ins["x"][b:b + 4].rearrange("b (t p) d -> p (b t) d", p=P)).then_inc(x_in, 16)
            sp.wait_ge(x_in, 16 * (B // 4))

        @block.gpsimd
        def _(pool):
            pool.memset(m.ident[:], 0.0).then_inc(pool_c, 1)
            pool.memset(ones[:], 1.0).then_inc(pool_c, 1)
            pool.memset(m.neg_half[:], -0.5).then_inc(pool_c, 1)
            pool.wait_ge(pool_c, 3)
            pool.affine_select(out=m.ident[:], in_=m.ident[:], compare_op=ALU.not_equal, fill=1.0, base=0,
                               pattern=[[-1, P]], channel_multiplier=1).then_inc(pool_c, 1)
            pool.wait_ge(a_in, 16)
            pool.tensor_scalar(flat(m.mask_ij[:]), flat(A[:]), 0.0, MASKED, ALU.is_equal, ALU.mult).then_inc(v_mij, 1)
            pool.wait_ge(c_AT, NT)
            pool.tensor_scalar(flat(m.mask_ji[:]), flat(ATf[:]), 0.0, MASKED, ALU.is_equal, ALU.mult).then_inc(v_mji, 1)
            pool.wait_ge(v_deg, 4)
            pool.tensor_tensor(dinv[:], deg[:, 2], m.neg_half[:, 0:NT], ALU.pow).then_inc(p_dinv, 1)

        @block.scalar
        def _(act):
            act.wait_ge(small_in, 80)
            act.activation(ea[:], al[:], ACT.Exp, scale=-1.0).then_inc(exp_a, 1)
            for q in range(NT):
                act.wait_ge(t_AT, q + 1)
                act.activation(ATf[:, q], bank[q][:], ACT.Copy, accum_out=deg[:, 3, q:q + 1]).then_inc(c_AT, 1)
            for q in range(NT):
                act.wait_ge(t_LT, q + 1)
                act.copy(LTf[:, q], bank[q][:]).then_inc(c_LTf, 1)
            for q in range(NT):
                act.wait_ge(c_LTf, q + 1)
                act.copy(m.LT[0][:, q], LTf[:, q]).then_inc(c_LTh, 1)

            def high(dst, q, ready, done):
                act.wait_ge(ready, q + 1)
                act.copy(dst[0][:, q], bank[q % 2][:]).then_inc(done, 1)

            def adjacency(q):
                act.wait_ge(p_dinv, 1)
                act.wait_ge(t_Ah, q + 1)
                act.activation(m.AhT[0][:, q], bank[2 + q % 2][:], ACT.Copy, scale=dinv[:, q:q + 1]).then_inc(c_Ahh, 1)

            for q in range(NT):
                high(m.L2T, q, t_L2, c_L2h)
            adjacency(0)
            adjacency(1)
            high(m.L3T, 0, t_L3, c_L3h)
            adjacency(2)
            high(m.L3T, 1, t_L3, c_L3h)
            adjacency(3)
            high(m.L3T, 2, t_L3, c_L3h)
            high(m.L3T, 3, t_L3, c_L3h)

        @block.vector
        def _(dve):
            dve.wait_ge(pool_c, 4)
            dve.tensor_copy(m.identb[:], m.ident[:]).then_inc(ident_b, 1)
            dve.wait_ge(small_in, 80)
            dve.tensor_scalar(d_col[:], d_col[:], 0.0, 1.0, ALU.max, ALU.min).then_inc(v_dc, 1)
            dve.tensor_scalar(bB[:], ones[:], b_col[:], None, ALU.mult).then_inc(v_bB, 1)
            dve.wait_ge(exp_a, 1)
            dve.tensor_scalar(col[:, 3, :], ea[:], 1.0, None, ALU.add).then_inc(v_col, 1)
            dve.wait_ge(v_col, 1)
            dve.reciprocal(col[:, 4, :], col[:, 3, :]).then_inc(v_col, 1)
            dve.wait_ge(v_col, 2)
            dve.tensor_scalar(c_c, col[:, 4, :], DT / 2, None, ALU.mult).then_inc(v_col, 1)
            dve.wait_ge(v_col, 3)
            dve.tensor_scalar(c_d, c_c, -1.0, 1.0 - DT, ALU.mult, ALU.add).then_inc(v_col, 1)
            dve.wait_ge(v_col, 4)
            dve.wait_ge(a_in, 16)
            for t in range(NT):
                dve.tensor_scalar(L[:, t], A[:, t], c_c[:, t:t + 1], None, ALU.mult).then_inc(v_L, 1)
            dve.wait_ge(v_L, NT)
            for t in range(NT):
                s = slice(t * P, t * P + P)
                dve.scalar_tensor_tensor(out=L[:, t, s], in0=m.ident[:], scalar=c_d[:, t:t + 1], in1=L[:, t, s],
                                         op0=ALU.mult, op1=ALU.add).then_inc(v_L, 1)
            dve.wait_ge(t_wT, 1)
            dve.tensor_copy(wT[:], bank[4][:, 0:D]).then_inc(v_wT, 1)
            dve.wait_ge(v_dc, 1)
            dve.wait_ge(v_wT, 1)
            dve.tensor_scalar(wTs[:], wT[:], d_col[:], DT, ALU.mult, ALU.mult).then_inc(v_wT, 1)
            dve.wait_ge(v_L, 2 * NT)
            dve.tensor_copy(flat(Lr[0][:]), flat(L[:])).then_inc(v_Lhi, 1)
            dve.wait_ge(v_Lhi, 1)
            dve.tensor_tensor(flat(Lr[1][:]), flat(L[:]), flat(Lr[0][:].bitcast(F32)), ALU.subtract).then_inc(v_Llo, 1)

            def low(mat, q, high_done, done):
                dve.wait_ge(high_done, q + 1)
                dve.tensor_tensor(mat[1][:, q], bank[q % 2][:], mat[0][:, q].bitcast(F32), ALU.subtract).then_inc(done, 1)

            def adjacency_low(q):
                dve.wait_ge(c_Ahh, q + 1)
                dve.scalar_tensor_tensor(out=m.AhT[1][:, q], in0=bank[2 + q % 2][:], scalar=dinv[:, q:q + 1],
                                         in1=m.AhT[0][:, q].bitcast(F32), op0=ALU.mult,
                                         op1=ALU.subtract).then_inc(v_Ahl, 1)

            def power(k):
                a, n = ((1, 1), (2, 1), (3, 2), (5, 4))[k]
                dve.wait_ge(t_R, k + 1)
                dve.tensor_copy(flat(RP[:, a:a + n]), bank[5 + k % 2][:, 0:n * D]).then_inc(v_R, 1)

            def in_bank(first, k):
                return bank[first + 2][:, 0:D] if k == 0 else bank[first + (k - 1) // 4][:, (k - 1) % 4 * D:(k - 1) % 4 * D + D]

            def P_with(k):
                dve.wait_ge(v_P, 9 + sum(8 - i for i in range(k)))
                for j in range(8 - k):
                    dve.scalar_tensor_tensor(out=Pf[:, j], in0=RP[:, k], scalar=DT * comb(j + k, j), in1=Pf[:, j],
                                             op0=ALU.mult, op1=ALU.add).then_inc(v_P, 1)

            dve.tensor_copy(RP[:, 0], m.ident[:]).then_inc(v_R, 1)
            power(0)
            for q in range(NT):
                dve.wait_ge(c_LTh, q + 1)
                dve.tensor_tensor(m.LT[1][:, q], LTf[:, q], m.LT[0][:, q].bitcast(F32), ALU.subtract).then_inc(v_LTl, 1)
            dve.tensor_copy(flat(A1[:]), flat(A[:])).then_inc(v_A1, 1)
            dve.wait_ge(v_A1, 1)
            for t in range(NT):
                s = slice(t * P, t * P + P)
                dve.tensor_tensor(A1[:, t, s], A[:, t, s], m.ident[:], ALU.add).then_inc(v_A1, 1)
            power(1)
            dve.wait_ge(v_A1, 1 + NT)
            for t in range(NT):
                s = slice(t * P, t * P + P)
                dve.tensor_tensor_reduce(out=junk[:], in0=A1[:, t, s], in1=m.ident[:], scale=1.0, scalar=0.0,
                                         op0=ALU.mult, op1=ALU.add, accum_out=diag[:, t:t + 1]).then_inc(v_A1, 1)
                dve.wait_ge(v_A1, 2 + NT + t)
            dve.tensor_reduce(deg[:, 0], A1[:], AX.X, ALU.add).then_inc(v_deg, 1)
            dve.wait_ge(v_deg, 1)
            dve.tensor_tensor(deg[:, 1], deg[:, 0], diag[:], ALU.subtract).then_inc(v_deg, 1)
            dve.wait_ge(v_deg, 2)
            dve.wait_ge(c_AT, NT)
            dve.scalar_tensor_tensor(out=deg[:, 2], in0=deg[:, 1], scalar=1.0, in1=deg[:, 3], op0=ALU.add,
                                     op1=ALU.add).then_inc(v_deg, 2)
            low(m.L2T, 0, c_L2h, v_L2l)
            power(2)
            low(m.L2T, 1, c_L2h, v_L2l)
            power(3)
            dve.tensor_reduce(Y[:, 0], L[:], AX.X, ALU.add).then_inc(v_Y1, 1)
            dve.wait_ge(p_dinv, 1)
            for t in range(NT):
                dve.tensor_scalar(A1[:, t], A1[:, t], dinv[:, t:t + 1], None, ALU.mult).then_inc(v_As, 1)
            low(m.L2T, 2, c_L2h, v_L2l)
            dve.wait_ge(t_Q, 3)
            for j in range(9):
                dve.tensor_scalar(Pf[:, j], in_bank(4, 8 - j), float(comb(8, j)), None, ALU.mult).then_inc(v_P, 1)
            low(m.L2T, 3, c_L2h, v_L2l)
            adjacency_low(0)
            adjacency_low(1)
            P_with(0)
            low(m.L3T, 0, c_L3h, v_L3l)
            adjacency_low(2)
            for k in range(1, 8):
                P_with(k)
            dve.wait_ge(v_P, 9 + 36)
            dve.tensor_tensor(Pf[:, 0], Pf[:, 0], m.ident[:], ALU.add).then_inc(v_P, 1)
            dve.wait_ge(v_P, 9 + 36 + 1)
            dve.tensor_copy(flat(m.Pj[0][:]), flat(Pf[:])).then_inc(v_P, 1)
            low(m.L3T, 1, c_L3h, v_L3l)
            adjacency_low(3)
            dve.wait_ge(v_P, 9 + 36 + 2)
            dve.tensor_tensor(flat(m.Pj[1][:]), flat(Pf[:]), flat(m.Pj[0][:].bitcast(F32)), ALU.subtract).then_inc(v_P, 1)
            dve.wait_ge(t_cB, 3)
            for j in range(9):
                dve.tensor_scalar(cB[:, j], in_bank(4, 8 - j), float(comb(8, j)), None, ALU.mult).then_inc(v_cB, 1)
            dve.wait_ge(t_Y2, 1)
            dve.tensor_copy(Y[:, 1], bank[7][:, 8:8 + NT]).then_inc(v_Y2, 1)
            low(m.L3T, 2, c_L3h, v_L3l)
            dve.wait_ge(v_Y2, 1)
            dve.wait_ge(v_cB, 9)
            c_view = cB[:].rearrange("p (g i) d -> p g i d", i=BABY)
            for i in (1, 2):
                for t in range(NT):
                    dve.scalar_tensor_tensor(out=m.bias[:, t], in0=c_view[:, :, i], scalar=Y[:, i - 1, t:t + 1],
                                             in1=c_view[:, :, 0] if i == 1 else m.bias[:, t],
                                             op0=ALU.mult, op1=ALU.add).then_inc(v_bias, 1)
                dve.wait_ge(v_bias, NT * i)
            low(m.L3T, 3, c_L3h, v_L3l)

        @block.tensor
        def _(pe):
            def transpose(src, q, out, done):
                for t in range(NT):
                    last = pe.transpose(out[:, t * P:t * P + P], src[:, t, q * P:q * P + P], m.ident[:])
                last.then_inc(done, 1)

            def times_L(q, mov, done):
                for k in range(NT):
                    s = slice(q * P, q * P + P)
                    last = three_pass(pe, bank[q % 2][:], (Lr[0][:, k, s], Lr[1][:, k, s]),
                                      (mov[0][:, k], mov[1][:, k]), start=(k == 0), stop=(k == NT - 1))
                last.then_inc(done, 1)

            def square(q):
                if q < 2:
                    pe.wait_ge(c_LTf, q + 1)
                else:
                    pe.wait_ge(v_L2l, q - 1)
                times_L(q, m.LT, t_L2)

            def cube(q):
                pe.wait_ge(v_L2l, NT)
                if q >= 2:
                    pe.wait_ge(v_L3l, q - 1)
                times_L(q, m.L2T, t_L3)

            def adjacency(q):
                pe.wait_ge(v_As, NT)
                if q < 2:
                    pe.wait_ge(c_LTf, NT)
                else:
                    pe.wait_ge(v_Ahl, q - 1)
                transpose(A1, q, bank[2 + q % 2], t_Ah)

            def against_powers(stationary, done):
                for k, r in enumerate((RP[:, 1:5], RP[:, 5:9], RP[:, 0:1])):
                    pe.matmul(bank[4 + k][:, 0:r.shape[1] * D], stationary, flat(r), start=True, stop=True).then_inc(done, 1)

            pe.wait_ge(pool_c, 4)
            pe.wait_ge(small_in, 80)
            pe.transpose(bank[4][:, 0:D], w_sb[:], m.ident[:]).then_inc(t_wT, 1)
            pe.wait_ge(a_in, 16)
            for q in range(NT):
                transpose(A, q, bank[q], t_AT)
            pe.wait_ge(v_L, 2 * NT)
            for q in range(NT):
                pe.wait_ge(c_AT, q + 1)
                transpose(L, q, bank[q], t_LT)
            pe.wait_ge(v_wT, 2)
            pe.matmul(bank[5][:, 0:D], wTs[:], wT[:], start=True, stop=True).then_inc(t_R, 1)
            pe.wait_ge(v_R, 2)
            pe.matmul(bank[6][:, 0:D], RP[:, 1], RP[:, 1], start=True, stop=True).then_inc(t_R, 1)
            pe.wait_ge(v_Llo, 1)
            pe.wait_ge(v_LTl, NT)
            square(0)
            pe.wait_ge(v_R, 3)
            pe.matmul(bank[5][:, 0:2 * D], RP[:, 2], flat(RP[:, 1:3]), start=True, stop=True).then_inc(t_R, 1)
            square(1)
            pe.wait_ge(v_R, 4)
            pe.matmul(bank[6][:, 0:4 * D], RP[:, 4], flat(RP[:, 1:5]), start=True, stop=True).then_inc(t_R, 1)
            square(2)
            pe.wait_ge(v_R, 5)
            against_powers(fc[:], t_Q)
            square(3)
            adjacency(0)
            adjacency(1)
            cube(0)
            adjacency(2)
            pe.wait_ge(v_Y1, 1)
            for t in range(NT):
                for q in range(NT):
                    last = pe.matmul(bank[7][:, 8 + t:9 + t], LTf[:, q, t * P:t * P + P], Y[:, 0, q:q + 1],
                                     start=(q == 0), stop=(q == NT - 1))
            last.then_inc(t_Y2, 1)
            cube(1)
            adjacency(3)
            pe.wait_ge(v_P, 9)
            pe.wait_ge(v_bB, 1)
            against_powers(bB[:], t_cB)
            cube(2)
            cube(3)

    nc.clear_and_free_semaphores(sems)
    nc.all_engine_barrier()


def pairs(eng, steps, depth, step):
    def alive(s):
        return [0 <= s - k < steps for k in range(depth)]

    lead = (depth - 1) + (depth - 1) % 2
    for s in range(lead):
        step(s, s % 2, alive(s), s // 2)
    with eng.Fori(lead // 2, steps // 2) as r:
        for parity in range(2):
            step(r * 2 + parity, parity, [True] * depth, r)
    for s in range(steps, steps + depth - 1):
        step(s, s % 2, alive(s), s // 2)


def tile_of(X, b, t):
    return X[:, bass.ds(b, 1), t].rearrange("p a d -> p (a d)")


def batch_of(X, b):
    return X[:, bass.ds(b, 1)].rearrange("p a t d -> p (a t) d")


def batch_flat(X, b):
    return X[:, bass.ds(b, 1)].rearrange("p a t d -> p (a t d)")


class Norm:

    def __init__(self, nc, ctx, m, name):
        self.m = m
        self.stats = [ctx.enter_context(nc.sbuf_tensor(f"{name}_stats{k}", [P, 4, 6], F32)) for k in range(2)]
        self.aggr = [ctx.enter_context(nc.sbuf_tensor(f"{name}_aggr{k}", [P, 4, 2], F32)) for k in range(2)]
        self.rstd = [ctx.enter_context(nc.sbuf_tensor(f"{name}_rstd{k}", [P, 4], F32)) for k in range(2)]
        self.gate = ctx.enter_context(nc.semaphore(f"{name}_gate"))
        self.s_stats, self.s_aggr, self.s_eps, self.s_rstd, self.s_x = (
            ctx.enter_context(nc.semaphore(f"{name}_{x}")) for x in ("stats", "aggr", "eps", "rstd", "x"))

    def credit_dve(self, dve, per=1):
        dve.sem_inc(self.s_stats, 4 * CREDIT * per)
        dve.sem_inc(self.s_aggr, 4 * CREDIT * per)

    def credit_apply(self, eng, per=1):
        eng.sem_inc(self.s_x, 4 * CREDIT * per)

    def credit_pool(self, pool, per=1):
        pool.sem_inc(self.s_eps, CREDIT * per)
        pool.sem_inc(self.s_rstd, CREDIT * per)

    def statistics(self, dve, i, parity, r):
        dve.wait_ge(self.s_eps, i - 1)
        for k in range(4):
            dve.bn_stats(self.stats[parity][:, k], r[:, k]).then_inc(self.s_stats, 1)

    def aggregate(self, dve, i, parity):
        dve.wait_ge(self.s_stats, i * 4 + 4)
        hold(dve, self.gate)
        for k in range(4):
            dve.bn_aggr(self.aggr[parity][:, k], self.stats[parity][:, k]).then_inc(self.s_aggr, 1)

    def root(self, pool, i, parity):
        rstd = self.rstd[parity]
        pool.wait_ge(self.s_aggr, i * 4 + 4)
        pool.wait_ge(self.s_x, (i - 1) * 4)
        hold(pool, self.gate)
        pool.tensor_scalar(rstd[:], self.aggr[parity][:, :, 1], EPS, 1.0, ALU.add, ALU.mult).then_inc(self.s_eps, 1)
        pool.wait_ge(self.s_eps, i + 1)
        pool.tensor_tensor(rstd[:], rstd[:], self.m.neg_half[:, 0:4], ALU.pow).then_inc(self.s_rstd, 1)

    def apply(self, eng, i, parity, r, out):
        eng.wait_ge(self.s_rstd, i + 1)
        hold(eng, self.gate)
        for k in range(4):
            eng.tensor_scalar(out(k), r[:, k], self.aggr[parity][:, k, 0:1], self.rstd[parity][:, k:k + 1],
                              ALU.subtract, ALU.mult).then_inc(self.s_x, 1)


def layer0(nc, m, bank):
    GB = 2
    groups = B // GB
    with ExitStack() as own:
        def sb(name, shape, dt=F32):
            return own.enter_context(nc.sbuf_tensor(name, shape, dt))

        def sem(name):
            return own.enter_context(nc.semaphore(name))

        Xf = [sb(f"Xf{k}", [P, NT, D]) for k in range(GB)]
        Xr = [[sb(f"Xr{k}{h}", [P, NT, D], F32R) for h in range(2)] for k in range(GB)]
        yT = [[[sb(f"yT{k}{i}{h}", [P, N], F32R) for h in range(2)] for i in range(BABY)] for k in range(GB)]
        G = [sb(f"G{k}", [P, BABY, NT, GB * D]) for k in range(2)]
        z = [sb(f"z{h}", [P, NT, GB * D], F32R) for h in range(2)]
        zf = sb("zf", [P, NT, GB * D])
        norm = Norm(nc, own, m, "n0")

        gate = sem("gate")
        x_st = [sem(f"x_staged{k}") for k in range(GB)]
        x_hi = sem("x_high")
        x_lo = sem("x_low")
        y_ps = sem("y_in_psum")
        y_hi = sem("y_high")
        y_lo = sem("y_low")
        g_ps = sem("g_in_psum")
        g_sb = sem("g_out")
        z_hi = sem("z_high")
        z_lo = sem("z_low")
        h_ps = sem("h_in_psum")
        h_sb = sem("h_out")
        psum_y, psum_g, psum_h = bank[0:3], bank[3:5], bank[5:7]
        P_of = [p[:].rearrange("p (g i) d -> p g i d", i=BABY) for p in m.Pj]
        block = own.enter_context(nc.Block())

        STAGE = dict(h=0, y=0, g=0, z=1, p=1, n=1, a=1, N=2, A=2)
        ORDER = []
        for what in ("h h y z z N y z z y A p p g p g g p g y z z y z z y p p g g n p p g g a").split():
            ORDER.append((what, sum(w == what for w, _ in ORDER)))

        def four(u):
            return zf[:, 2 * u:2 * u + 2].rearrange("p t (b d) -> p (t b) d", b=GB)

        @block.sync
        def _(sp):
            with sp.Fori(0, groups) as g:
                for bb in range(GB):
                    b = g * GB + bb
                    sp.wait_ge(x_lo, after(b - 2, 1))
                    sp.wait_ge(y_ps, after(b - 2, BABY, 1))
                    hold(sp, gate)
                    sp.dma_start(Xf[bb][:], batch_of(m.X, b)).then_inc(x_st[bb], 16)

        @block.scalar
        def _(act):
            act.sem_inc(x_hi, CREDIT)
            act.sem_inc(y_hi, CREDIT * BABY)
            act.sem_inc(z_hi, CREDIT * 2 * NT)

            def step(s, par, alive, nth):
                for what, k in ORDER:
                    if not alive[STAGE[what]]:
                        continue
                    if what == "h":
                        act.wait_ge(x_st[k], s * 16 + 16)
                        act.wait_ge(y_ps, after(s * GB + k - 2, BABY))
                        act.copy(flat(Xr[k][0][:]), flat(Xf[k][:])).then_inc(x_hi, 1)
                    elif what == "y":
                        bb, i = divmod(k, BABY)
                        act.wait_ge(y_ps, after(s * GB + bb, BABY, i + 1))
                        act.wait_ge(g_ps, after(s * GB + bb - 2, NT))
                        act.copy(yT[bb][i][0][:], psum_y[i][:]).then_inc(y_hi, 1)
                    elif what == "z":
                        t = k % NT
                        if k < NT:
                            act.wait_ge(g_sb, after(s * GB - 1, NT, t + 1))
                            act.wait_ge(h_ps, after(s - 2, 2 * NT))
                            act.copy(z[0][:, t], G[1 - par][:, 2, t]).then_inc(z_hi, 1)
                        else:
                            act.wait_ge(h_ps, after(s - 1, 2 * NT, NT))
                            act.wait_ge(h_sb, after(s - 1, 2 * NT, t + 1))
                            act.copy(z[0][:, t], zf[:, t]).then_inc(z_hi, 1)

            pairs(act, groups, 3, step)

        @block.gpsimd
        def _(pool):
            norm.credit_pool(pool, 2)
            pool.sem_inc(x_lo, CREDIT)

            def step(s, par, alive, nth):
                if alive[0]:
                    for k in range(GB):
                        pool.wait_ge(x_hi, after(s * GB + k, 1))
                        pool.tensor_tensor(flat(Xr[k][1][:]), flat(Xf[k][:]), flat(Xr[k][0][:].bitcast(F32)),
                                           ALU.subtract).then_inc(x_lo, 1)
                if alive[2]:
                    for u in range(2):
                        norm.root(pool, (s - 2 + CREDIT) * 2 + u, u)

            pairs(pool, groups, 3, step)

        @block.vector
        def _(dve):
            dve.sem_inc(y_lo, CREDIT * BABY)
            dve.sem_inc(g_sb, CREDIT * NT)
            dve.sem_inc(z_lo, CREDIT * 2 * NT)
            dve.sem_inc(h_sb, CREDIT * 2 * NT)
            norm.credit_dve(dve, 2)
            norm.credit_apply(dve, 2)

            def step(s, par, alive, nth):
                for what, k in ORDER:
                    if not alive[STAGE[what]]:
                        continue
                    if what == "y":
                        bb, i = divmod(k, BABY)
                        dve.wait_ge(y_hi, after(s * GB + bb, BABY, i + 1))
                        dve.tensor_tensor(yT[bb][i][1][:], psum_y[i][:], yT[bb][i][0][:].bitcast(F32),
                                          ALU.subtract).then_inc(y_lo, 1)
                    elif what == "g":
                        bb, t = divmod(k, NT)
                        if k == 0:
                            dve.wait_ge(z_lo, after(s - 2, 2 * NT, NT))
                            dve.wait_ge(h_sb, after(s - 2, 2 * NT))
                        dve.wait_ge(g_ps, after(s * GB + bb, NT, t + 1))
                        dve.tensor_tensor(G[par][:, :, t, bb * D:bb * D + D],
                                          psum_g[t % 2][:, 0:BABY * D].rearrange("p (g d) -> p g d", g=BABY),
                                          m.bias[:, t], ALU.add).then_inc(g_sb, 1)
                    elif what == "z":
                        t = k % NT
                        dve.wait_ge(z_hi, after(s - 1, 2 * NT, k + 1))
                        dve.tensor_tensor(z[1][:, t], G[1 - par][:, 2, t] if k < NT else zf[:, t],
                                          z[0][:, t].bitcast(F32), ALU.subtract).then_inc(z_lo, 1)
                    elif what == "p":
                        t = k % NT
                        dve.wait_ge(h_ps, after(s - 1, 2 * NT, k + 1))
                        if k < NT:
                            dve.wait_ge(norm.s_x, after(s - 2, 8))
                        else:
                            dve.wait_ge(z_lo, after(s - 1, 2 * NT, k + 1))
                        dve.tensor_tensor(zf[:, t], psum_h[k % 2][:, 0:GB * D],
                                          G[1 - par][:, 1 if k < NT else 0, t], ALU.add).then_inc(h_sb, 1)
                    elif what in "nN":
                        u = "nN".index(what)
                        b = s - STAGE[what]
                        dve.wait_ge(h_sb, after(b, 2 * NT, NT + 2 * u + 2))
                        norm.statistics(dve, (b + CREDIT) * 2 + u, u, four(u))
                        norm.aggregate(dve, (b + CREDIT) * 2 + u, u)
                    elif what in "aA":
                        u = "aA".index(what)
                        b = s - STAGE[what]
                        norm.apply(dve, (b + CREDIT) * 2 + u, u, four(u),
                                   lambda n: tile_of(m.X, b * GB + n % GB, 2 * u + n // GB))

            pairs(dve, groups, 3, step)

        @block.tensor
        def _(pe):
            pe.sem_inc(y_ps, CREDIT * BABY)
            pe.sem_inc(g_ps, CREDIT * NT)
            pe.sem_inc(h_ps, CREDIT * 2 * NT)

            def step(s, par, alive, nth):
                for what, k in ORDER:
                    if not alive[STAGE[what]]:
                        continue
                    if what == "y":
                        bb, i = divmod(k, BABY)
                        b = s * GB + bb
                        pe.wait_ge(y_lo, after(b - 1, BABY, i + 1))
                        if i == 0:
                            pe.wait_ge(x_st[bb], s * 16 + 16)
                            for t in range(NT):
                                last = pe.transpose(psum_y[0][:, t * P:t * P + P], Xf[bb][:, t], m.ident[:])
                        else:
                            pe.wait_ge(x_lo, after(b, 1))
                            mat = (None, m.LT, m.L2T)[i]
                            for q in range(NT):
                                last = three_pass(pe, psum_y[i][:], [h[:, q] for h in Xr[bb]], [h[:, q] for h in mat],
                                                  start=(q == 0), stop=(q == NT - 1))
                        last.then_inc(y_ps, 1)
                    elif what == "g":
                        bb, t = divmod(k, NT)
                        b = s * GB + bb
                        pe.wait_ge(y_lo, after(b, BABY))
                        pe.wait_ge(g_sb, after(b, NT, t - 1))
                        for i in range(BABY):
                            last = three_pass(pe, psum_g[t % 2][:, 0:BABY * D],
                                              [h[:, t * P:t * P + P] for h in yT[bb][i]],
                                              [h[:, :, i] for h in P_of], start=(i == 0), stop=(i == BABY - 1))
                        last.then_inc(g_ps, 1)
                    elif what == "p":
                        t = k % NT
                        pe.wait_ge(z_lo, after(s - 1, 2 * NT, NT if k < NT else 2 * NT))
                        pe.wait_ge(h_sb, after(s - 1, 2 * NT, k - 1))
                        for q in range(NT):
                            last = three_pass(pe, psum_h[k % 2][:, 0:GB * D], [h[:, q, t * P:t * P + P] for h in m.L3T],
                                              [h[:, q] for h in z], start=(q == 0), stop=(q == NT - 1))
                        last.then_inc(h_ps, 1)

            pairs(pe, groups, 3, step)


def split(dve, high, low, src, s_high, n_high, s_low):
    dve.tensor_copy(high, src).then_inc(s_high, 1)
    dve.wait_ge(s_high, n_high)
    return dve.tensor_tensor(low, src, high.bitcast(F32), ALU.subtract).then_inc(s_low, 1)


def layer1(nc, ctx, m, ins, bank):
    m.O = ctx.enter_context(nc.sbuf_tensor("O", [P, B, N], F32))
    m.aff2 = ctx.enter_context(nc.sbuf_tensor("aff2", [P, 2, 1], F32))
    with ExitStack() as own:
        def sb(name, shape, dt=F32):
            return own.enter_context(nc.sbuf_tensor(name, shape, dt))

        W1T = [sb(f"W1T{h}", [P, CH, P], F32R) for h in range(2)]
        W2T = sb("W2T", [P, CH, P])
        par1 = sb("par1", [P, 3, CH])
        par2 = sb("par2", [P, 3, 1])
        Hb = sb("Hb", [P, CH, B, N])
        st1 = sb("st1", [P, CH, B, 6])
        st2 = sb("st2", [P, 1, B, 6])
        aff1 = sb("aff1", [P, 2, CH])
        layer1_first(nc, m, ins, bank, W1T, W2T, par1, par2, Hb, st1)
        batch_norm_affine(nc, m, "bn1", st1, par1, aff1, CH)
        layer1_second(nc, m, bank, W2T, par2, Hb, aff1, m.O, st2)
        batch_norm_affine(nc, m, "bn2", st2, par2, m.aff2, 1)


def layer1_first(nc, m, ins, bank, W1T, W2T, par1, par2, Hb, st1):
    with ExitStack() as own:
        def sb(name, shape, dt=F32):
            return own.enter_context(nc.sbuf_tensor(name, shape, dt))

        def sem(name):
            return own.enter_context(nc.semaphore(name))

        w1 = sb("w1", [P, CH, D])
        w2 = sb("w2", [P, CH, P])
        wf = sb("wf", [P, CH, P])
        Xr = [[sb(f"Xa{k}{h}", [P, NT, D], F32R) for h in range(2)] for k in range(2)]
        agT = [[sb(f"agT{k}{h}", [P, N], F32R) for h in range(2)] for k in range(2)]
        w_in = sem("w_in"); par_in = sem("par_in")
        w_ps = sem("w_in_psum"); w_sb = sem("w_out"); w_hi = sem("w_high"); w_lo = sem("w_low")
        x_hi = sem("x_high"); x_lo = sem("x_low")
        a_ps = sem("agg_in_psum"); a_hi = sem("agg_high"); a_lo = sem("agg_low")
        h_ps = sem("h_in_psum"); h_sb = sem("h_out"); h_st = sem("h_stats")
        block = own.enter_context(nc.Block())

        @block.sync
        def _(sp):
            sp.dma_start(w1[:], ins["L1_gnn_W1"].rearrange("(c p) d -> p c d", p=P)).then_inc(w_in, 16)
            sp.dma_start(flat(w2[:]), ins["L1_gnn_W2"]).then_inc(w_in, 16)
            with nc.allow_non_contiguous_dma(reason="a few hundred words once"):
                for k, n in enumerate(("b1", "g1", "be1")):
                    sp.dma_start(par1[:, k], ins[f"L1_gnn_{n}"].rearrange("(c p) -> p c", p=P)).then_inc(par_in, 16)
                for k, n in enumerate(("b2", "g2", "be2")):
                    sp.dma_start(par2[:, k], ins[f"L1_gnn_{n}"].rearrange("(p a) -> p a", a=1)).then_inc(par_in, 16)
            sp.wait_ge(w_in, 2 * 16)
            sp.wait_ge(par_in, 6 * 16)

        @block.scalar
        def _(act):
            for s in (x_hi, a_hi):
                act.sem_inc(s, CREDIT)
            act.sem_inc(h_sb, CREDIT * CH)

            def step(s, par, alive, nth):
                if alive[0]:
                    act.wait_ge(a_ps, after(s - 2, 1))
                    act.copy(flat(Xr[par][0][:]), batch_flat(m.X, s)).then_inc(x_hi, 1)
                if alive[1]:
                    b = s - 1
                    act.wait_ge(a_ps, after(b, 1))
                    act.wait_ge(h_ps, after(b - 2, CH))
                    act.copy(agT[1 - par][0][:], bank[1 - par][:]).then_inc(a_hi, 1)
                if alive[2]:
                    b = s - 2
                    act.wait_ge(par_in, 6 * 16)
                    for c in range(CH):
                        act.wait_ge(h_ps, after(b, CH, c + 1))
                        act.activation(Hb[:, c, bass.ds(b, 1)].rearrange("p a n -> p (a n)"),
                                       bank[2 + 2 * par + c][:], ACT.Identity,
                                       bias=par1[:, 0, c:c + 1]).then_inc(h_sb, 1)

            pairs(act, B, 3, step)

        @block.vector
        def _(dve):
            for s in (x_lo, a_lo):
                dve.sem_inc(s, CREDIT)
            dve.sem_inc(h_st, CREDIT * CH)

            def weights():
                dve.wait_ge(w_ps, 2 * CH)
                for k, w in enumerate((wf, W2T)):
                    dve.tensor_copy(flat(w[:]), bank[7][:, k * CH * P:(k + 1) * CH * P]).then_inc(w_sb, 1)
                dve.wait_ge(w_sb, 2)
                split(dve, flat(W1T[0][:]), flat(W1T[1][:]), flat(wf[:]), w_hi, 1, w_lo)

            def step(s, par, alive, nth):
                if alive[0]:
                    dve.wait_ge(x_hi, after(s, 1))
                    dve.tensor_tensor(flat(Xr[par][1][:]), batch_flat(m.X, s), flat(Xr[par][0][:].bitcast(F32)),
                                      ALU.subtract).then_inc(x_lo, 1)
                if alive[1]:
                    if isinstance(s, int) and s == 1:
                        weights()
                    dve.wait_ge(a_hi, after(s - 1, 1))
                    dve.tensor_tensor(agT[1 - par][1][:], bank[1 - par][:], agT[1 - par][0][:].bitcast(F32),
                                      ALU.subtract).then_inc(a_lo, 1)
                if alive[2]:
                    b = s - 2
                    for c in range(CH):
                        dve.wait_ge(h_sb, after(b, CH, c + 1))
                        dve.bn_stats(st1[:, c, bass.ds(b, 1)].rearrange("p a n -> p (a n)"),
                                     Hb[:, c, bass.ds(b, 1)].rearrange("p a n -> p (a n)")).then_inc(h_st, 1)

            pairs(dve, B, 3, step)

        @block.tensor
        def _(pe):
            pe.sem_inc(a_ps, CREDIT)
            pe.sem_inc(h_ps, CREDIT * CH)

            def weights():
                pe.wait_ge(w_in, 2 * 16)
                for k, w in enumerate((w1, w2)):
                    for c in range(CH):
                        pe.transpose(bank[7][:, (k * CH + c) * P:(k * CH + c + 1) * P], w[:, c], m.ident[:]).then_inc(w_ps, 1)

            def step(s, par, alive, nth):
                if isinstance(s, int) and s == 1:
                    weights()
                if alive[1]:
                    b = s - 1
                    pe.wait_ge(x_lo, after(b, 1))
                    pe.wait_ge(a_lo, after(b - 2, 1))
                    for k in range(NT):
                        last = three_pass(pe, bank[1 - par][:], [h[:, k] for h in Xr[1 - par]],
                                          [h[:, k] for h in m.AhT], start=(k == 0), stop=(k == NT - 1))
                    last.then_inc(a_ps, 1)
                if alive[2]:
                    b = s - 2
                    pe.wait_ge(a_lo, after(b, 1))
                    pe.wait_ge(w_lo, 1)
                    for c in range(CH):
                        pe.wait_ge(h_sb, after(b - 2, CH, c + 1))
                        three_pass(pe, bank[2 + 2 * par + c][:], [h[:, c] for h in W1T],
                                   [h[:] for h in agT[par]]).then_inc(h_ps, 1)

            pairs(pe, B, 3, step)


def batch_norm_affine(nc, m, name, st, par, aff, channels):
    with ExitStack() as own:
        mv = own.enter_context(nc.sbuf_tensor(f"{name}_mv", [P, channels, 2], F32))
        ve = own.enter_context(nc.sbuf_tensor(f"{name}_ve", [P, channels], F32))
        ms = own.enter_context(nc.sbuf_tensor(f"{name}_ms", [P, channels], F32))
        agg = own.enter_context(nc.semaphore(f"{name}_agg"))
        root = own.enter_context(nc.semaphore(f"{name}_root"))
        out = own.enter_context(nc.semaphore(f"{name}_out"))
        block = own.enter_context(nc.Block())

        @block.vector
        def _(dve):
            for c in range(channels):
                dve.bn_aggr(mv[:, c], st[:, c].rearrange("p b s -> p (b s)")).then_inc(agg, 1)
            dve.wait_ge(root, 2)
            dve.tensor_tensor(aff[:, 0], ve[:], par[:, 1], ALU.mult).then_inc(out, 1)
            dve.wait_ge(out, 1)
            dve.tensor_tensor(ms[:], mv[:, :, 0], aff[:, 0], ALU.mult).then_inc(out, 1)
            dve.wait_ge(out, 2)
            dve.tensor_tensor(aff[:, 1], par[:, 2], ms[:], ALU.subtract).then_inc(out, 1)

        @block.gpsimd
        def _(pool):
            pool.wait_ge(agg, channels)
            pool.tensor_scalar(ve[:], mv[:, :, 1], EPS, 1.0, ALU.add, ALU.mult).then_inc(root, 1)
            pool.wait_ge(root, 1)
            pool.tensor_tensor(ve[:], ve[:], m.neg_half[:, 0:channels], ALU.pow).then_inc(root, 1)


def layer1_second(nc, m, bank, W2T, par2, Hb, aff1, O, st2):
    with ExitStack() as own:
        hf = [own.enter_context(nc.sbuf_tensor(f"hf{k}", [P, CH, N], F32)) for k in range(2)]
        relu = own.enter_context(nc.semaphore("relu"))
        o_ps, o_sb, o_st = (own.enter_context(nc.semaphore(f"o_{x}")) for x in ("in_psum", "out", "stats"))
        block = own.enter_context(nc.Block())

        @block.scalar
        def _(act):
            act.sem_inc(relu, CREDIT * CH)

            def step(s, par, alive, nth):
                act.wait_ge(o_ps, after(s - 2, 1))
                for c in range(CH):
                    act.activation(hf[par][:, c], Hb[:, c, bass.ds(s, 1)].rearrange("p a n -> p (a n)"), ACT.Relu,
                                   scale=aff1[:, 0, c:c + 1], bias=aff1[:, 1, c:c + 1]).then_inc(relu, 1)

            pairs(act, B, 1, step)

        @block.vector
        def _(dve):
            dve.sem_inc(o_sb, CREDIT)

            def step(s, par, alive, nth):
                if alive[0]:
                    dve.wait_ge(o_ps, after(s, 1))
                    dve.tensor_scalar(O[:, bass.ds(s, 1)].rearrange("p a n -> p (a n)"), bank[par][:],
                                      par2[:, 0, 0:1], None, ALU.add).then_inc(o_sb, 1)
                if alive[1]:
                    b = s - 1
                    dve.wait_ge(o_sb, after(b, 1))
                    dve.bn_stats(st2[:, 0, bass.ds(b, 1)].rearrange("p a n -> p (a n)"),
                                 O[:, bass.ds(b, 1)].rearrange("p a n -> p (a n)")).then_inc(o_st, 1)

            pairs(dve, B, 2, step)

        @block.tensor
        def _(pe):
            pe.sem_inc(o_ps, CREDIT)

            def step(s, par, alive, nth):
                pe.wait_ge(o_sb, after(s - 2, 1))
                for c in range(CH):
                    pe.wait_ge(relu, after(s, CH, c + 1))
                    last = pe.matmul(bank[par][:], W2T[:, c], hf[par][:, c], start=(c == 0), stop=(c == CH - 1))
                last.then_inc(o_ps, 1)

            pairs(pe, B, 1, step)


def layer2(nc, m, ins, bank, wide):
    SCALE = float(HD) ** -0.5
    JP = NT // 2
    PAIRS = H * JP
    TILES = H * NT
    with ExitStack() as own:
        def sb(name, shape, dt=F32):
            return own.enter_context(nc.sbuf_tensor(name, shape, dt))

        def sem(name):
            return own.enter_context(nc.semaphore(name))

        W = sb("W", [P, 3 * D])
        Wr = [sb(f"Wr{h}", [P, 2 * D], F32R) for h in range(2)]
        ones = sb("ones_hd", [P, HD])
        Xf = [sb(f"Xb{k}", [P, NT, D]) for k in range(2)]
        xT = [sb(f"xT{k}", [P, N]) for k in range(2)]
        xTr = [[sb(f"xT{k}{h}", [P, N], F32R) for h in range(2)] for k in range(2)]
        qkT = [sb(f"qkT{k}", [P, 4, N], F32R) for k in range(2)]
        Q_LO, Q_HI, K_HI, K_LO = range(4)
        qk_st = [sb(f"qk_st{k}", [P, 2, H, N], F32R) for k in range(2)]
        q_st = [s[:, 0] for s in qk_st]
        k_st = [s[:, 1] for s in qk_st]
        v = [sb(f"v{k}", [P, NT, D]) for k in range(2)]
        junk = [sb(f"junk{k}", [P, N], BF16) for k in range(2)]
        mx = [sb(f"mx{k}", [P, TILES]) for k in range(2)]
        neg = [sb(f"neg{k}", [P, TILES]) for k in range(2)]
        neg_row = [sb(f"neg_row{k}", [TILES, P], F32R) for k in range(2)]
        prob = [[sb(f"prob{k}{h}", [P, 2, N]) for h in range(H)] for k in range(JP)]
        oT = sb("oT", [P, N])
        denT = sb("denT", [P, N])
        rec = sb("rec", [P, NT, H, 1])
        r = sb("rb", [P, NT, D])
        on = [sb(f"on{k}", [P, N]) for k in range(2)]
        norm1 = Norm(nc, own, m, "n1")
        norm = Norm(nc, own, m, "n2")

        bn = sem("bn_applied"); b_ps = sem("bn_turned"); res1 = sem("residual1")

        w_in = sem("w_in"); w_hi = sem("w_high"); w_lo = sem("w_low"); const = sem("const")
        x_f = sem("x_in_place")
        x_ps = sem("x_turned"); x_hi = sem("xT_high"); x_c = sem("xT_out"); x_lo = sem("xT_low")
        q_ps = sem("q_in_psum"); q_hi = sem("q_high"); q_lo = sem("q_low")
        k_ps = sem("k_in_psum"); k_hi = sem("k_high"); k_lo = sem("k_low")
        v_ps = sem("v_in_psum"); v_c = sem("v_out")
        stacked = [[sem(f"stacked{k}{h}") for h in range(H)] for k in range(2)]
        s_ps = sem("scores"); s_mx = sem("row_max")
        n_sb = sem("negated"); n_ps = sem("neg_turned"); n_row = sem("neg_row_out")
        row_in = [sem(f"row_in{k}") for k in range(2)]
        t_ps = sem("scores_t"); t_exp = sem("exp_done")
        av = sem("values")
        o_c = sem("outT_out"); d_c = sem("denominatorT_out")
        o_ps = sem("out_turned"); d_ps = sem("denominator_turned")
        rcp = sem("reciprocal"); o_n = sem("out_divided"); o_r = sem("residual")
        gate = sem("gate")
        psO, psD = bank[4], bank[5]
        STACKED = 3 * 16
        block = own.enter_context(nc.Block())

        STAGE = dict(N=0, T=0, R=0, B=0, Y=1, x=1, q=1, k=1, v=2, s=2, g=3, n=3, t=3,
                     a=4, e=4, o=4, d=4, m=4, r=4, b=4, y=4)
        ORDER = []
        for what in ("s s g Y a n s N R x T a B s q k a s e s a s s t s t s d t m o r s t t s v b t s s y t t s s").split():
            ORDER.append((what, sum(w == what for w, _ in ORDER)))
        RING = [item for item in ORDER if item[0] in "Txqkvsnod"]
        ring = {item: bank[6 + n % 2] for n, item in enumerate(RING)}

        def released(s, what, k):
            b = s - STAGE[what]
            return {"x": (x_c, after(b, 1)), "q": (q_lo, after(b, 1)), "k": (k_lo, after(b, 1)),
                    "v": (v_c, after(b, 1)), "s": (s_mx, after(b, TILES, k + 1)),
                    "n": (n_row, after(b, 1)), "o": (o_n, after(b, 1)),
                    "d": (rcp, after(b, 1)), "T": (res1, after(b, 1))}[what]

        def of_batch(what, s, par, nth):
            back = STAGE[what]
            return s - back, (par + back) % 2, nth + (par - back) // 2

        @block.sync
        def _(sp):
            sp.dma_start(W[:], ins["L2_gnn_W"]).then_inc(w_in, 16)
            for k in range(2):
                sp.sem_inc(row_in[k], 16)

            def step(s, par, alive, nth):
                if alive[2]:
                    sp.wait_ge(n_row, after(s - 2, 1))
                    hold(sp, gate)
                    sp.dma_start(q_st[par][3 * HD:3 * HD + 1].bitcast(F32).rearrange("a h (t p) -> a (h t) p", p=P),
                                 neg_row[par][:].bitcast(F32)).then_inc(row_in[par], 16)
                if alive[0]:
                    sp.wait_ge(k_lo, after(s, 1))
                    for h in range(H):
                        sp.wait_ge(t_ps, after(s - 2, PAIRS, (h + 1) * JP))
                        if h == 0:
                            hold(sp, gate)
                        for g, (q, k) in enumerate(((Q_HI, K_HI), (Q_HI, K_LO), (Q_LO, K_HI))):
                            sp.dma_start(qk_st[par][g * HD:(g + 1) * HD, :, h].bitcast(F32),
                                         qkT[par][h * HD:(h + 1) * HD, q:k + 1:k - q].bitcast(F32)
                                         ).then_inc(stacked[par][h], 16)

            pairs(sp, B, 4, step)

        @block.gpsimd
        def _(pool):
            pool.sem_inc(x_f, CREDIT)
            norm.credit_pool(pool)
            pool.memset(ones[:], 1.0).then_inc(const, 1)
            for n, (buf, end, value) in enumerate([(b, e, x) for e, x, bufs in
                                                   ((P, 0.0, q_st + k_st), (3 * HD + 1, 1.0, k_st)) for b in bufs]):
                pool.wait_ge(const, n + 1)
                pool.memset(buf[3 * HD:end].bitcast(F32), value).then_inc(const, 1)
            pool.wait_ge(const, 7)

            norm1.credit_pool(pool)

            def step(s, par, alive, nth):
                if alive[0]:
                    pool.wait_ge(x_f, after(s - 1, 1))
                    norm1.root(pool, s + CREDIT, par)
                if alive[4]:
                    if alive[0]:
                        pool.wait_ge(norm1.s_rstd, after(s, 1))
                    norm.root(pool, s - 4 + CREDIT, par)
                if alive[0]:
                    pool.wait_ge(norm1.s_x, after(s, 4))
                    pool.tensor_copy(batch_flat(m.X, s), flat(Xf[par][:])).then_inc(x_f, 1)

            pairs(pool, B, 5, step)

        @block.scalar
        def _(act):
            for s in (bn, x_hi, x_c, q_hi, k_hi, v_c, n_row, o_c, d_c):
                act.sem_inc(s, CREDIT)
            act.sem_inc(t_exp, CREDIT * PAIRS)

            def step(s, par, alive, nth):
                for what, k in ORDER:
                    if not alive[STAGE[what]]:
                        continue
                    src = ring.get((what, k))
                    b, bp, nb = of_batch(what, s, par, nth)
                    if what == "N":
                        act.wait_ge(b_ps, after(b - 2, 1))
                        act.activation(on[bp][:], m.O[:, bass.ds(b, 1)].rearrange("p a n -> p (a n)"), ACT.Identity,
                                       scale=m.aff2[:, 0, 0:1], bias=m.aff2[:, 1, 0:1]).then_inc(bn, 1)
                    elif what == "x":
                        act.wait_ge(x_ps, after(b, 1))
                        act.wait_ge(k_ps, after(b - 2, 1))
                        act.copy(xTr[bp][0][:], src[:]).then_inc(x_hi, 1)
                        act.wait_ge(v_ps, after(b - 2, 1))
                        act.copy(xT[bp][:], src[:]).then_inc(x_c, 1)
                    elif what == "q":
                        for h in range(H):
                            act.wait_ge(stacked[bp][h], nb * STACKED)
                        act.wait_ge(q_ps, after(b, 1))
                        act.copy(qkT[bp][:, Q_HI], src[:]).then_inc(q_hi, 1)
                    elif what == "k":
                        act.wait_ge(k_ps, after(b, 1))
                        act.copy(qkT[bp][:, K_HI], src[:]).then_inc(k_hi, 1)
                    elif what == "v":
                        act.wait_ge(v_ps, after(b, 1))
                        act.wait_ge(av, after(b - 2, NT))
                        act.copy(flat(v[bp][:]), src[:]).then_inc(v_c, 1)
                    elif what == "t":
                        h, jp = divmod(k, JP)
                        act.wait_ge(t_ps, after(b, PAIRS, k + 1))
                        if k == 0:
                            act.wait_ge(av, after(b - 1, NT))
                        act.activation(flat(prob[jp][h][:]), wide[k % 2][:], ACT.Exp, scale=SCALE).then_inc(t_exp, 1)
                    elif what == "n":
                        act.wait_ge(n_ps, after(b, 1))
                        act.wait_ge(row_in[bp], (nb + 1) * 16)
                        act.copy(neg_row[bp][:], src[0:TILES, 0:P]).then_inc(n_row, 1)
                    elif what == "e":
                        act.wait_ge(av, after(b, NT))
                        act.wait_ge(o_ps, after(b - 1, 1))
                        act.copy(oT[:], psO[:]).then_inc(o_c, 1)
                        act.wait_ge(d_ps, after(b - 1, 1))
                        act.copy(denT[:], psD[:]).then_inc(d_c, 1)

            pairs(act, B, 5, step)

        @block.vector
        def _(dve):
            for s in (res1, x_lo, q_lo, k_lo, n_sb, rcp, o_n, o_r):
                dve.sem_inc(s, CREDIT)
            dve.sem_inc(s_mx, CREDIT * TILES)
            norm1.credit_dve(dve)
            norm1.credit_apply(dve)
            norm.credit_dve(dve)
            norm.credit_apply(dve)

            def step(s, par, alive, nth):
                for what, k in ORDER:
                    if not alive[STAGE[what]]:
                        continue
                    src = ring.get((what, k))
                    b, bp, nb = of_batch(what, s, par, nth)
                    if what == "x" and isinstance(s, int) and s == 1:
                        dve.wait_ge(w_in, 16)
                        split(dve, Wr[0][:], Wr[1][:], W[:, 0:2 * D], w_hi, 1, w_lo)
                    if what == "R":
                        dve.wait_ge(b_ps, after(b, 1))
                        dve.wait_ge(x_ps, after(b - 2, 1))
                        dve.wait_ge(x_f, after(b - 2, 1))
                        dve.tensor_tensor(flat(Xf[bp][:]), ring["T", 0][:], batch_flat(m.X, b), ALU.add).then_inc(res1, 1)
                    elif what == "B":
                        dve.wait_ge(res1, after(b, 1))
                        norm1.statistics(dve, b + CREDIT, bp, Xf[bp])
                        norm1.aggregate(dve, b + CREDIT, bp)
                    elif what == "Y":
                        norm1.apply(dve, b + CREDIT, bp, Xf[bp], lambda k: Xf[bp][:, k])
                    elif what == "x":
                        dve.wait_ge(x_c, after(b, 1))
                        dve.wait_ge(k_ps, after(b - 2, 1))
                        dve.tensor_tensor(xTr[bp][1][:], xT[bp][:], xTr[bp][0][:].bitcast(F32),
                                          ALU.subtract).then_inc(x_lo, 1)
                    elif what == "q":
                        dve.wait_ge(q_hi, after(b, 1))
                        dve.tensor_tensor(qkT[bp][:, Q_LO], src[:], qkT[bp][:, Q_HI].bitcast(F32),
                                          ALU.subtract).then_inc(q_lo, 1)
                    elif what == "k":
                        dve.wait_ge(k_hi, after(b, 1))
                        dve.tensor_tensor(qkT[bp][:, K_LO], src[:], qkT[bp][:, K_HI].bitcast(F32),
                                          ALU.subtract).then_inc(k_lo, 1)
                    elif what == "s":
                        dve.wait_ge(s_ps, after(b, TILES, k + 1))
                        dve.wait_ge(s_mx, after(b, TILES, k - 1))
                        hold(dve, gate)
                        dve.tensor_tensor_reduce(out=junk[k % 2][:], in0=src[:], in1=m.mask_ij[:, k % NT],
                                                 scale=1.0, scalar=3.0 * MASKED, op0=ALU.add, op1=ALU.max,
                                                 accum_out=mx[bp][:, k:k + 1]).then_inc(s_mx, 1)
                    elif what == "g":
                        dve.wait_ge(s_mx, after(b, TILES))
                        dve.wait_ge(n_ps, after(b - 2, 1))
                        dve.tensor_scalar(neg[bp][:], mx[bp][:], -1.0, None, ALU.mult).then_inc(n_sb, 1)
                    elif what == "m":
                        dve.wait_ge(d_ps, after(b, 1))
                        dve.wait_ge(o_n, after(b - 1, 1))
                        dve.reciprocal(rec[:, :, :, 0],
                                       ring["d", 0][:].rearrange("p (t h d) -> p t h d", h=H, d=HD)[:, :, :, 0]
                                       ).then_inc(rcp, 1)
                        dve.wait_ge(o_ps, after(b, 1))
                        dve.wait_ge(rcp, after(b, 1))
                        dve.wait_ge(norm.s_x, after(b - 1, 4))
                        dve.tensor_tensor(r[:].rearrange("p t (h d) -> p t h d", h=H),
                                          ring["o", 0][:].rearrange("p (t h d) -> p t h d", h=H, d=HD),
                                          rec[:].broadcast_to([P, NT, H, HD]), ALU.mult).then_inc(o_n, 1)
                    elif what == "r":
                        dve.wait_ge(o_n, after(b, 1))
                        dve.wait_ge(x_f, after(b, 1))
                        dve.tensor_tensor(flat(r[:]), flat(r[:]), batch_flat(m.X, b),
                                          ALU.add).then_inc(o_r, 1)
                    elif what == "b":
                        dve.wait_ge(o_r, after(b, 1))
                        norm.statistics(dve, b + CREDIT, bp, r)
                        norm.aggregate(dve, b + CREDIT, bp)
                    elif what == "y":
                        norm.apply(dve, b + CREDIT, bp, r, lambda k: tile_of(m.X, b, k))

            pairs(dve, B, 5, step)

        @block.tensor
        def _(pe):
            for s in (b_ps, x_ps, q_ps, k_ps, v_ps, n_ps, o_ps, d_ps):
                pe.sem_inc(s, CREDIT)
            pe.sem_inc(s_ps, CREDIT * TILES)
            pe.sem_inc(t_ps, CREDIT * PAIRS)
            pe.sem_inc(av, CREDIT * NT)

            def wait_for_bank(s, alive, item):
                was = [True] * 5 if alive[0] and not isinstance(s, int) else [0 <= s - 1 - k < B for k in range(5)]
                turns = [(s - 1, was, i) for i in RING] + [(s, alive, i) for i in RING]
                for at, live, (what, k) in turns[RING.index(item) + len(RING) - 2::-2]:
                    if live[STAGE[what]]:
                        pe.wait_ge(*released(at, what, k))
                        return

            def step(s, par, alive, nth):
                for what, k in ORDER:
                    if not alive[STAGE[what]]:
                        continue
                    out = ring.get((what, k))
                    b, bp, nb = of_batch(what, s, par, nth)
                    if out is not None:
                        wait_for_bank(s, alive, (what, k))
                    if what == "T":
                        pe.wait_ge(bn, after(b, 1))
                        for t in range(NT):
                            last = pe.transpose(out[:, t * P:t * P + P], on[bp][:, t * P:t * P + P], m.ident[:])
                        last.then_inc(b_ps, 1)
                    elif what == "x":
                        pe.wait_ge(norm1.s_x, after(b, 4))
                        for t in range(NT):
                            last = pe.transpose(out[:, t * P:t * P + P], Xf[bp][:, t], m.ident[:])
                        last.then_inc(x_ps, 1)
                    elif what == "q":
                        if isinstance(s, int) and s == 1:
                            pe.wait_ge(const, 7)
                            pe.wait_ge(w_lo, 1)
                        pe.wait_ge(x_lo, after(b, 1))
                        three_pass(pe, out[:], [h[:, 0:D] for h in Wr], [h[:] for h in xTr[bp]]).then_inc(q_ps, 1)
                    elif what == "k":
                        three_pass(pe, out[:], [h[:, D:2 * D] for h in Wr], [h[:] for h in xTr[bp]]).then_inc(k_ps, 1)
                    elif what == "v":
                        for t in range(NT):
                            last = pe.matmul(out[:, t * P:t * P + P], xT[bp][:, t * P:t * P + P], W[:, 2 * D:],
                                             start=True, stop=True)
                        last.then_inc(v_ps, 1)
                    elif what == "s":
                        h, i = divmod(k, NT)
                        if i == 0:
                            pe.wait_ge(stacked[bp][h], (nb + 1) * STACKED)
                        pe.matmul(out[:], q_st[bp][0:3 * HD, h, i * P:i * P + P], k_st[bp][0:3 * HD, h],
                                  start=True, stop=True).then_inc(s_ps, 1)
                    elif what == "n":
                        pe.wait_ge(n_sb, after(b, 1))
                        pe.transpose(out[0:TILES, 0:P], neg[bp][:], m.ident[:]).then_inc(n_ps, 1)
                    elif what == "t":
                        h, jp = divmod(k, JP)
                        if k == 0:
                            pe.wait_ge(row_in[bp], (nb + 2) * 16)
                        pe.wait_ge(t_exp, after(b, PAIRS, k - 1))
                        for jj in range(2):
                            j = jp * 2 + jj
                            ps = wide[k % 2][:, jj * N:jj * N + N]
                            pe.matmul(ps, k_st[bp][:, h, j * P:j * P + P], q_st[bp][:, h], start=True, stop=False)
                            last = pe.matmul(ps, m.identb[:], m.mask_ji[:, j], start=False, stop=True)
                        last.then_inc(t_ps, 1)
                    elif what == "a":
                        if k == 0:
                            pe.wait_ge(t_exp, after(b, PAIRS))
                            pe.wait_ge(o_c, after(b - 1, 1))
                            pe.wait_ge(d_c, after(b - 1, 1))
                        jp, jj = divmod(k, 2)
                        for ps, stat in ((psO, None), (psD, ones)):
                            for h in range(H):
                                c = slice(h * HD, (h + 1) * HD)
                                last = pe.matmul(ps[c, :], v[bp][:, k, c] if stat is None else stat[:],
                                                 prob[jp][h][:, jj], start=(k == 0), stop=(k == NT - 1),
                                                 skip_group_check=True)
                        last.then_inc(av, 1)
                    elif what == "o":
                        pe.wait_ge(o_c, after(b, 1))
                        for t in range(NT):
                            last = pe.transpose(out[:, t * P:t * P + P], oT[:, t * P:t * P + P], m.ident[:])
                        last.then_inc(o_ps, 1)
                    elif what == "d":
                        pe.wait_ge(d_c, after(b, 1))
                        for t in range(NT):
                            last = pe.transpose(out[:, t * P:t * P + P], denT[:, t * P:t * P + P], m.ident[:])
                        last.then_inc(d_ps, 1)

            pairs(pe, B, 5, step)


def layer3(nc, m, ins, bank, out):
    SLOPE = 0.2
    with ExitStack() as own:
        def sb(name, shape, dt=F32):
            return own.enter_context(nc.sbuf_tensor(name, shape, dt))

        def sem(name):
            return own.enter_context(nc.semaphore(name))

        WX = sb("WX", [P, D + 2])
        a_sb = sb("a_sb", [P, 2])
        WT = sb("WT", [P, D])
        ones = sb("ones3", [P, P])
        onesb = sb("onesb", [P, P], BF16)
        wB = [sb(f"wB{k}", [P, P]) for k in range(2)]
        Xf = [sb(f"Xc{k}", [P, NT, D]) for k in range(2)]
        xT = [sb(f"xTc{k}", [P, N]) for k in range(2)]
        Wh = [sb(f"Wh{k}", [P, NT, D + 2]) for k in range(2)]
        s12 = [sb(f"s12{k}", [P, NT, 2]) for k in range(2)]
        s2s = [sb(f"s2s{k}", [P, 2, NT]) for k in range(2)]
        junk = [sb(f"junk3{k}", [P, N], BF16) for k in range(2)]
        mx = [sb(f"mx3{k}", [P, NT]) for k in range(2)]
        em = [sb(f"em{k}", [P, 3, NT]) for k in range(2)]
        dg = [sb(f"dg{k}", [P, NT, P], BF16) for k in range(2)]
        rl = [sb(f"rl{k}", [P, NT, N]) for k in range(2)]
        pr = [sb(f"pr{k}", [P, NT, N]) for k in range(2)]
        rec = [sb(f"rec3{k}", [P, NT]) for k in range(2)]
        r = [sb(f"rc{k}", [P, NT, D]) for k in range(2)]
        norm = Norm(nc, own, m, "n3")

        w_in = sem("w_in"); const = sem("const"); wt_ps = sem("WT_in_psum"); wt_c = sem("WT_out")
        wa_ps = sem("Wa_in_psum"); wa_c = sem("Wa_out"); wb_c = sem("Wa_spread")
        x_f = sem("x_copied")
        x_ps = sem("x_turned"); x_c = sem("xT_out")
        wh_ps = sem("Wh_in_psum"); s_c = sem("s_out"); wh_c = sem("Wh_out")
        ss = sem("s2_scaled")
        s2_ps = sem("s2_rows"); s1_ps = sem("s1_rows")
        s_mx = sem("row_max")
        e_m = sem("max_terms")
        d_g = sem("diagonals")
        relu = sem("relu")
        r_ps = sem("mask_and_rows"); e_s = sem("e_summed")
        ex = sem("exp_done"); av = sem("values")
        rcp = sem("reciprocal")
        res = sem("residual")
        stored = [sem(f"stored{k}") for k in range(2)]
        gate = sem("gate")
        half = [bank[3], bank[0]]
        out_bank = [bank[6], bank[7]]
        block = own.enter_context(nc.Block())

        STAGE = dict(x=0, w=0, j=0, i=0, m=0, c=0, g=0, l=0, e=1, E=1, a=2, d=2, r=2, b=2, B=2)
        ORDER = []
        for what in "a a x a a d r r d r r e e w w e e j i E E b m B m m l m c l c l l g c".split():
            ORDER.append((what, sum(w == what for w, _ in ORDER)))

        @block.sync
        def _(sp):
            sp.dma_start(WX[:, 0:D], ins["L3_gnn_W"]).then_inc(w_in, 16)
            with nc.allow_non_contiguous_dma(reason="256 words once"):
                sp.dma_start(a_sb[:], ins["L3_gnn_a"].rearrange("(k p) a -> p (k a)", p=P)).then_inc(w_in, 16)
            sp.wait_ge(w_in, 32)
            for k in range(2):
                sp.sem_inc(stored[k], 16)

            def step(s, par, alive, nth):
                if alive[0]:
                    sp.wait_ge(norm.s_x, after(s, 4))
                    hold(sp, gate)
                    sp.dma_start(out[bass.ds(s, 1)].rearrange("a (t p) d -> p (a t) d", p=P),
                                 r[par][:]).then_inc(stored[par], 16)

            pairs(sp, B, 1, step)
            for k in range(2):
                sp.wait_ge(stored[k], 16 + 16 * (B // 2))

        @block.gpsimd
        def _(pool):
            pool.sem_inc(x_f, CREDIT)
            norm.credit_pool(pool)
            norm.credit_apply(pool)
            for n, ap in enumerate((ones[:], onesb[:], Wh[0][:, :, D:D + 1], Wh[1][:, :, D:D + 1])):
                pool.wait_ge(const, n)
                pool.memset(ap, 1.0).then_inc(const, 1)
            pool.wait_ge(const, 4)

            def step(s, par, alive, nth):
                if alive[0]:
                    pool.wait_ge(x_ps, after(s - 2, 1))
                    if alive[3]:
                        pool.wait_ge(norm.s_x, after(s - 4, 4))
                    pool.tensor_copy(flat(Xf[par][:]), batch_flat(m.X, s)).then_inc(x_f, 1)
                if alive[3]:
                    b = s - 3
                    pool.wait_ge(x_f, after(s if alive[0] else B - 1, 1))
                    norm.root(pool, b + CREDIT, 1 - par)
                    norm.apply(pool, b + CREDIT, 1 - par, r[1 - par], lambda k: r[1 - par][:, k])

            pairs(pool, B, 4, step)

        @block.scalar
        def _(act):
            act.sem_inc(x_c, CREDIT)
            act.sem_inc(ex, CREDIT * 2)
            act.sem_inc(wh_c, CREDIT * 2)
            act.sem_inc(relu, CREDIT * NT)
            act.sem_inc(d_g, CREDIT * NT)

            def step(s, par, alive, nth):
                for what, k in ORDER:
                    if not alive[STAGE[what]]:
                        continue
                    b = s - STAGE[what]
                    if what == "x":
                        act.wait_ge(x_ps, after(s, 1))
                        act.wait_ge(s1_ps, after(s - 2, 1))
                        act.copy(xT[par][:], bank[0][:]).then_inc(x_c, 1)
                    elif what == "w":
                        act.wait_ge(av, after(s - 2, NT))
                        act.wait_ge(s_c, after(s, 2, k + 1))
                        act.copy(Wh[par][:, 2 * k:2 * k + 2, 0:D],
                                 half[k][:, 0:2 * (D + 2)].rearrange("p (t d) -> p t d", t=2)[:, :, 0:D]).then_inc(wh_c, 1)
                    elif what == "l":
                        if k == 0:
                            act.wait_ge(s1_ps, after(s, 1))
                            act.wait_ge(ss, after(s, 2))
                            act.wait_ge(e_s, after(s - 2, NT))
                        act.activation(rl[par][:, k], bank[1][:], ACT.Relu, scale=1.0 - SLOPE,
                                       bias=s2s[par][:, 0, k:k + 1]).then_inc(relu, 1)
                    elif what == "g":
                        act.wait_ge(e_m, after(s, 3))
                        act.wait_ge(r_ps, after(s - 2, NT))
                        for t in range(NT):
                            act.activation(dg[par][:, t], m.identb[:], ACT.Copy,
                                           scale=em[par][:, 2, t:t + 1]).then_inc(d_g, 1)
                    elif what == "E":
                        act.wait_ge(e_s, after(b, NT, 2 * k + 2))
                        two = flat(pr[1 - par][:, 2 * k:2 * k + 2])
                        act.activation(two, two, ACT.Exp).then_inc(ex, 1)

            pairs(act, B, 3, step)

        @block.vector
        def _(dve):
            dve.sem_inc(s_c, CREDIT * 2)
            dve.sem_inc(ss, CREDIT * 2)
            dve.sem_inc(s_mx, CREDIT * NT)
            dve.sem_inc(e_m, CREDIT * 3)
            dve.sem_inc(e_s, CREDIT * NT)
            dve.sem_inc(rcp, CREDIT * 2)
            dve.sem_inc(res, CREDIT * NT)
            norm.credit_dve(dve)
            dve.wait_ge(wt_ps, 1)
            dve.tensor_copy(WT[:], bank[0][:, 0:D]).then_inc(wt_c, 1)
            dve.wait_ge(wa_ps, 1)
            dve.tensor_copy(WX[:, D:D + 2], bank[1][:, 0:2]).then_inc(wa_c, 1)
            dve.wait_ge(wa_c, 1)
            dve.wait_ge(const, 1)
            for k in range(2):
                dve.tensor_scalar(wB[k][:], ones[:], WX[:, D + k:D + k + 1], None, ALU.mult).then_inc(wb_c, 1)

            def step(s, par, alive, nth):
                for what, k in ORDER:
                    if not alive[STAGE[what]]:
                        continue
                    b = s - STAGE[what]
                    if what == "w":
                        dve.wait_ge(wh_ps, after(s, 2, k + 1))
                        dve.tensor_copy(s12[par][:, 2 * k:2 * k + 2],
                                        half[k][:, 0:2 * (D + 2)].rearrange("p (t d) -> p t d", t=2)[:, :, D:]).then_inc(s_c, 1)
                        if k == 1:
                            dve.wait_ge(s_c, after(s, 2))
                            dve.wait_ge(relu, after(s - 2, NT))
                            for n, f in enumerate((1.0 - SLOPE, SLOPE)):
                                dve.tensor_scalar(s2s[par][:, n], s12[par][:, :, 1], f, None, ALU.mult).then_inc(ss, 1)
                    elif what == "m":
                        dve.wait_ge(s2_ps, after(s, 1))
                        dve.wait_ge(s_mx, after(s, NT, k - 1))
                        hold(dve, gate)
                        dve.tensor_tensor_reduce(out=junk[k % 2][:], in0=bank[2][:], in1=m.mask_ij[:, k],
                                                 scale=1.0, scalar=3.0 * MASKED, op0=ALU.add, op1=ALU.max,
                                                 accum_out=mx[par][:, k:k + 1]).then_inc(s_mx, 1)
                    elif what == "e":
                        if k == 0:
                            dve.wait_ge(av, after(b - 2, NT))
                        dve.wait_ge(relu, after(b, NT, k + 1))
                        dve.wait_ge(r_ps, after(b, NT, k + 1))
                        dve.scalar_tensor_tensor(out=pr[1 - par][:, k], in0=bank[4 + k % 2][:],
                                                 scalar=s2s[1 - par][:, 1, k:k + 1], in1=rl[1 - par][:, k],
                                                 op0=ALU.add, op1=ALU.add).then_inc(e_s, 1)
                    elif what == "c":
                        s1 = s12[par][:, :, 0]
                        if k == 0:
                            dve.wait_ge(s_mx, after(s, NT))
                            dve.tensor_tensor(em[par][:, 0], s1, mx[par][:], ALU.add).then_inc(e_m, 1)
                        elif k == 1:
                            dve.wait_ge(e_m, after(s, 3, 1))
                            dve.scalar_tensor_tensor(out=em[par][:, 1], in0=em[par][:, 0], scalar=SLOPE, in1=em[par][:, 0],
                                                     op0=ALU.mult, op1=ALU.max).then_inc(e_m, 1)
                        else:
                            dve.wait_ge(e_m, after(s, 3, 2))
                            dve.wait_ge(d_g, after(s - 2, NT))
                            dve.scalar_tensor_tensor(out=em[par][:, 2], in0=s1, scalar=SLOPE, in1=em[par][:, 1],
                                                     op0=ALU.mult, op1=ALU.subtract).then_inc(e_m, 1)
                    elif what == "d":
                        dve.wait_ge(av, after(b, NT, 2 * k + 2))
                        dve.wait_ge(res, after(b - 2, NT))
                        dve.reciprocal(rec[par][:, 2 * k:2 * k + 2],
                                       out_bank[k][:, 0:2 * (D + 2)].rearrange("p (t d) -> p t d", t=2)[:, :, D]
                                       ).then_inc(rcp, 1)
                    elif what == "r":
                        h, t = divmod(k, 2)
                        if t == 0:
                            dve.wait_ge(rcp, after(b, 2, h + 1))
                            dve.wait_ge(stored[par], nth * 16)
                        dve.scalar_tensor_tensor(out=r[par][:, k], in0=out_bank[h][:, t * (D + 2):t * (D + 2) + D],
                                                 scalar=rec[par][:, k:k + 1], in1=tile_of(m.X, b, k),
                                                 op0=ALU.mult, op1=ALU.add).then_inc(res, 1)
                    elif what == "b":
                        dve.wait_ge(res, after(b, NT))
                        norm.statistics(dve, b + CREDIT, par, r[par])
                    elif what == "B":
                        norm.aggregate(dve, b + CREDIT, par)

            pairs(dve, B, 3, step)

        @block.tensor
        def _(pe):
            for s in (x_ps, s2_ps, s1_ps):
                pe.sem_inc(s, CREDIT)
            pe.sem_inc(av, CREDIT * NT)
            pe.sem_inc(wh_ps, CREDIT * 2)
            pe.sem_inc(r_ps, CREDIT * NT)
            pe.wait_ge(w_in, 32)
            pe.transpose(bank[0][:, 0:D], WX[:, 0:D], m.ident[:]).then_inc(wt_ps, 1)
            pe.wait_ge(wt_c, 1)
            pe.matmul(bank[1][:, 0:2], WT[:], a_sb[:], start=True, stop=True).then_inc(wa_ps, 1)
            pe.wait_ge(wb_c, 2)
            pe.wait_ge(const, 4)

            def step(s, par, alive, nth):
                for what, k in ORDER:
                    if not alive[STAGE[what]]:
                        continue
                    b = s - STAGE[what]
                    if what == "x":
                        pe.wait_ge(x_f, after(s, 1))
                        pe.wait_ge(wh_c, after(s - 1, 2))
                        for t in range(NT):
                            last = pe.transpose(bank[0][:, t * P:t * P + P], Xf[par][:, t], m.ident[:])
                        last.then_inc(x_ps, 1)
                    elif what == "w":
                        pe.wait_ge(x_c, after(s, 1))
                        for t in range(2):
                            last = pe.matmul(half[k][:, t * (D + 2):(t + 1) * (D + 2)],
                                             xT[par][:, (2 * k + t) * P:(2 * k + t + 1) * P], WX[:],
                                             start=True, stop=True)
                        last.then_inc(wh_ps, 1)
                    elif what == "j":
                        pe.wait_ge(x_c, after(s, 1))
                        pe.wait_ge(s_mx, after(s - 1, NT))
                        pe.matmul(bank[2][:], wB[1][:], xT[par][:], start=True, stop=True).then_inc(s2_ps, 1)
                    elif what == "i":
                        pe.wait_ge(relu, after(s - 1, NT))
                        pe.matmul(bank[1][:], wB[0][:], xT[par][:], start=True, stop=True).then_inc(s1_ps, 1)
                    elif what == "a":
                        h, t = divmod(k, 2)
                        pe.wait_ge(ex, after(b, 2))
                        pe.wait_ge(res, after(b - 1, NT, 2 * h + 2))
                        for j in range(NT):
                            last = pe.matmul(out_bank[h][:, t * (D + 2):t * (D + 2) + D + 1],
                                             pr[par][:, j, k * P:k * P + P], Wh[par][:, j, 0:D + 1],
                                             start=(j == 0), stop=(j == NT - 1))
                        last.then_inc(av, 1)
                    elif what == "e":
                        pe.wait_ge(d_g, after(b, NT))
                        pe.wait_ge(e_s, after(b, NT, k - 1))
                        pe.matmul(bank[4 + k % 2][:], m.identb[:], m.mask_ji[:, k], start=True, stop=False)
                        pe.matmul(bank[4 + k % 2][:], onesb[:], flat(dg[1 - par][:]), start=False, stop=True).then_inc(r_ps, 1)

            pairs(pe, B, 3, step)


def build(nc, ins, out):
    with ExitStack() as ctx:
        wide = [ctx.enter_context(nc.psum_tensor(f"wide{k}", [P, 1024], F32)) for k in range(2)]
        bank = [w[:, k * 512:k * 512 + 512] for w in wide for k in range(2)]
        bank += [ctx.enter_context(nc.psum_tensor(f"bank{k}", [P, 512], F32))[:] for k in range(4, 8)]
        m = Memory()
        setup_constants(nc, ctx, m, ins, bank)
        with ExitStack() as first:
            layer0_setup(nc, first, m, ins, bank)
            layer0(nc, m, bank)
        with ExitStack() as second:
            layer1(nc, second, m, ins, bank)
            layer2(nc, m, ins, bank, wide)
        layer3(nc, m, ins, bank, out)


_INS = ["x", "adj", "L0_gnn_alpha_train", "L0_gnn_w", "L0_gnn_d", "L0_gnn_fc_in_w", "L0_gnn_fc_in_b",
        "L1_gnn_W1", "L1_gnn_b1", "L1_gnn_g1", "L1_gnn_be1", "L1_gnn_W2", "L1_gnn_b2", "L1_gnn_g2", "L1_gnn_be2",
        "L2_gnn_W", "L3_gnn_W", "L3_gnn_a"]


def kernel(**inputs):
    import numpy as _np
    import concourse.bacc as _bacc
    from concourse.bass_utils import run_bass_kernel_spmd as _run

    nc = _bacc.Bacc("TRN2", target_bir_lowering=False, num_devices=1)
    arrays, ins = {}, {}
    for name in _INS:
        a = _np.ascontiguousarray(inputs[name])
        arrays[f"in_{name}_dram"] = a
        ins[name] = nc.dram_tensor(f"in_{name}_dram", a.shape, mybir.dt.from_np(a.dtype), kind="ExternalInput").ap()
    out = nc.dram_tensor("out_0_dram", (B, N, D), F32, kind="ExternalOutput").ap()
    build(nc, ins, out)
    r = _run(nc, [arrays], core_ids=[0])
    return r.results[0]["out_0_dram"]
```
